# Optimizing a Trainium2 kernel written in Bass

```python
import numpy as np
import jax
import jax.numpy as jnp

def _softmax(x, axis=-1):
    return jax.nn.softmax(x, axis=axis)

def _gelu(x):
    return jax.nn.gelu(x, approximate=True)

def _silu(x):
    return jax.nn.silu(x)

def _sigmoid(x):
    return jax.nn.sigmoid(x)

def _layernorm(x, axis=-1, eps=1e-05):
    m = jnp.mean(x, axis=axis, keepdims=True)
    v = jnp.var(x, axis=axis, keepdims=True)
    return (x - m) / jnp.sqrt(v + eps)

def _scatter_add(tgt, idx, src, axis=0):
    return tgt.at[idx].add(src)

def _segment_sum(src, seg, n):
    return jax.ops.segment_sum(src, seg, n)
kernel_name = 'mk_gnn_resnorm_d4_gnn_r64_3b595a'

def setup_inputs(seed: int=0):
    np.random.seed(seed)
    _w = jnp.asarray

    def _rec_inputs():
        import jax
        import jax.numpy as jnp
        _gk = jax.random.key(seed)
        x = -0.0002117 + 1 * jax.random.normal(jax.random.fold_in(_gk, 1), (50000, 256), jnp.float32)
        src = jax.random.randint(jax.random.fold_in(_gk, 2), (25000,), 0, 50000, jnp.int32)
        dst = jnp.minimum((50000 * jax.random.uniform(jax.random.fold_in(_gk, 3), (25000,)) ** 2.0).astype(jnp.int32), 49999)
        _o = jnp.argsort(dst, stable=True)
        src = src[_o]
        dst = dst[_o]
        edge_weight = jax.random.uniform(jax.random.fold_in(_gk, 13), (25000,), jnp.float32, 0.0, 1)
        return (x, src, dst, edge_weight)
    x, src, dst, edge_weight = _rec_inputs()

    def _L0_gnn_setup():
        import jax, jax.numpy as jnp
        import numpy as np
        N = 100000
        E = 25000
        D = 256
        BN_EPS = 1e-05
        key = jax.random.key(seed)
        ks = jax.random.split(key, 6)
        node_feats = jax.random.normal(ks[0], (N, D), dtype=jnp.float32)
        src = jax.random.randint(ks[1], (E,), 0, N, dtype=jnp.int64)
        dst = jax.random.randint(ks[2], (E,), 0, N, dtype=jnp.int64)
        eps = jnp.zeros((1,), dtype=jnp.float32)
        W1 = jax.random.normal(ks[3], (D, 2 * D), dtype=jnp.float32) * (1.0 / np.sqrt(D))
        b1 = jnp.zeros((2 * D,), dtype=jnp.float32)
        W2 = jax.random.normal(ks[4], (2 * D, D), dtype=jnp.float32) * (1.0 / np.sqrt(2 * D))
        b2 = jnp.zeros((D,), dtype=jnp.float32)
        gamma = jnp.ones((D,), dtype=jnp.float32)
        beta = jnp.zeros((D,), dtype=jnp.float32)
        return {'node_feats': node_feats, 'src': src, 'dst': dst, 'eps': eps, 'W1': W1, 'b1': b1, 'W2': W2, 'b2': b2, 'gamma': gamma, 'beta': beta}
    _L0_gnn_all = _L0_gnn_setup()
    _L0_gnn_in = {k: v for k, v in _L0_gnn_all.items() if k in ('eps', 'W1', 'b1', 'W2', 'b2', 'gamma', 'beta')}
    del _L0_gnn_all

    def _L1_gnn_setup():
        import jax, jax.numpy as jnp
        import numpy as np
        NEG_SLOPE = 0.2
        EPS = 1e-08
        N, E, IN_F, OUT_F, H = (50000, 12500, 256, 32, 8)
        key = jax.random.key(seed)
        k1, k2, k3, k4, k5 = jax.random.split(key, 5)
        x = jax.random.normal(k1, (N, IN_F), dtype=jnp.float32)
        edge_index = jax.random.randint(k2, (2, E), 0, N, dtype=jnp.int32)
        bw = float(np.sqrt(6.0 / (IN_F + OUT_F)))
        W = jax.random.uniform(k3, (H, IN_F, OUT_F), minval=-bw, maxval=bw, dtype=jnp.float32)
        ba = float(np.sqrt(6.0 / (OUT_F + 1)))
        a_src = jax.random.uniform(k4, (H, OUT_F), minval=-ba, maxval=ba, dtype=jnp.float32)
        a_dst = jax.random.uniform(k5, (H, OUT_F), minval=-ba, maxval=ba, dtype=jnp.float32)
        return {'x': x, 'edge_index': edge_index, 'W': W, 'a_src': a_src, 'a_dst': a_dst}
    _L1_gnn_all = _L1_gnn_setup()
    _L1_gnn_in = {k: v for k, v in _L1_gnn_all.items() if k in ('W', 'a_src', 'a_dst')}
    del _L1_gnn_all

    def _L2_gnn_setup():
        import jax, jax.numpy as jnp
        import numpy as np
        N_NODES = 100000
        K_HOPS = 2
        ALPHA = 0.5

        def _gcn_norm(edge_index, edge_weight, num_nodes):
            loops = jnp.arange(num_nodes, dtype=edge_index.dtype)
            src = jnp.concatenate([edge_index[0], loops])
            dst = jnp.concatenate([edge_index[1], loops])
            w = jnp.concatenate([edge_weight, jnp.ones((num_nodes,), edge_weight.dtype)])
            deg = jax.ops.segment_sum(w, dst, num_segments=num_nodes)
            dinv = jnp.where(deg > 0, jax.lax.rsqrt(jnp.maximum(deg, 1e-12)), 0.0)
            norm = dinv[src] * w * dinv[dst]
            return (src, dst, norm)
        key = jax.random.key(seed)
        k1, k2, k3, k4, k5 = jax.random.split(key, 5)
        N, E, D_IN, D_OUT = (N_NODES, 50000, 256, 256)
        x = jax.random.normal(k1, (N, D_IN), dtype=jnp.float32)
        edge_index = jax.random.randint(k2, (2, E), 0, N, dtype=jnp.int64)
        edge_weight = jax.random.uniform(k3, (E,), dtype=jnp.float32)
        W = jax.random.normal(k4, (D_OUT, D_IN), dtype=jnp.float32) / np.sqrt(D_IN)
        b = jax.random.normal(k5, (D_OUT,), dtype=jnp.float32) * 0.01
        return {'x': x, 'edge_index': edge_index, 'edge_weight': edge_weight, 'W': W, 'b': b}
    _L2_gnn_all = _L2_gnn_setup()
    _L2_gnn_in = {k: v for k, v in _L2_gnn_all.items() if k in ('W', 'b')}
    del _L2_gnn_all

    def _L3_gnn_setup():
        import jax, jax.numpy as jnp
        import numpy as np
        N_NODES = 100000
        N_EDGES = 25000
        HIDDEN = 256
        N_LAYERS = 2
        key = jax.random.key(seed)
        k = jax.random.split(key, 7)
        x = jax.random.normal(k[0], (N_NODES, HIDDEN), dtype=jnp.float32)
        edge_index = jax.random.randint(k[1], (2, N_EDGES), 0, N_NODES, dtype=jnp.int64)
        s = 1.0 / np.sqrt(HIDDEN)
        W = jax.random.uniform(k[2], (N_LAYERS, HIDDEN, HIDDEN), jnp.float32, -s, s)
        b = jax.random.uniform(k[3], (N_LAYERS, HIDDEN), jnp.float32, -s, s)
        resW = jax.random.uniform(k[4], (HIDDEN, HIDDEN), jnp.float32, -s, s)
        resb = jax.random.uniform(k[5], (HIDDEN,), jnp.float32, -s, s)
        return {'x': x, 'edge_index': edge_index, 'W': W, 'b': b, 'resW': resW, 'resb': resb}
    _L3_gnn_all = _L3_gnn_setup()
    _L3_gnn_in = {k: v for k, v in _L3_gnn_all.items() if k in ('W', 'b', 'resW', 'resb')}
    del _L3_gnn_all
    return {'x': x, 'src': src, 'dst': dst, 'edge_weight': edge_weight, 'L0_gnn_eps': _L0_gnn_in['eps'], 'L0_gnn_W1': _L0_gnn_in['W1'], 'L0_gnn_b1': _L0_gnn_in['b1'], 'L0_gnn_W2': _L0_gnn_in['W2'], 'L0_gnn_b2': _L0_gnn_in['b2'], 'L0_gnn_gamma': _L0_gnn_in['gamma'], 'L0_gnn_beta': _L0_gnn_in['beta'], 'L1_gnn_W': _L1_gnn_in['W'], 'L1_gnn_a_src': _L1_gnn_in['a_src'], 'L1_gnn_a_dst': _L1_gnn_in['a_dst'], 'L2_gnn_W': _L2_gnn_in['W'], 'L2_gnn_b': _L2_gnn_in['b'], 'L3_gnn_W': _L3_gnn_in['W'], 'L3_gnn_b': _L3_gnn_in['b'], 'L3_gnn_resW': _L3_gnn_in['resW'], 'L3_gnn_resb': _L3_gnn_in['resb']}

def reference(x, src, dst, edge_weight, L0_gnn_eps, L0_gnn_W1, L0_gnn_b1, L0_gnn_W2, L0_gnn_b2, L0_gnn_gamma, L0_gnn_beta, L1_gnn_W, L1_gnn_a_src, L1_gnn_a_dst, L2_gnn_W, L2_gnn_b, L3_gnn_W, L3_gnn_b, L3_gnn_resW, L3_gnn_resb):
    import jax
    import jax.numpy as jnp

    def _L0_gnn_ref(node_feats, src, dst, eps, W1, b1, W2, b2, gamma, beta):
        import jax, jax.numpy as jnp
        import numpy as np
        N = 100000
        E = 25000
        D = 256
        BN_EPS = 1e-05
        n = node_feats.shape[0]
        neigh = jax.ops.segment_sum(node_feats[src], dst, num_segments=n)
        h = (1.0 + eps) * node_feats + neigh
        h = jax.nn.relu(h @ W1 + b1) @ W2 + b2
        mean = jnp.mean(h, axis=0)
        var = jnp.mean(jnp.square(h - mean), axis=0)
        h = (h - mean) * jax.lax.rsqrt(var + BN_EPS) * gamma + beta
        return h

    def _L1_gnn_ref(x, edge_index, W, a_src, a_dst):
        import jax, jax.numpy as jnp
        import numpy as np
        NEG_SLOPE = 0.2
        EPS = 1e-08
        N, E, IN_F, OUT_F, H = (50000, 12500, 256, 32, 8)
        num_nodes = x.shape[0]
        src, dst = (edge_index[0], edge_index[1])
        h = jnp.einsum('ni,hif->hnf', x, W)
        s_src = jnp.einsum('hnf,hf->hn', h, a_src)
        s_dst = jnp.einsum('hnf,hf->hn', h, a_dst)
        ea = (s_src[:, src] + s_dst[:, dst]).T
        ea = jnp.where(ea > 0, ea, NEG_SLOPE * ea)
        m = jax.ops.segment_max(ea, dst, num_segments=num_nodes)
        ea = jnp.exp(ea - m[dst])
        s = jax.ops.segment_sum(ea, dst, num_segments=num_nodes)
        ea = ea / (s[dst] + EPS)
        hn = jnp.transpose(h, (1, 0, 2))
        wf = hn[src] * ea[:, :, None]
        out = jax.ops.segment_sum(wf, dst, num_segments=num_nodes)
        return out.reshape(num_nodes, -1)

    def _L2_gnn_ref(x, edge_index, edge_weight, W, b):
        import jax, jax.numpy as jnp
        import numpy as np
        N_NODES = 100000
        K_HOPS = 2
        ALPHA = 0.5

        def _gcn_norm(edge_index, edge_weight, num_nodes):
            loops = jnp.arange(num_nodes, dtype=edge_index.dtype)
            src = jnp.concatenate([edge_index[0], loops])
            dst = jnp.concatenate([edge_index[1], loops])
            w = jnp.concatenate([edge_weight, jnp.ones((num_nodes,), edge_weight.dtype)])
            deg = jax.ops.segment_sum(w, dst, num_segments=num_nodes)
            dinv = jnp.where(deg > 0, jax.lax.rsqrt(jnp.maximum(deg, 1e-12)), 0.0)
            norm = dinv[src] * w * dinv[dst]
            return (src, dst, norm)
        N = x.shape[0]
        src, dst, norm = _gcn_norm(edge_index, edge_weight, N)
        h = x
        for _ in range(K_HOPS):
            msg = jax.ops.segment_sum(norm[:, None] * h[src], dst, num_segments=N)
            h = (1.0 - ALPHA) * msg + ALPHA * x
        h = jax.nn.relu(h)
        return h @ W.T + b

    def _L3_gnn_ref(x, edge_index, W, b, resW, resb):
        import jax, jax.numpy as jnp
        import numpy as np
        N_NODES = 100000
        N_EDGES = 25000
        HIDDEN = 256
        N_LAYERS = 2
        N = x.shape[0]
        loop = jnp.arange(N, dtype=edge_index.dtype)
        src = jnp.concatenate([edge_index[0], loop])
        dst = jnp.concatenate([edge_index[1], loop])
        ew = jnp.ones(src.shape[0], dtype=x.dtype)
        deg = jax.ops.segment_sum(ew, dst, num_segments=N)
        dis = jnp.where(deg > 0, jax.lax.rsqrt(jnp.where(deg > 0, deg, 1.0)), 0.0)
        norm = dis[src] * ew * dis[dst]
        for l in range(W.shape[0]):
            x_res = x
            h = x @ W[l]
            msg = norm[:, None] * h[src]
            agg = jax.ops.segment_sum(msg, dst, num_segments=N) + b[l]
            x = jax.nn.relu(agg + x_res @ resW + resb)
        return x
    edge_index = jnp.stack([src, dst])
    x = _layernorm(x + _L0_gnn_ref(x, src, dst, L0_gnn_eps, L0_gnn_W1, L0_gnn_b1, L0_gnn_W2, L0_gnn_b2, L0_gnn_gamma, L0_gnn_beta), axis=-1)
    x = _layernorm(x + _L1_gnn_ref(x, edge_index, L1_gnn_W, L1_gnn_a_src, L1_gnn_a_dst), axis=-1)
    x = _layernorm(x + _L2_gnn_ref(x, edge_index, edge_weight, L2_gnn_W, L2_gnn_b), axis=-1)
    x = _layernorm(x + _L3_gnn_ref(x, edge_index, L3_gnn_W, L3_gnn_b, L3_gnn_resW, L3_gnn_resb), axis=-1)
    return x

_drawn_inputs = setup_inputs


def setup_inputs(seed=0):
    import zlib

    import numpy as np

    out = dict(_drawn_inputs(seed))
    spreads = {'L0_gnn_b1': (0.0, 0.1),
     'L0_gnn_b2': (0.0, 0.8),
     'L0_gnn_gamma': (1.0, 0.2),
     'L0_gnn_beta': (0.0, 0.1)}
    factors = {'L2_gnn_b': 6.918}
    for name, (base, spread) in spreads.items():
        noise = np.random.default_rng([zlib.crc32(name.encode()), seed]).standard_normal(out[name].shape)
        drawn = base * np.exp(spread * noise) if base else spread * noise
        out[name] = jnp.asarray(drawn.astype(out[name].dtype))
    for name, factor in factors.items():
        out[name] = (out[name] * factor).astype(out[name].dtype)
    return out
```

```python
from contextlib import ExitStack

import concourse.bass as bass
from concourse import mybir

F32 = mybir.dt.float32
F32R = mybir.dt.float32r
I32 = mybir.dt.int32
U16 = mybir.dt.uint16
ALU = mybir.AluOpType
ACT = mybir.ActivationFunctionType

P = 128
D = 256
KC = D // P
H = 8
DH = D // H
T4 = 4
R4 = 4
BLOCK = P * R4
LN_EPS = 1e-5
BN_EPS = 1e-5
GAT_EPS = 1e-8
NEG_SLOPE = 0.2
BIG = 1e30
SKIP = float(1 << 23)

(KEY, CARRY, SRC, DSTG, SCAT, ROW, ROW_H, C_APPNP, C_GCN, D_HALF, D_KEEP, D_HALF2, DIS, DIS2, EW, LAST) = range(16)
NFIELD = 16


def snap(eng, v):
    return v if isinstance(v, int) else eng.snap(v)


def tail_shape(rows):
    for r in range(1, R4 + 1):
        if rows % r == 0 and rows // r <= P and (rows // r) % 16 == 0:
            return rows // r, r
    raise ValueError(f"no layout for {rows} rows")


class Memory:

    def __init__(self, nc, ctx, phase):
        self.nc, self.ctx, self.phase, self.used = nc, ctx, phase, []
        ctx.callback(self.end)

    def end(self):
        if self.used:
            self.nc.clear_and_free_semaphores(self.used)
            self.nc.all_engine_barrier()

    def sb(self, name, shape, dt=F32):
        return self.ctx.enter_context(self.nc.sbuf_tensor(f"{self.phase}_{name}", shape, dt))

    def ps(self, name, shape):
        return self.ctx.enter_context(self.nc.psum_tensor(f"{self.phase}_{name}_psum", shape, F32))

    def sem(self, name):
        self.used.append(self.nc.alloc_semaphore(f"{self.phase}_{name}"))
        return self.used[-1]

    def sems(self, name, n):
        return [self.sem(f"{name}{i}") for i in range(n)]


class Program:
    pass


def mm3(pe, out, lhs, rhs, first, last):
    for n, (a, b) in enumerate(((0, 0), (0, 1), (1, 0))):
        m = pe.matmul(out, lhs[a], rhs[b], start=first and n == 0, stop=last and n == 2,
                      skip_group_check=True)
    return m




def setup(nc, g):
    N, E, ET, NB = g.N, g.E, g.ET, g.NB
    with ExitStack() as ctx:
        m = Memory(nc, ctx, "set")
        stage = m.sb("stage", [P, 13, 512])
        arow = m.sb("arow", [P, 2, D])
        prod = m.sb("prod", [P, 2, KC, D])
        brow = m.sb("brow", [P, 3, 2, D])
        bg_col = m.sb("bg_col", [P, 2, KC])
        bres_col = m.sb("bres_col", [P, KC])
        eps_in = m.sb("eps_in", [P, 1])
        raw_i = m.sb("raw_i", [P, 3, NB, P], I32)
        raw_f = m.sb("raw_f", [P, 4, NB, P])
        key16 = m.sb("key16", [P, NB, P], U16)
        rowid = m.sb("rowid", [P, ET], I32)
        pid = m.sb("pid", [P, 1], I32)
        pidf = m.sb("pidf", [P, 1])
        p127 = m.sb("p127", [P, 1])
        ones = m.sb("ones", [P, P])
        colf = m.sb("colf", [P, P])
        zeros = m.sb("zeros", [P, 4096])
        nt = m.sb("nt", [g.NTP, g.NTR, 4])
        ps = m.ps("ps", [P, 8, 512])
        load_w = m.sem("load_w")
        load_e = m.sem("load_e")
        blank = m.sem("blank")
        iotas = m.sem("iotas")
        ident_ready = m.sem("ident_ready")
        key16_ready = m.sem("key16_ready")
        rawf_ready = m.sem("rawf_ready")
        fields_copied = m.sem("fields_copied")
        step = m.sem("step")
        turned = m.sem("turned")
        w_turned = m.sem("w_turned")
        zeroed = m.sem("zeroed")
        init = m.sem("init")
        keys_out = m.sem("keys_out")
        keys_in = m.sem("keys_in")

        def two(n):
            return stage[:, n, :].rearrange("p (k n) -> p k n", n=D)

        st_w1 = stage[:, 0:2, :]
        st_w2 = stage[:, 2:4, :].rearrange("p a (b n) -> p (a b) n", n=D)
        st_gat, st_l2, st_g0, st_g1, st_res, st_s0, st_s1, st_l2t, st_at = (two(n) for n in range(4, 13))

        by_k = "(k p) n -> p k n"
        weights = [(st_w1, g.W1.rearrange(by_k, p=P)), (st_w2, g.W2.rearrange(by_k, p=P)),
                   (st_l2, g.WL2.rearrange(by_k, p=P)), (st_g0, g.WL3[0].rearrange(by_k, p=P)),
                   (st_g1, g.WL3[1].rearrange(by_k, p=P)), (st_res, g.resW.rearrange(by_k, p=P)),
                   (arow[:, 0, :], g.a_src.rearrange("(a h) f -> a (h f)", a=1).broadcast_to([P, D])),
                   (arow[:, 1, :], g.a_dst.rearrange("(a h) f -> a (h f)", a=1).broadcast_to([P, D])),
                   (eps_in[:, :], g.eps.rearrange("(a b) -> a b", a=1).broadcast_to([P, 1]))]
        for k in range(KC):
            weights.append((st_gat[:, k, :].rearrange("p (h f) -> p h f", h=H),
                            g.Wgat[:, k * P:(k + 1) * P, :].rearrange("h p f -> p h f")))
        for out, vec in ((g.b1_col[:, :], g.b1), (g.b2_col[:, :], g.b2), (g.gamma_col[:, :], g.gamma),
                         (g.beta_col[:, :], g.beta), (bg_col[:, 0], g.bL3[0]), (bg_col[:, 1], g.bL3[1]),
                         (bres_col[:, :], g.resb)):
            weights.append((out, vec.rearrange("(c p) -> p c", p=P)))
        rows = [(brow[0:1, 0, 0, :], g.bL2), (brow[0:1, 1, 0, :], g.bL3[0]), (brow[0:1, 2, 0, :], g.bL3[1]),
                (brow[0:1, 1, 1, :], g.resb), (brow[0:1, 2, 1, :], g.resb)]
        weights += [(out, vec.rearrange("(a n) -> a n", a=1)) for out, vec in rows]

        edges = []
        for n, (vec, skip) in enumerate(((g.dst, 0), (g.dst, 1), (g.src, 0), (g.ew, 0))):
            tile = raw_i[:, n] if n < 3 else raw_f[:, 3]
            full, rest = divmod(E - skip, P)
            for q in range(NB):
                n_rows = min(P, full - q * P)
                if n_rows > 0:
                    lo = skip + q * P * P
                    edges.append((tile[0:n_rows, q, :], vec[lo:lo + n_rows * P].rearrange("(t p) -> t p", p=P)))
            if rest:
                lo = skip + full * P
                edges.append((tile[full % P:full % P + 1, full // P, 0:rest],
                              vec[lo:lo + rest].rearrange("(a n) -> a n", a=1)))
        zero_rows = N * D // 4096
        zero_n = -(-zero_rows // P)

        block = ctx.enter_context(nc.Block())

        @block.sync
        def _(sp):
            sp.wait_ge(blank, 2)
            sp.wait_ge(blank, 5)
            for out, src in edges:
                sp.dma_start(out, src).then_inc(load_e, 16)
            sp.wait_ge(blank, 6)
            flat = g.agg_table.rearrange("(a r) d -> a (r d)", r=4096 // D)
            for lo in range(0, zero_rows, P):
                n = min(P, zero_rows - lo)
                sp.dma_start(flat[lo:lo + n, :], zeros[0:n, :]).then_inc(zeroed, 16)
            sp.wait_ge(iotas, 3)
            sp.wait_ge(blank, 8)
            sp.dma_start(g.node_table.rearrange("(p r) c -> p (r c)", p=g.NTP),
                         nt[:, :, :].rearrange("p r c -> p (r c)")).then_inc(init, 16)
            sp.wait_ge(key16_ready, 1)
            for q in range(NB):
                n = min(P, ET - q * P)
                sp.dma_start(g.key_rows[0:1, q * P * P:q * P * P + n * P].rearrange("a (t p) -> (a t) p", p=P),
                             key16[0:n, q, :]).then_inc(keys_out, 16)
            sp.wait_ge(keys_out, 16 * NB)
            sp.wait_ge(blank, 9)
            sp.dma_start(g.keys[:, 1:1 + g.EP], g.key_rows.broadcast_to([P, g.EP])).then_inc(keys_in, 16)
            sp.wait_ge(keys_in, 16)
            sp.wait_ge(init, 16)
            sp.wait_ge(zeroed, 16 * zero_n)

        @block.scalar
        def _(act):
            act.wait_ge(blank, 1)
            for out, src in weights:
                act.dma_start(out, src, allow_slow_non_contiguous=True).then_inc(load_w, 16)

        @block.gpsimd
        def _(pool):
            pool.iota(rowid[:, :], [[2 * P, ET // 2], [1, 2]], base=N, channel_multiplier=2).then_inc(iotas, 1)
            pool.iota(pid[:, :], [[1, 1]], base=0, channel_multiplier=1).then_inc(iotas, 1)
            pool.iota(nt[:, :, 0:1].bitcast(I32).rearrange("p r c -> p (r c)"), [[1, g.NTR]], base=0,
                      channel_multiplier=g.NTR).then_inc(iotas, 1)

        @block.vector
        def _(v):
            linked = 0

            def link(ins):
                nonlocal linked
                ins.then_inc(step, 1)
                linked += 1
                v.wait_ge(step, linked)

            v.memset(brow[:, :, :, :], 0.0).then_inc(blank, 1)
            v.memset(raw_i[:, 0:2], N).then_inc(blank, 1)
            v.memset(raw_i[:, 2], 0).then_inc(blank, 1)
            v.memset(raw_f[:, 3], 0.0).then_inc(blank, 1)
            v.memset(g.ln_eps[:, :], LN_EPS).then_inc(blank, 1)
            v.memset(zeros[:, :], 0.0).then_inc(blank, 1)
            v.memset(nt[:, :, 1:3], 1.0).then_inc(blank, 1)
            v.memset(nt[:, :, 3:4], 0.0).then_inc(blank, 1)
            v.memset(g.keys[:, :], 65535).then_inc(blank, 1)
            v.memset(g.edge_fields[:, :, :], 0.0).then_inc(blank, 1)
            v.memset(stage[:, 12, :], 0.0).then_inc(blank, 1)
            v.wait_ge(iotas, 3)
            v.wait_ge(blank, 11)
            link(v.tensor_copy(pidf[:, :], pid[:, :]))
            link(v.memset(ones[:, :], 1.0))
            link(v.tensor_tensor_scan(colf[:, :], ones[:, :], ones[:, :], -1.0, ALU.mult, ALU.add))
            link(v.tensor_scalar(g.ident[:, :], colf[:, :], pidf[:, 0:1], None, ALU.is_equal))
            link(v.tensor_scalar(g.sel0[:, :], ones[:, :], g.ident[:, 0:1], None, ALU.mult))
            v.tensor_scalar(p127[:, :], pidf[:, :], float(P - 1), None, ALU.is_equal).then_inc(ident_ready, 1)
            v.wait_ge(ident_ready, 1)
            v.wait_ge(load_e, 16 * len(edges))
            v.tensor_copy(key16[:, :, :], raw_i[:, 0]).then_inc(key16_ready, 1)
            v.tensor_copy(raw_f[:, 0:3], raw_i[:, :]).then_inc(rawf_ready, 1)
            fields = g.edge_fields
            n_ps = 0
            for field in (KEY, LAST, SRC, EW):
                for q in range(NB):
                    n = min(P, ET - q * P)
                    v.wait_ge(turned, n_ps + 1)
                    v.tensor_copy(fields[:, q * P:q * P + n, field], ps[:, n_ps % 8, 0:n]).then_inc(fields_copied, 1)
                    n_ps += 1
            v.wait_ge(fields_copied, 4 * NB)

            def f(c):
                return fields[:, 0:ET, c]

            link(v.tensor_tensor(f(LAST), f(LAST), f(KEY), ALU.not_equal))
            link(v.tensor_scalar(f(SCAT), f(LAST), -SKIP, SKIP, ALU.mult, ALU.add))
            link(v.tensor_tensor(f(SCAT), f(SCAT), f(KEY), ALU.add))
            link(v.tensor_scalar(f(DSTG), f(KEY), float(N - 1), None, ALU.min))
            link(v.tensor_scalar(fields[:, 1:ET, CARRY], fields[:, 0:ET - 1, KEY], 1.0, p127[:, 0:1],
                                 ALU.add, ALU.mult))
            link(v.tensor_scalar(f(CARRY), f(CARRY), -1.0, None, ALU.add))
            link(v.tensor_copy(g.deg_in[:, :, 0], f(EW)))
            link(v.tensor_tensor(g.deg_in[:, :, 1], f(EW), g.deg_in[:, :, 0].bitcast(F32), ALU.subtract))
            link(v.tensor_scalar(g.deg_in[:, :, 2], f(EW), 0.0, 1.0, ALU.mult, ALU.add))
            link(v.tensor_scalar(g.deg_in[:, :, 3], f(EW), 0.0, None, ALU.mult))
            link(v.tensor_copy(g.slot_row[:, :], rowid[:, :]))

            v.wait_ge(load_w, 16 * len(weights))
            for s in range(2):
                for k in range(KC):
                    link(v.tensor_tensor(prod[:, s, k, :], st_gat[:, k, :], arow[:, s, :], ALU.mult))
                for k in range(KC):
                    link(v.tensor_reduce(st_at[:, k, s * P:s * P + H],
                                         prod[:, s, k].rearrange("p (h f) -> p h f", h=H),
                                         mybir.AxisListType.X, ALU.add))
            link(v.tensor_tensor(st_s0, st_g0, st_res, ALU.add))
            link(v.tensor_tensor(st_s1, st_g1, st_res, ALU.add))
            for l in range(2):
                link(v.tensor_tensor(g.bs_col[:, l], bg_col[:, l], bres_col[:, :], ALU.add))
            link(v.tensor_tensor(brow[:, :, 0, :], brow[:, :, 0, :], brow[:, :, 1, :], ALU.add))
            link(v.tensor_scalar(g.eps1[:, :], eps_in[:, :], 1.0, None, ALU.add))
            v.wait_ge(w_turned, KC * KC)
            for k in range(KC):
                for n in range(KC):
                    link(v.tensor_copy(st_l2t[:, k, n * P:(n + 1) * P], ps[:, 2 * k + n, 0:P]))
            for w, src in ((g.w1, st_w1), (g.w2, st_w2), (g.wl2, st_l2t), (g.wg0, st_g0), (g.wg1, st_g1),
                           (g.wres, st_res), (g.ws0, st_s0), (g.ws1, st_s1), (g.wgat, st_gat), (g.wat, st_at),
                           (g.bias_rows, brow[:, :, 0, :])):
                link(v.tensor_copy(w[:, 0], src))
                link(v.tensor_tensor(w[:, 1], src, w[:, 0].bitcast(F32), ALU.subtract))

        @block.tensor
        def _(pe):
            pe.wait_ge(ident_ready, 1)
            pe.wait_ge(rawf_ready, 1)
            n_ps = 0
            for n in range(4):
                for q in range(NB):
                    n_rows = min(P, ET - q * P)
                    if n_ps >= 8:
                        pe.wait_ge(fields_copied, n_ps - 7)
                    pe.transpose(ps[:, n_ps % 8, 0:n_rows], raw_f[0:n_rows, n, q, :], g.ident[0:n_rows, 0:n_rows]
                                 ).then_inc(turned, 1)
                    n_ps += 1
            pe.wait_ge(fields_copied, 4 * NB)
            pe.wait_ge(load_w, 16 * len(weights))
            for k in range(KC):
                for n in range(KC):
                    pe.transpose(ps[:, 2 * k + n, 0:P], st_l2[:, n, k * P:(k + 1) * P], g.ident[:, :]
                                 ).then_inc(w_turned, 1)




class EdgeSum:

    def __init__(self, m, g, table, index, coef, width=D):
        self.g, self.table, self.index, self.coef, self.width = g, table, index, coef, width
        self.degrees = index == SRC
        self.rows = m.sb("rows", [P, T4, width])
        self.high = m.sb("high", [P, T4, width], F32R)
        self.low = m.sb("low", [P, T4, width], F32R)
        self.same = m.sb("same", [P, T4, P], F32R)
        self.carry = m.sb("carry", [P, T4, P])
        self.here = m.sb("here", [P, T4, NFIELD])
        self.next_index = m.sb("next_index", [P, T4], I32)
        self.summed = m.sb("summed", [P, T4, width + (4 if self.degrees else 0)])
        self.ps = [m.ps(f"sums{b}", [P, 512]) for b in range(T4)]
        self.index_ready = m.sems("index_ready", T4)
        self.index_seen = m.sem("index_seen")
        self.gathered = m.sems("gathered", T4)
        self.here_ready = m.sems("here_ready", T4)
        self.high_ready = m.sems("high_ready", T4)
        self.same_ready = m.sems("same_ready", T4)
        self.low_ready = m.sems("low_ready", T4)
        self.summed_in_psum = m.sems("summed_in_psum", T4)
        self.summed_ready = m.sems("summed_ready", T4)
        self.blank = m.sem("blank")

    def first(self, v):
        v.memset(self.summed[:, :, :], 0.0).then_inc(self.blank, 1)
        for b in range(T4 if self.table is not None else 0):
            v.tensor_copy(self.next_index[:, b:b + 1], self.g.edge_fields[:, b, self.index:self.index + 1]
                          ).then_inc(self.index_ready[b], 1)

    def pool_gather(self, pool, s, b):
        pool.wait_ge(self.index_ready[b], snap(pool, s + 1))
        pool.sem_inc(self.index_seen, 1)
        pool.indirect_dma_start(self.rows[:, b, 0:D], None, self.table,
                                bass.IndirectOffsetOnAxis(self.next_index[:, b:b + 1], 0)
                                ).then_inc(self.gathered[b], 16)

    def act_high(self, act, s, b, s1, s0):
        act.wait_ge(self.here_ready[b], s1)
        act.wait_ge(self.gathered[b], snap(act, s * 16 + 16) if self.table is not None else s1)
        act.wait_ge(self.summed_in_psum[b], s0)
        scale = 1.0 if self.coef is None else self.here[:, b, self.coef:self.coef + 1]
        act.activation(self.high[:, b, :], self.rows[:, b, :], ACT.Copy, scale=scale
                       ).then_inc(self.high_ready[b], 1)

    def act_evacuate(self, act, b, s1):
        act.wait_ge(self.summed_in_psum[b], s1)
        w = self.summed.shape[2]
        act.activation(self.summed[:, b, :], self.ps[b][:, 0:w], ACT.Copy).then_inc(self.summed_ready[b], 1)

    def vec_fields(self, v, s, b, s1, s0, used=()):
        g = self.g
        for sems in used:
            v.wait_ge(sems[b], s0)
        v.wait_ge(self.summed_in_psum[b], s0)
        v.tensor_scalar(self.here[:, b, :], g.edge_fields[:, bass.ds(s * T4 + b, 1), :].rearrange("p a c -> p (a c)"),
                        1.0, None, ALU.mult).then_inc(self.here_ready[b], 1)
        v.wait_ge(self.here_ready[b], s1)
        keys = g.keys[:, bass.ds(s * (T4 * P) + (b * P + 1), P)]
        v.tensor_scalar(self.same[:, b, :], keys, self.here[:, b, KEY:KEY + 1], None, ALU.is_equal)
        v.tensor_scalar(self.carry[:, b, :], keys, self.here[:, b, CARRY:CARRY + 1], None, ALU.is_equal
                        ).then_inc(self.same_ready[b], 1)

    def vec_low(self, v, s, b, s1):
        g = self.g
        v.wait_ge(self.high_ready[b], s1)
        scale = 1.0 if self.coef is None else self.here[:, b, self.coef:self.coef + 1]
        v.scalar_tensor_tensor(out=self.low[:, b, :], in0=self.rows[:, b, :], scalar=scale,
                               in1=self.high[:, b, :].bitcast(F32), op0=ALU.mult, op1=ALU.subtract
                               ).then_inc(self.low_ready[b], 1)
        if self.table is not None:
            v.tensor_scalar(self.next_index[:, b:b + 1],
                            g.edge_fields[:, bass.ds(s * T4 + (T4 + b), 1), self.index], 1.0, None, ALU.mult
                            ).then_inc(self.index_ready[b], 1)

    def pe_sum(self, pe, s, b, s1):
        g = self.g
        pe.wait_ge(self.same_ready[b], s1)
        pe.wait_ge(self.low_ready[b], s1)
        ps, w = self.ps[b], self.width
        pe.wait_ge(self.summed_ready[b], s)
        pe.matmul(ps[:, 0:w], self.same[:, b, :], self.high[:, b, :], start=True, stop=False, skip_group_check=True)
        pe.matmul(ps[:, 0:w], self.same[:, b, :], self.low[:, b, :], start=False, stop=False, skip_group_check=True)
        if self.degrees:
            pe.matmul(ps[:, w:w + 4], self.same[:, b, :],
                      g.deg_in[:, bass.ds(s * T4 + b, 1), :].rearrange("p a c -> p (a c)"),
                      start=False, stop=False, skip_group_check=True)
            w += 4
        if b:
            pe.wait_ge(self.summed_ready[b - 1], s1)
        else:
            pe.wait_ge(self.summed_ready[T4 - 1], s)
            if isinstance(s, int) and s == 0:
                pe.wait_ge(self.blank, 1)
        pe.matmul(ps[:, 0:w], self.carry[:, b, :], self.summed[:, (b - 1) % T4, :], start=False, stop=True,
                  skip_group_check=True).then_inc(self.summed_in_psum[b], 1)


def edge_loop(eng, steps, lead=None, tail1=None, tail2=None, tail3=None):

    def step(s, before, after):
        for b in range(T4):
            if tail3 and b:
                tail3(s, b - 1)
            elif tail3 and before is not None:
                tail3(before, T4 - 1)
            if tail1:
                tail1(s, b)
            if lead and after is not None:
                lead(after, s, b)
            if tail2:
                tail2(s, b)

    if lead:
        for b in range(T4):
            lead(0, None, b)
    step(0, None, 1)
    with eng.Fori(1, steps - 2) as s:
        step(s, snap(eng, s - 1), snap(eng, s + 1))
    step(steps - 2, steps - 3, steps - 1)
    step(steps - 1, steps - 2, None)
    if tail3:
        tail3(steps - 1, T4 - 1)


def slot_rows(table, base, s, duo):
    return table[bass.ds(s * (T4 * P) + (base + duo * 2 * P), 2 * P), :].rearrange("(p j) f -> p j f", p=P)


def edge_layer(nc, g, phase, table, index, coef, states=(), keep=None, self_coef=None, sum_coef=None,
               weights=None, relu_first=False, bias=None, result=None, norm=False):
    ES = g.ES
    degrees = index == SRC
    products = weights is not None
    chunks = KC * (len(weights) if products else 0)
    scatter_to = g.agg_table if degrees else (g.out if result is None else None)
    with ExitStack() as ctx:
        m = Memory(nc, ctx, phase)
        e = EdgeSum(m, g, table, index, coef)
        state = [m.sb(f"state{n}", [P, T4, D]) for n in range(len(states))]
        loaded = [m.sems(f"loaded{n}_", 2) for n in range(len(states))]
        own = m.sb("own", [P, T4, D])
        own_ready = m.sems("own_ready", T4)
        res = m.sb("res", [P, T4, D])
        res_ready = m.sems("res_ready", T4)
        stored = m.sems("stored", 2)
        scattered = m.sems("scattered", T4)
        scatter_ready = m.sems("scatter_ready", T4)
        scatter_seen = m.sem("scatter_seen")
        next_scatter = m.sb("next_scatter", [P, T4], I32)
        deg_ready = m.sems("deg_ready", T4)
        sp_seen = m.sem("sp_seen")
        if products:
            half = m.sb("half", [P, T4, D])
            half_ready = m.sems("half_ready", T4)
            mixed = m.sb("mixed", [P, T4, D])
            mixed_ready = m.sems("mixed_ready", T4)
            turned_ps = [m.ps(f"turned{k}", [P, chunks, P]) for k in range(2)]
            turned_high = m.sb("turned_high", [P, 2, chunks, P], F32R)
            turned_low = m.sb("turned_low", [P, 2, chunks, P], F32R)
            turned = m.sems("turned", T4)
            turned_high_ready = m.sems("turned_high_ready", T4)
            turned_low_ready = m.sems("turned_low_ready", T4)
            layer_ps = [m.ps(f"layer{k}", [P, 512]) for k in range(2)]
            layer_ready = m.sems("layer_ready", T4)
            layer_read = m.sems("layer_read", T4)
        if norm:
            stats = m.sb("stats", [P, T4, 6])
            moments = m.sb("moments", [P, T4, 2])
            dev = m.sb("dev", [P, T4, 2])
            stats_ready = m.sems("stats_ready", T4)
            stats_seen = m.sem("stats_seen")
            var_ready = m.sems("var_ready", T4)
            std_ready = m.sems("std_ready", T4)
            rstd_ready = m.sems("rstd_ready", T4)
        block = ctx.enter_context(nc.Block())

        @block.sync
        def _(sp):
            if not states and result is None:
                return

            def load(s, duo):
                for n, (tab, base) in enumerate(states):
                    sp.wait_ge(res_ready[2 * duo], s)
                    sp.wait_ge(res_ready[2 * duo + 1], s)
                    sp.sem_inc(sp_seen, 1)
                    sp.dma_start(state[n][:, 2 * duo:2 * duo + 2, :], slot_rows(tab, base, s, duo)
                                 ).then_inc(loaded[n][duo], 16)

            def store(s, duo):
                if result is None:
                    return
                s1 = snap(sp, s + 1)
                sp.wait_ge(res_ready[2 * duo], s1)
                sp.wait_ge(res_ready[2 * duo + 1], s1)
                sp.sem_inc(sp_seen, 1)
                sp.dma_start(slot_rows(*result, s, duo), res[:, 2 * duo:2 * duo + 2, :]).then_inc(stored[duo], 16)

            for duo in range(2):
                load(0, duo)
            with sp.Fori(0, ES - 1) as s:
                s1 = snap(sp, s + 1)
                for duo in range(2):
                    load(s1, duo)
                    store(s, duo)
            for duo in range(2):
                store(ES - 1, duo)
                if result is not None:
                    sp.wait_ge(stored[duo], 16 * ES)

        @block.gpsimd
        def _(pool):
            def scatter(s, b, rows, ready):
                s1 = snap(pool, s + 1)
                pool.wait_ge(scatter_ready[b], s1)
                pool.wait_ge(ready[b], s1)
                pool.sem_inc(scatter_seen, 1)
                pool.indirect_dma_start(scatter_to, bass.IndirectOffsetOnAxis(next_scatter[:, b:b + 1], 0),
                                        rows[:, b, 0:D], None, bounds_check=limit, oob_is_err=False
                                        ).then_inc(scattered[b], 16)

            if scatter_to is not None:
                limit = pool.alloc_register(f"{phase}_limit")
                pool.reg_mov(limit, g.N - 1)
            edge_loop(pool, ES, lead=lambda s, before, b: e.pool_gather(pool, s, b),
                      tail1=(lambda s, b: scatter(s, b, e.summed, e.summed_ready)) if degrees else None,
                      tail3=(lambda s, b: scatter(s, b, res, res_ready)) if scatter_to is g.out else None)
            if scatter_to is not None:
                for b in range(T4):
                    pool.wait_ge(scattered[b], 16 * ES)

        @block.scalar
        def _(act):
            def lead(s, before, b):
                e.act_high(act, s, b, snap(act, s + 1), s)
                if b:
                    evacuate(s, b - 1)
                elif before is not None:
                    evacuate(before, T4 - 1)

            def evacuate(s, b):
                if degrees:
                    act.wait_ge(deg_ready[b], s)
                    act.wait_ge(scattered[b], snap(act, s * 16))
                elif products:
                    act.wait_ge(mixed_ready[b], s)
                else:
                    act.wait_ge(res_ready[b], s)
                e.act_evacuate(act, b, snap(act, s + 1))

            def tail1(s, b):
                if isinstance(s, int) and s == ES - 1 and b == 0:
                    evacuate(ES - 1, T4 - 1)
                if keep is None:
                    return
                act.wait_ge(loaded[keep][b // 2], snap(act, s * 16 + 16))
                if products:
                    act.wait_ge(mixed_ready[b], s)
                else:
                    act.wait_ge(res_ready[b], s)
                act.activation(own[:, b, :], state[keep][:, b, :], ACT.Copy,
                               scale=e.here[:, b, self_coef:self_coef + 1]).then_inc(own_ready[b], 1)

            def tail2(s, b):
                s1 = snap(act, s + 1)
                act.wait_ge(turned[b], s1)
                act.wait_ge(layer_ready[(b - 2) % T4], s if b < 2 else s1)
                act.activation(turned_high[:, b % 2], turned_ps[b % 2][:, :, :], ACT.Relu if relu_first else ACT.Copy
                               ).then_inc(turned_high_ready[b], 1)

            def tail3(s, b):
                s1 = snap(act, s + 1)
                if norm:
                    act.wait_ge(var_ready[b], s1)
                    act.activation(dev[:, b, 0:1], moments[:, b, 1:2], ACT.Sqrt, bias=g.ln_eps[:, :]
                                   ).then_inc(std_ready[b], 1)
                else:
                    act.wait_ge(layer_ready[b], s1)
                    act.wait_ge(stored[b // 2], snap(act, s * 16))
                    act.activation(res[:, b, :], layer_ps[b % 2][:, 0:D], ACT.Relu).then_inc(res_ready[b], 1)

            edge_loop(act, ES, lead, tail1, tail2 if products else None, tail3 if products else None)

        @block.vector
        def _(v):
            e.first(v)
            used = [scatter_ready] if scatter_to is not None else []
            used += [] if degrees else [mixed_ready if products else res_ready]

            def lead(s, before, b):
                s1 = snap(v, s + 1)
                e.vec_fields(v, s, b, s1, s, used)
                e.vec_low(v, s, b, s1)

            def tail1(s, b):
                s1 = snap(v, s + 1)
                if scatter_to is not None:
                    v.wait_ge(scattered[b], snap(v, s * 16))
                    v.tensor_copy(next_scatter[:, b:b + 1], e.here[:, b, SCAT:SCAT + 1]).then_inc(scatter_ready[b], 1)
                if degrees:
                    v.wait_ge(e.summed_ready[b], s1)
                    v.tensor_scalar(g.deg[:, bass.ds(s * T4 + b, 1), :].rearrange("p a c -> p (a c)"),
                                    e.summed[:, b, D:D + 4], 1.0, None, ALU.mult).then_inc(deg_ready[b], 1)
                    return
                v.wait_ge(own_ready[b], s1)
                rest = own
                if len(states) > 1 and phase == "hop2":
                    v.wait_ge(loaded[1][b // 2], snap(v, s * 16 + 16))
                    v.scalar_tensor_tensor(out=half[:, b, :], in0=state[1][:, b, :], scalar=0.5, in1=own[:, b, :],
                                           op0=ALU.mult, op1=ALU.add).then_inc(half_ready[b], 1)
                    v.wait_ge(half_ready[b], s1)
                    rest = half
                v.wait_ge(e.summed_ready[b], s1)
                if products:
                    v.wait_ge(turned[b], s)
                    to, ready = mixed, mixed_ready
                else:
                    v.wait_ge(stored[b // 2], snap(v, s * 16))
                    to, ready = res, res_ready
                v.scalar_tensor_tensor(out=to[:, b, :], in0=e.summed[:, b, 0:D],
                                       scalar=e.here[:, b, sum_coef:sum_coef + 1], in1=rest[:, b, :],
                                       op0=ALU.mult, op1=ALU.add).then_inc(ready[b], 1)

            def tail2(s, b):
                s1 = snap(v, s + 1)
                v.wait_ge(turned_high_ready[b], s1)
                high = turned_high[:, b % 2].bitcast(F32)
                if relu_first:
                    ins = v.scalar_tensor_tensor(out=turned_low[:, b % 2], in0=turned_ps[b % 2][:, :, :], scalar=0.0,
                                                 in1=high, op0=ALU.max, op1=ALU.subtract)
                else:
                    ins = v.tensor_tensor(turned_low[:, b % 2], turned_ps[b % 2][:, :, :], high, ALU.subtract)
                ins.then_inc(turned_low_ready[b], 1)

            def tail3(s, b):
                s1 = snap(v, s + 1)
                v.wait_ge(layer_ready[b], s1)
                if scatter_to is None:
                    v.wait_ge(stored[b // 2], snap(v, s * 16))
                else:
                    v.wait_ge(scattered[b], snap(v, s * 16))
                own_row = state[-1]
                v.wait_ge(loaded[-1][b // 2], snap(v, s * 16 + 16))
                last_op = ALU.max if relu_last else ALU.add
                v.scalar_tensor_tensor(out=res[:, b, :], in0=layer_ps[b % 2][:, 0:D], scalar=0.0,
                                       in1=own_row[:, b, :], op0=last_op, op1=ALU.add).then_inc(layer_read[b], 1)
                v.wait_ge(layer_read[b], s1)
                v.bn_stats(stats[:, b, :], res[:, b, :]).then_inc(stats_ready[b], 1)
                v.wait_ge(stats_ready[b], s1)
                v.sem_inc(stats_seen, 1)
                v.bn_aggr(moments[:, b, :], stats[:, b, :]).then_inc(var_ready[b], 1)
                v.wait_ge(std_ready[b], s1)
                v.reciprocal(dev[:, b, 1:2], dev[:, b, 0:1]).then_inc(rstd_ready[b], 1)
                v.wait_ge(rstd_ready[b], s1)
                v.tensor_scalar(res[:, b, :], res[:, b, :], moments[:, b, 0:1], dev[:, b, 1:2],
                                ALU.subtract, ALU.mult).then_inc(res_ready[b], 1)

            relu_last = phase == "gcn2"
            edge_loop(v, ES, lead, tail1, tail2 if products else None, tail3 if norm else None)

        @block.tensor
        def _(pe):
            def tail1(s, b):
                s1 = snap(pe, s + 1)
                pe.wait_ge(mixed_ready[b], s1)
                pe.wait_ge(turned_low_ready[(b - 2) % T4], s if b < 2 else s1)
                rows = [mixed]
                if len(weights) > 1:
                    rows.append(state[0])
                    pe.wait_ge(loaded[0][b // 2], snap(pe, s * 16 + 16))
                for n, row in enumerate(rows):
                    for k in range(KC):
                        ins = pe.transpose(turned_ps[b % 2][:, KC * n + k, :], row[:, b, k * P:(k + 1) * P],
                                           g.ident[:, :])
                ins.then_inc(turned[b], 1)

            def tail2(s, b):
                s1 = snap(pe, s + 1)
                pe.wait_ge(turned_low_ready[b], s1)
                read = layer_read if norm else res_ready
                pe.wait_ge(read[(b - 2) % T4], s if b < 2 else s1)
                out = layer_ps[b % 2][:, 0:D]
                for n in range(2):
                    pe.matmul(out, g.sel0[:, :], g.bias_rows[:, n, bias, :], start=n == 0, stop=False,
                              skip_group_check=True)
                for c in range(chunks):
                    w = weights[c // KC]
                    ins = mm3(pe, out, (turned_high[:, b % 2, c, :], turned_low[:, b % 2, c, :]),
                              (w[:, 0, c % KC, :], w[:, 1, c % KC, :]), False, c == chunks - 1)
                ins.then_inc(layer_ready[b], 1)

            edge_loop(pe, ES, lambda s, before, b: e.pe_sum(pe, s, b, snap(pe, s + 1)),
                      tail1 if products else None, tail2 if products else None)


def gat_scores(nc, g):
    ES, ET = g.ES, g.ET
    with ExitStack() as ctx:
        m = Memory(nc, ctx, "score")
        src_rows = m.sb("src_rows", [P, T4, D])
        dst_rows = m.sb("dst_rows", [P, T4, D])
        next_src = m.sb("next_src", [P, T4], I32)
        next_dst = m.sb("next_dst", [P, T4], I32)
        high = m.sb("high", [P, T4, 2 * KC, P], F32R)
        low = m.sb("low", [P, T4, 2 * KC, P], F32R)
        h_rows = m.sb("h_rows", [P, T4, D])
        raw = m.sb("raw", [H, T4, P])
        fence = m.sb("fence", [H, T4, P])
        lines = m.sb("lines", [H, 2, T4, P])
        turned_ps = [m.ps(f"turned{k}", [P, 2 * KC, P]) for k in range(2)]
        h_ps = [m.ps(f"h{k}", [P, 512]) for k in range(2)]
        s_ps = [m.ps(f"s{k}", [P, 512]) for k in range(2)]
        index_ready = m.sems("index_ready", T4)
        index_seen = m.sem("index_seen")
        src_gathered = m.sems("src_gathered", T4)
        dst_gathered = m.sems("dst_gathered", T4)
        x1_stored = m.sems("x1_stored", 2)
        turned = m.sems("turned", T4)
        high_ready = m.sems("high_ready", T4)
        low_ready = m.sems("low_ready", T4)
        h_done = m.sems("h_done", T4)
        s_done = m.sems("s_done", T4)
        h_ready = m.sems("h_ready", T4)
        h_stored = m.sems("h_stored", 2)
        raw_ready = m.sems("raw_ready", T4)
        fence_ready = m.sems("fence_ready", T4)
        fence_cut = m.sems("fence_cut", T4)
        score_ready = m.sems("score_ready", T4)
        line_ready = m.sems("line_ready", T4)
        lines_stored = m.sem("lines_stored")
        first_line = m.sem("first_line")
        sp_seen = m.sem("sp_seen")

        def slot(b):
            return T4 - 1 - b

        def tile(s, b):
            return (ET - 1 - b) - s * T4

        def turn(s, b):
            return slot((b - 2) % T4), (lambda s1: s if b < 2 else s1)

        block = ctx.enter_context(nc.Block())

        @block.sync
        def _(sp):
            def store_x1(s, duo):
                s16 = snap(sp, s * 16 + 16)
                sp.wait_ge(dst_gathered[2 * duo], s16)
                sp.wait_ge(dst_gathered[2 * duo + 1], s16)
                sp.sem_inc(sp_seen, 1)
                sp.dma_start(slot_rows(g.x1_slots, 0, (ES - 1) - s, duo), dst_rows[:, 2 * duo:2 * duo + 2, :]
                             ).then_inc(x1_stored[duo], 16)

            def store_rest(s):
                s1 = snap(sp, s + 1)
                for duo in (1, 0):
                    sp.wait_ge(h_ready[2 * duo], s1)
                    sp.wait_ge(h_ready[2 * duo + 1], s1)
                    sp.sem_inc(sp_seen, 1)
                    sp.dma_start(slot_rows(g.h_slots, 0, (ES - 1) - s, duo), h_rows[:, 2 * duo:2 * duo + 2, :]
                                 ).then_inc(h_stored[duo], 16)
                for b in range(T4):
                    sp.wait_ge(line_ready[b], s1)
                sp.sem_inc(sp_seen, 1)
                sp.dma_start(g.score_lines[:, :, bass.ds((ES - 1) * T4 * P - s * (T4 * P), T4 * P)],
                             lines[:, :, :, :].rearrange("h a t p -> h a (t p)")).then_inc(lines_stored, 16)

            for duo in (1, 0):
                store_x1(0, duo)
            with sp.Fori(0, ES - 1) as s:
                s1 = snap(sp, s + 1)
                for duo in (1, 0):
                    store_x1(s1, duo)
                store_rest(s)
            store_rest(ES - 1)
            for duo in range(2):
                sp.wait_ge(x1_stored[duo], 16 * ES)
                sp.wait_ge(h_stored[duo], 16 * ES)
            sp.wait_ge(lines_stored, 16 * ES)

        @block.gpsimd
        def _(pool):
            def lead(s, before, b):
                c = slot(b)
                pool.wait_ge(index_ready[c], snap(pool, s + 1))
                pool.wait_ge(x1_stored[c // 2], snap(pool, s * 16))
                pool.sem_inc(index_seen, 1)
                pool.indirect_dma_start(src_rows[:, c, :], None, g.x1_table,
                                        bass.IndirectOffsetOnAxis(next_src[:, c:c + 1], 0)
                                        ).then_inc(src_gathered[c], 16)
                pool.indirect_dma_start(dst_rows[:, c, :], None, g.x1_table,
                                        bass.IndirectOffsetOnAxis(next_dst[:, c:c + 1], 0)
                                        ).then_inc(dst_gathered[c], 16)

            edge_loop(pool, ES, lead)

        @block.tensor
        def _(pe):
            def lead(s, before, b):
                c = slot(b)
                s1 = snap(pe, s + 1)
                s16 = snap(pe, s * 16 + 16)
                prev, count = turn(s, b)
                pe.wait_ge(src_gathered[c], s16)
                pe.wait_ge(dst_gathered[c], s16)
                pe.wait_ge(low_ready[prev], count(s1))
                for n, rows in enumerate((src_rows, dst_rows)):
                    for k in range(KC):
                        ins = pe.transpose(turned_ps[b % 2][:, KC * n + k, :], rows[:, c, k * P:(k + 1) * P],
                                           g.ident[:, :])
                ins.then_inc(turned[c], 1)

            def tail1(s, b):
                c = slot(b)
                s1 = snap(pe, s + 1)
                prev, count = turn(s, b)
                pe.wait_ge(low_ready[c], s1)
                pe.wait_ge(h_ready[prev], count(s1))
                pe.wait_ge(raw_ready[prev], count(s1))
                for k in range(KC):
                    ins = mm3(pe, h_ps[b % 2][:, 0:D], (high[:, c, k, :], low[:, c, k, :]),
                              (g.wgat[:, 0, k, :], g.wgat[:, 1, k, :]), k == 0, k == KC - 1)
                ins.then_inc(h_done[c], 1)
                for n in range(2):
                    for k in range(KC):
                        w = [g.wat[:, part, k, n * P:(n + 1) * P] for part in range(2)]
                        ins = mm3(pe, s_ps[b % 2][:, 0:P], w, (high[:, c, KC * n + k, :], low[:, c, KC * n + k, :]),
                                  n == k == 0, n == 1 and k == KC - 1)
                ins.then_inc(s_done[c], 1)

            edge_loop(pe, ES, lead, tail1)

        @block.scalar
        def _(act):
            def lead(s, before, b):
                c = slot(b)
                act.wait_ge(turned[c], snap(act, s + 1))
                act.wait_ge(s_done[c], s)
                act.activation(high[:, c], turned_ps[b % 2][:, :, :], ACT.Copy).then_inc(high_ready[c], 1)

            def tail1(s, b):
                c = slot(b)
                s1 = snap(act, s + 1)
                act.wait_ge(h_done[c], s1)
                act.wait_ge(h_stored[c // 2], snap(act, s * 16))
                act.activation(h_rows[:, c, :], h_ps[b % 2][:, 0:D], ACT.Copy).then_inc(h_ready[c], 1)
                act.wait_ge(s_done[c], s1)
                act.wait_ge(score_ready[c], s)
                act.activation(raw[:, c, :], s_ps[b % 2][0:H, 0:P], ACT.Copy).then_inc(raw_ready[c], 1)

            edge_loop(act, ES, lead, tail1)

        @block.vector
        def _(v):
            v.memset(lines[:, :, :, :], 0.0).then_inc(first_line, 1)
            for b in range(T4):
                for to, field in ((next_src, SRC), (next_dst, DSTG)):
                    ins = v.tensor_copy(to[:, slot(b):slot(b) + 1], g.edge_fields[:, tile(0, b), field:field + 1])
                ins.then_inc(index_ready[slot(b)], 1)
            v.wait_ge(first_line, 1)

            def lead(s, before, b):
                c = slot(b)
                s1 = snap(v, s + 1)
                v.wait_ge(high_ready[c], s1)
                v.tensor_tensor(low[:, c], turned_ps[b % 2][:, :, :], high[:, c].bitcast(F32), ALU.subtract
                                ).then_inc(low_ready[c], 1)
                if isinstance(s, int) and s == ES - 1:
                    return
                for to, field in ((next_src, SRC), (next_dst, DSTG)):
                    at = (ET - T4 - 1 - b) - s * T4
                    ins = v.tensor_scalar(to[:, c:c + 1], g.edge_fields[:, bass.ds(at, 1), field], 1.0, None, ALU.mult)
                ins.then_inc(index_ready[c], 1)

            def tail1(s, b):
                c = slot(b)
                s1 = snap(v, s + 1)
                at = tile(s, b) * P + 1 if isinstance(s, int) else ((ET - 1 - b) * P + 1) - s * (T4 * P)
                v.tensor_tensor(fence[:, c, :], g.keys[0:H, bass.ds(at, P)], g.keys[0:H, bass.ds(at + 1, P)],
                                ALU.is_equal).then_inc(fence_ready[c], 1)
                v.wait_ge(fence_ready[c], s1)
                v.tensor_scalar(fence[:, c, :], fence[:, c, :], 1.0, BIG, ALU.subtract, ALU.mult
                                ).then_inc(fence_cut[c], 1)
                v.wait_ge(raw_ready[c], s1)
                v.wait_ge(lines_stored, snap(v, s * 16))
                v.scalar_tensor_tensor(out=lines[:, 0, c, :], in0=raw[:, c, :], scalar=NEG_SLOPE, in1=raw[:, c, :],
                                       op0=ALU.mult, op1=ALU.max).then_inc(score_ready[c], 1)
                v.wait_ge(fence_cut[c], s1)
                v.wait_ge(score_ready[c], s1)
                prev = slot((b - 1) % T4)
                v.wait_ge(line_ready[prev], s1 if b else s)
                v.tensor_tensor_scan(lines[:, 1, c, ::-1], fence[:, c, ::-1], lines[:, 0, c, ::-1],
                                     lines[:, 1, prev, 0:1], ALU.add, ALU.max).then_inc(line_ready[c], 1)

            edge_loop(v, ES, lead, tail1)


def gat_sum(nc, g):
    ES = g.ES
    W = D + H
    with ExitStack() as ctx:
        m = Memory(nc, ctx, "gat")
        e = EdgeSum(m, g, None, None, None, width=W)
        lines = m.sb("lines", [H, 2, T4 * P])
        fence = m.sb("fence", [H, T4 * P])
        top = m.sb("top", [H, T4 * P])
        diff = m.sb("diff", [H, T4 * P])
        prob = m.sb("prob", [H, T4 * P])
        prob_ps = m.ps("prob", [P, 512])
        h_rows = m.sb("h_rows", [P, T4, D])
        x1 = m.sb("x1", [P, T4, D])
        den = m.sb("den", [P, T4, 2, H])
        mean = m.sb("mean", [P, T4, D])
        res = m.sb("res", [P, T4, D])
        stats = m.sb("stats", [P, T4, 6])
        moments = m.sb("moments", [P, T4, 2])
        dev = m.sb("dev", [P, 2, T4])
        lines_loaded = m.sem("lines_loaded")
        fence_ready = m.sem("fence_ready")
        fence_cut = m.sem("fence_cut")
        top_ready = m.sem("top_ready")
        diff_ready = m.sem("diff_ready")
        exp_ready = m.sem("exp_ready")
        prob_ready = m.sem("prob_ready")
        h_loaded = m.sems("h_loaded", 2)
        x1_loaded = m.sems("x1_loaded", 2)
        den_ready = m.sems("den_ready", T4)
        rden_ready = m.sems("rden_ready", T4)
        mean_ready = m.sems("mean_ready", T4)
        sum_ready = m.sems("sum_ready", T4)
        stats_ready = m.sems("stats_ready", T4)
        stats_seen = m.sem("stats_seen")
        var_ready = m.sem("var_ready")
        std_ready = m.sem("std_ready")
        rstd_ready = m.sem("rstd_ready")
        res_ready = m.sem("res_ready")
        stored = m.sem("stored")
        sp_seen = m.sem("sp_seen")
        pe_seen = m.sem("pe_seen")
        block = ctx.enter_context(nc.Block())

        def is_last(s):
            return isinstance(s, int) and s == ES - 1

        @block.sync
        def _(sp):
            def load_lines(s):
                sp.wait_ge(diff_ready, s)
                sp.sem_inc(sp_seen, 1)
                sp.dma_start(lines[:, :, :], g.score_lines[:, :, bass.ds(s * (T4 * P), T4 * P)]
                             ).then_inc(lines_loaded, 16)

            def load_h(s):
                for duo in range(2):
                    for b in (2 * duo, 2 * duo + 1):
                        sp.wait_ge(e.gathered[b], s)
                    sp.sem_inc(sp_seen, 1)
                    sp.dma_start(h_rows[:, 2 * duo:2 * duo + 2, :], slot_rows(g.h_slots, 0, s, duo)
                                 ).then_inc(h_loaded[duo], 16)

            def load_x1(s):
                for duo in range(2):
                    for b in (2 * duo, 2 * duo + 1):
                        sp.wait_ge(sum_ready[b], s)
                    sp.sem_inc(sp_seen, 1)
                    sp.dma_start(x1[:, 2 * duo:2 * duo + 2, :], slot_rows(g.x1_slots, 0, s, duo)
                                 ).then_inc(x1_loaded[duo], 16)

            def store(s):
                sp.wait_ge(res_ready, snap(sp, s + 1))
                sp.sem_inc(sp_seen, 1)
                for duo in range(2):
                    sp.dma_start(slot_rows(g.x2_table, g.N, s, duo), res[:, 2 * duo:2 * duo + 2, :]
                                 ).then_inc(stored, 16)

            load_lines(0)
            load_h(0)
            load_lines(1)
            load_x1(0)
            with sp.Fori(0, ES - 2) as s:
                load_h(snap(sp, s + 1))
                load_lines(snap(sp, s + 2))
                load_x1(snap(sp, s + 1))
                store(s)
            load_h(ES - 1)
            load_x1(ES - 1)
            store(ES - 2)
            store(ES - 1)
            sp.wait_ge(stored, 32 * ES)

        @block.tensor
        def _(pe):
            def weigh(s):
                pe.wait_ge(exp_ready, snap(pe, s + 1))
                for b in range(T4):
                    pe.wait_ge(e.gathered[b], s)
                pe.sem_inc(pe_seen, 1)
                for b in range(T4):
                    ins = pe.transpose(prob_ps[:, b * H:(b + 1) * H], prob[:, b * P:(b + 1) * P], g.ident[0:H, 0:H])
                ins.then_inc(prob_ready, 1)

            def lead(s, before, b):
                e.pe_sum(pe, s, b, snap(pe, s + 1))
                if b == T4 - 1 and not is_last(s):
                    weigh(snap(pe, s + 1))

            weigh(0)
            edge_loop(pe, ES, lead)

        @block.scalar
        def _(act):
            def weigh(s):
                act.wait_ge(diff_ready, snap(act, s + 1))
                act.wait_ge(prob_ready, s)
                act.activation(prob[:, :], diff[:, :], ACT.Exp).then_inc(exp_ready, 1)

            def evacuate(s, b):
                act.wait_ge(mean_ready[b], s)
                e.act_evacuate(act, b, snap(act, s + 1))

            def lead(s, before, b):
                e.act_high(act, s, b, snap(act, s + 1), s)
                if b:
                    evacuate(s, b - 1)
                elif before is not None:
                    evacuate(before, T4 - 1)
                if b == T4 - 1 and not is_last(s):
                    weigh(snap(act, s + 1))

            def tail1(s, b):
                if is_last(s) and b == 0:
                    evacuate(ES - 1, T4 - 1)

            def tail3(s, b):
                if b == T4 - 1:
                    act.wait_ge(var_ready, snap(act, s + 1))
                    act.activation(dev[:, 0, :], moments[:, :, 1], ACT.Sqrt, bias=g.ln_eps[:, :]).then_inc(std_ready, 1)

            weigh(0)
            edge_loop(act, ES, lead, tail1, None, tail3)

        @block.vector
        def _(v):
            e.first(v)
            v.memset(top[:, :], 0.0).then_inc(fence_cut, 1)

            def weigh(s):
                s1 = snap(v, s + 1)
                s2 = snap(v, s + 2)
                at = s * (T4 * P)
                v.tensor_tensor(fence[:, :], g.keys[0:H, bass.ds(at + 1, T4 * P)], g.keys[0:H, bass.ds(at, T4 * P)],
                                ALU.is_equal).then_inc(fence_ready, 1)
                v.wait_ge(fence_ready, s1)
                v.tensor_scalar(fence[:, :], fence[:, :], 1.0, BIG, ALU.subtract, ALU.mult).then_inc(fence_cut, 1)
                v.wait_ge(lines_loaded, snap(v, s * 16 + 16))
                v.wait_ge(fence_cut, s2)
                v.wait_ge(top_ready, s)
                v.tensor_tensor_scan(top[:, :], fence[:, :], lines[:, 1, :], top[:, T4 * P - 1:T4 * P],
                                     ALU.add, ALU.max).then_inc(top_ready, 1)
                v.wait_ge(top_ready, s1)
                v.wait_ge(exp_ready, s)
                v.tensor_tensor(diff[:, :], lines[:, 0, :], top[:, :], ALU.subtract).then_inc(diff_ready, 1)

            def lead(s, before, b):
                s1 = snap(v, s + 1)
                if b == 0:
                    v.wait_ge(prob_ready, s1)
                v.wait_ge(h_loaded[b // 2], snap(v, s * 16 + 16))
                p = prob_ps[:, b * H:(b + 1) * H]
                v.tensor_tensor(e.rows[:, b, 0:D].rearrange("p (h f) -> p h f", h=H),
                                h_rows[:, b, :].rearrange("p (h f) -> p h f", h=H),
                                p.unsqueeze(2).broadcast_to([P, H, DH]), ALU.mult)
                v.tensor_copy(e.rows[:, b, D:W], p).then_inc(e.gathered[b], 1)
                e.vec_fields(v, s, b, s1, s)
                e.vec_low(v, s, b, s1)
                if b == T4 - 1 and not is_last(s):
                    weigh(s1)

            def tail1(s, b):
                s1 = snap(v, s + 1)
                v.wait_ge(e.summed_ready[b], s1)
                v.tensor_scalar(den[:, b, 0, :], e.summed[:, b, D:W], GAT_EPS, None, ALU.add).then_inc(den_ready[b], 1)
                v.wait_ge(den_ready[b], s1)
                v.reciprocal(den[:, b, 1, :], den[:, b, 0, :]).then_inc(rden_ready[b], 1)
                v.wait_ge(rden_ready[b], s1)
                v.tensor_tensor(mean[:, b, :].rearrange("p (h f) -> p h f", h=H),
                                e.summed[:, b, 0:D].rearrange("p (h f) -> p h f", h=H),
                                den[:, b, 1, :].unsqueeze(2).broadcast_to([P, H, DH]), ALU.mult
                                ).then_inc(mean_ready[b], 1)
                v.wait_ge(mean_ready[b], s1)
                v.wait_ge(x1_loaded[b // 2], snap(v, s * 16 + 16))
                v.tensor_tensor(mean[:, b, :], mean[:, b, :], x1[:, b, :], ALU.add).then_inc(sum_ready[b], 1)
                v.wait_ge(sum_ready[b], s1)
                v.bn_stats(stats[:, b, :], mean[:, b, :]).then_inc(stats_ready[b], 1)

            def tail3(s, b):
                if b < T4 - 1:
                    return
                s1 = snap(v, s + 1)
                v.wait_ge(stats_ready[T4 - 1], s1)
                v.sem_inc(stats_seen, 1)
                for c in range(T4):
                    ins = v.bn_aggr(moments[:, c, :], stats[:, c, :])
                ins.then_inc(var_ready, 1)
                v.wait_ge(std_ready, s1)
                v.reciprocal(dev[:, 1, :], dev[:, 0, :]).then_inc(rstd_ready, 1)
                v.wait_ge(rstd_ready, s1)
                v.wait_ge(stored, snap(v, s * 32))
                for c in range(T4):
                    ins = v.tensor_scalar(res[:, c, :], mean[:, c, :], moments[:, c, 0:1], dev[:, 1, c:c + 1],
                                          ALU.subtract, ALU.mult)
                ins.then_inc(res_ready, 1)

            weigh(0)
            edge_loop(v, ES, lead, tail1, None, tail3)




class Step:

    def __init__(self, eng, g, i, h, par, loop):
        self.i, self.par = i, par
        last = not loop and i == g.NBLK - 1
        self.parts, self.rows = g.tail if last else (P, R4)
        self.cols = self.parts * self.rows
        self.n, self.n1 = i, snap(eng, i + 1)
        self.h, self.h1 = h, snap(eng, h + 1)
        self.h16, self.h17 = snap(eng, h * 16), snap(eng, h * 16 + 16)

    def nodes(self, table):
        rows = table[bass.ds(self.i * BLOCK, self.cols), :]
        return rows.rearrange("(p r) f -> p r f", p=self.parts)


def block_loop(eng, g, stages):
    lags = [lag for lag, _ in stages]
    most, least = max(lags), min(lags)

    def step(q, c):
        loop = not isinstance(q, int)
        for lag, stage in stages:
            k = c - lag
            i, h = q * 2 + k, q + k // 2
            if loop or 0 <= i < g.NBLK:
                stage(Step(eng, g, i if not loop else eng.snap(i), h if not loop else eng.snap(h), k % 2, loop))

    q0 = (most + 3) // 2
    q1 = (g.NBLK - 2 + least + 1) // 2
    for q in range(q0):
        step(q, 0)
        step(q, 1)
    with eng.Fori(q0, q1) as q:
        step(q, 0)
        step(q, 1)
    q = q1
    while 2 * q <= g.NBLK - 1 + most:
        step(q, 0)
        step(q, 1)
        q += 1


def later(v, k):
    if isinstance(v, int):
        return v + k if v + k > 0 else None
    return v + k


def gin_hidden(nc, g):
    NCH = 2 * D // P
    with ExitStack() as ctx:
        m = Memory(nc, ctx, "gin")
        x = m.sb("x", [P, 2, R4, D])
        agg = m.sb("agg", [P, 2, R4, D])
        xin = m.sb("xin", [P, 2, R4, D])
        x_high = m.sb("x_high", [P, KC, BLOCK], F32R)
        x_low = m.sb("x_low", [P, KC, BLOCK], F32R)
        hid = m.sb("hid", [P, 2, BLOCK])
        hid_high = m.sb("hid_high", [P, NCH, BLOCK], F32R)
        hid_low = m.sb("hid_low", [P, NCH, BLOCK], F32R)
        y = m.sb("y", [P, 2, KC, BLOCK])
        map_index = m.sb("map_index", [P, T4], I32)
        map_rows = m.sb("map_rows", [P, T4, 4])
        x_ps = m.ps("x", [P, KC, BLOCK])
        hid_ps = m.ps("hid", [P, NCH, BLOCK])
        y_ps = m.ps("y", [P, KC, BLOCK])
        x_loaded = m.sems("x_loaded", 2)
        agg_loaded = m.sems("agg_loaded", 2)
        xin_ready = m.sems("xin_ready", 2)
        turned = m.sem("turned")
        x_high_ready = m.sem("x_high_ready")
        x_low_ready = m.sem("x_low_ready")
        hid_done = m.sems("hid_done", NCH)
        hid_ready = m.sems("hid_ready", NCH)
        hid_high_ready = m.sems("hid_high_ready", NCH)
        hid_low_ready = m.sems("hid_low_ready", NCH)
        y_done = m.sem("y_done")
        y_ready = m.sem("y_ready")
        y_stored = m.sems("y_stored", 2)
        stats_seen = m.sem("stats_seen")
        stats_done = m.sem("stats_done")
        map_staged = m.sem("map_staged")
        map_seen = m.sem("map_seen")
        map_written = m.sems("map_written", T4)
        map_read = m.sems("map_read", T4)
        map_kept = m.sem("map_kept")
        sp_seen = m.sem("sp_seen")
        block = ctx.enter_context(nc.Block())

        @block.sync
        def _(sp):
            def load(t):
                sp.wait_ge(xin_ready[t.par], t.h)
                sp.sem_inc(sp_seen, 1)
                sp.dma_start(x[0:t.parts, t.par, 0:t.rows, :], t.nodes(g.x)).then_inc(x_loaded[t.par], 16)
                sp.dma_start(agg[0:t.parts, t.par, 0:t.rows, :], t.nodes(g.agg_table)).then_inc(agg_loaded[t.par], 16)

            def store(t):
                sp.wait_ge(y_ready, t.n1)
                sp.sem_inc(sp_seen, 1)
                sp.dma_start(g.y_table[bass.ds(t.i * P, P), :].rearrange("p (k c) -> p k c", k=KC)[:, :, 0:t.cols],
                             y[:, t.par, :, 0:t.cols]).then_inc(y_stored[t.par], 16)

            block_loop(sp, g, [(0, load), (2, store)])
            for par in range(2):
                sp.wait_ge(y_stored[par], 16 * ((g.NBLK + 1 - par) // 2))

        @block.gpsimd
        def _(pool):
            limit = pool.alloc_register("map_limit")
            pool.reg_mov(limit, g.N - 1)
            with pool.Fori(0, g.ES) as s:
                s1, s17 = pool.snap(s + 1), pool.snap(s * 16 + 16)
                pool.tensor_copy(map_index[:, :], g.edge_fields[:, bass.ds(s * T4, T4), SCAT])
                pool.tensor_copy(map_rows[:, :, :], g.slot_info[:, bass.ds(s * T4, T4), :]).then_inc(map_staged, 1)
                pool.wait_ge(map_staged, s1)
                pool.sem_inc(map_seen, 1)
                for b in range(T4):
                    pool.indirect_dma_start(g.node_table, bass.IndirectOffsetOnAxis(map_index[:, b:b + 1], 0),
                                            map_rows[:, b, :], None, bounds_check=limit, oob_is_err=False
                                            ).then_inc(map_written[b], 16)
                for b in range(T4):
                    pool.wait_ge(map_written[b], s17)
                pool.sem_inc(map_seen, 1)
            with pool.Fori(0, g.ES) as s:
                s17 = pool.snap(s * 16 + 16)
                s1n = pool.snap(s + (g.ES + 1))
                pool.tensor_copy(map_index[:, :], g.edge_fields[:, bass.ds(s * T4, T4), SRC]).then_inc(map_staged, 1)
                pool.wait_ge(map_staged, s1n)
                pool.sem_inc(map_seen, 1)
                for b in range(T4):
                    pool.indirect_dma_start(map_rows[:, b, :], None, g.node_table,
                                            bass.IndirectOffsetOnAxis(map_index[:, b:b + 1], 0)
                                            ).then_inc(map_read[b], 16)
                for b in range(T4):
                    pool.wait_ge(map_read[b], s17)
                pool.sem_inc(map_seen, 1)
                pool.tensor_copy(g.src_info[:, bass.ds(s * T4, T4), :], map_rows[:, :, :]).then_inc(map_kept, 1)

        @block.vector
        def _(v):
            def prepare(t):
                v.wait_ge(x_loaded[t.par], t.h17)
                v.wait_ge(agg_loaded[t.par], t.h17)
                if (n := later(t.n, -1)) is not None:
                    v.wait_ge(turned, snap(v, n))
                v.scalar_tensor_tensor(out=xin[0:t.parts, t.par, 0:t.rows, :], in0=x[0:t.parts, t.par, 0:t.rows, :],
                                       scalar=g.eps1[0:t.parts, :], in1=agg[0:t.parts, t.par, 0:t.rows, :],
                                       op0=ALU.mult, op1=ALU.add).then_inc(xin_ready[t.par], 1)

            def hidden(t):
                for c in range(NCH):
                    v.wait_ge(hid_done[c], t.n1)
                    v.wait_ge(hid_low_ready[(c - 2) % NCH], t.n if c < 2 else t.n1)
                    v.tensor_scalar(hid[:, c % 2, 0:t.cols], hid_ps[:, c, 0:t.cols], g.b1_col[:, c:c + 1], 0.0,
                                    ALU.add, ALU.max).then_inc(hid_ready[c], 1)
                    v.wait_ge(hid_ready[c], t.n1)
                    v.wait_ge(hid_high_ready[c], t.n1)
                    v.tensor_tensor(hid_low[:, c, 0:t.cols], hid[:, c % 2, 0:t.cols],
                                    hid_high[:, c, 0:t.cols].bitcast(F32), ALU.subtract).then_inc(hid_low_ready[c], 1)

            def turned_low(t):
                v.wait_ge(x_high_ready, t.n1)
                v.tensor_tensor(x_low[:, :, 0:t.cols], x_ps[:, :, 0:t.cols], x_high[:, :, 0:t.cols].bitcast(F32),
                                ALU.subtract).then_inc(x_low_ready, 1)

            def moments(t):
                v.wait_ge(y_ready, t.n1)
                v.sem_inc(stats_seen, 1)
                for f in range(KC):
                    ins = v.bn_stats(g.bn_stats[:, f, bass.ds(t.i, 1), :].rearrange("p a c -> p (a c)"),
                                     y[:, t.par, f, 0:t.cols])
                ins.then_inc(stats_done, 1)

            block_loop(v, g, [(0, prepare), (1, hidden), (0, turned_low), (1, moments)])

        @block.scalar
        def _(act):
            def hidden(t):
                for c in range(NCH):
                    act.wait_ge(hid_ready[c], t.n1)
                    if c == 0:
                        act.wait_ge(y_done, t.n)
                    act.activation(hid_high[:, c, 0:t.cols], hid[:, c % 2, 0:t.cols], ACT.Copy
                                   ).then_inc(hid_high_ready[c], 1)

            def turned_high(t):
                act.wait_ge(turned, t.n1)
                act.wait_ge(hid_done[NCH - 1], t.n)
                act.activation(x_high[:, :, 0:t.cols], x_ps[:, :, 0:t.cols], ACT.Copy).then_inc(x_high_ready, 1)

            def evacuate(t):
                act.wait_ge(y_done, t.n1)
                act.wait_ge(y_stored[t.par], t.h16)
                if (n := later(t.n, -1)) is not None:
                    act.wait_ge(stats_done, snap(act, n))
                for f in range(KC):
                    ins = act.activation(y[:, t.par, f, 0:t.cols], y_ps[:, f, 0:t.cols], ACT.Identity,
                                         bias=g.b2_col[:, f:f + 1])
                ins.then_inc(y_ready, 1)

            block_loop(act, g, [(1, hidden), (0, turned_high), (1, evacuate)])

        @block.tensor
        def _(pe):
            def first(t):
                pe.wait_ge(x_low_ready, t.n1)
                for c in range(NCH):
                    pe.wait_ge(hid_low_ready[c], t.n)
                    for k in range(KC):
                        ins = mm3(pe, hid_ps[:, c, 0:t.cols],
                                  [g.w1[:, part, k, c * P:(c + 1) * P] for part in range(2)],
                                  (x_high[:, k, 0:t.cols], x_low[:, k, 0:t.cols]), k == 0, k == KC - 1)
                    ins.then_inc(hid_done[c], 1)

            def turn(t):
                pe.wait_ge(xin_ready[t.par], t.h1)
                pe.wait_ge(x_low_ready, t.n)
                for k in range(KC):
                    for r in range(t.rows):
                        ins = pe.transpose(x_ps[:, k, r * t.parts:(r + 1) * t.parts],
                                           xin[0:t.parts, t.par, r, k * P:(k + 1) * P], g.ident[0:t.parts, 0:t.parts])
                ins.then_inc(turned, 1)

            def second(t):
                for c in range(NCH):
                    pe.wait_ge(hid_low_ready[c], t.n1)
                    if c == 0:
                        pe.wait_ge(y_ready, t.n)
                    for f in range(KC):
                        ins = mm3(pe, y_ps[:, f, 0:t.cols],
                                  [g.w2[:, part, c, f * P:(f + 1) * P] for part in range(2)],
                                  (hid_high[:, c, 0:t.cols], hid_low[:, c, 0:t.cols]), c == 0, c == NCH - 1)
                ins.then_inc(y_done, 1)

            block_loop(pe, g, [(1, first), (0, turn), (1, second)])


def norm_and_fields(nc, g):
    ET = g.ET
    with ExitStack() as ctx:
        m = Memory(nc, ctx, "fin")
        mom = m.sb("mom", [P, KC, 2])
        tmp = m.sb("tmp", [P, KC, 2])
        bn_eps = m.sb("bn_eps", [P, 1])
        step = m.sem("step")
        var_ready = m.sem("var_ready")
        std_ready = m.sem("std_ready")
        block = ctx.enter_context(nc.Block())

        @block.scalar
        def _(act):
            act.wait_ge(var_ready, 1)
            act.activation(tmp[:, :, 0], mom[:, :, 1], ACT.Sqrt, bias=bn_eps[:, :]).then_inc(std_ready, 1)

        @block.vector
        def _(v):
            linked = 0

            def link(ins):
                nonlocal linked
                ins.then_inc(step, 1)
                linked += 1
                v.wait_ge(step, linked)

            link(v.memset(bn_eps[:, :], BN_EPS))
            for f in range(KC):
                ins = v.bn_aggr(mom[:, f, :], g.bn_stats[:, f, :, :].rearrange("p n c -> p (n c)"))
            ins.then_inc(var_ready, 1)
            fields = g.edge_fields

            def f(c):
                return fields[:, 0:ET, c]

            dinv, dis = g.slot_info[:, :, 1], g.slot_info[:, :, 2]
            link(v.tensor_copy(f(ROW), g.src_info[:, :, 0:1].bitcast(I32).rearrange("p t c -> p (t c)")))
            link(v.tensor_scalar(f(ROW_H), f(ROW), float(g.N), float(g.EP), ALU.is_ge, ALU.mult))
            link(v.tensor_tensor(f(ROW_H), f(ROW_H), f(ROW), ALU.add))
            link(v.tensor_tensor(f(C_APPNP), f(EW), g.src_info[:, :, 1], ALU.mult))
            link(v.tensor_copy(f(C_GCN), g.src_info[:, :, 2]))
            link(v.tensor_scalar(f(D_HALF), dinv, 0.5, None, ALU.mult))
            link(v.tensor_tensor(f(D_HALF2), f(D_HALF), dinv, ALU.mult))
            link(v.tensor_scalar(f(D_KEEP), f(D_HALF2), 0.5, None, ALU.add))
            link(v.tensor_copy(f(DIS), dis))
            link(v.tensor_tensor(f(DIS2), dis, dis, ALU.mult))
            v.wait_ge(std_ready, 1)
            link(v.reciprocal(tmp[:, :, 1], tmp[:, :, 0]))
            link(v.tensor_tensor(g.bn_scale[:, :], g.gamma_col[:, :], tmp[:, :, 1], ALU.mult))
            link(v.tensor_tensor(tmp[:, :, 0], mom[:, :, 0], g.bn_scale[:, :], ALU.mult))
            link(v.tensor_tensor(g.bn_shift[:, :], g.beta_col[:, :], tmp[:, :, 0], ALU.subtract))


def degrees(nc, g):
    ET = g.ET
    with ExitStack() as ctx:
        m = Memory(nc, ctx, "deg")
        deg = m.sb("deg", [P, 2, ET])
        held = m.sb("held", [P, 2, ET])
        pos = m.sb("pos", [P, 2, ET])
        zero = m.sb("zero", [P, 1])
        step = m.sem("step")
        held_ready = m.sem("held_ready")
        root_ready = m.sem("root_ready")
        block = ctx.enter_context(nc.Block())

        @block.scalar
        def _(act):
            act.wait_ge(held_ready, 1)
            act.activation(deg[:, :, :], held[:, :, :], ACT.Sqrt, bias=zero[:, :]).then_inc(root_ready, 1)

        @block.vector
        def _(v):
            linked = 0

            def link(ins):
                nonlocal linked
                ins.then_inc(step, 1)
                linked += 1
                v.wait_ge(step, linked)

            link(v.memset(zero[:, :], 0.0))
            link(v.scalar_tensor_tensor(out=deg[:, 0, :], in0=g.deg[:, :, 0], scalar=1.0, in1=g.deg[:, :, 1],
                                        op0=ALU.add, op1=ALU.add))
            link(v.tensor_scalar(deg[:, 1, :], g.deg[:, :, 2], 1.0, None, ALU.add))
            link(v.tensor_scalar(pos[:, :, :], deg[:, :, :], 0.0, None, ALU.is_gt))
            v.tensor_scalar(held[:, :, :], deg[:, :, :], 1e-12, None, ALU.max).then_inc(held_ready, 1)
            v.wait_ge(root_ready, 1)
            link(v.reciprocal(held[:, :, :], deg[:, :, :]))
            link(v.tensor_tensor(g.slot_info[:, :, 1], held[:, 0, :], pos[:, 0, :], ALU.mult))
            link(v.tensor_tensor(g.slot_info[:, :, 2], held[:, 1, :], pos[:, 1, :], ALU.mult))
            link(v.tensor_copy(g.slot_info[:, :, 0:1].bitcast(I32).rearrange("p t c -> p (t c)"), g.slot_row[:, :]))
            link(v.memset(g.slot_info[:, :, 3:4], 0.0))


def dense_layers(nc, g):
    with ExitStack() as ctx:
        m = Memory(nc, ctx, "dense")
        y = m.sb("y", [P, 2, KC, BLOCK])
        x = m.sb("x", [P, 2, R4, D])
        z = m.sb("z", [P, KC, BLOCK])
        raw = [m.sb(f"raw{n}", [P, R4, D]) for n in range(3)]
        rows1 = m.sb("rows1", [P, 2, R4, D])
        rows2 = m.sb("rows2", [P, 2, R4, D])
        rows3 = m.sb("rows3", [P, 2, R4, D])
        rows_y = m.sb("rows_y", [P, 2, R4, D])
        rows4 = m.sb("rows4", [P, 2, R4, D])
        high = [m.sb(f"high{n}", [P, KC, BLOCK], F32R) for n in range(3)]
        low = [m.sb(f"low{n}", [P, KC, BLOCK], F32R) for n in range(3)]
        gcn = m.sb("gcn", [P, KC, BLOCK])
        stats = m.sb("stats", [P, 4, R4, 6])
        mom = m.sb("mom", [P, 4, R4, 2])
        dev = m.sb("dev", [P, 4, 2, R4])
        turned_ps = m.ps("turned", [P, KC, BLOCK])
        layer_ps = m.ps("layer", [P, 2, 512])
        rows_ps = m.ps("rows", [P, R4, D])
        last_ps = m.ps("last", [P, R4, D])
        y_loaded = m.sems("y_loaded", 2)
        x_loaded = m.sems("x_loaded", 2)
        z_ready = m.sem("z_ready")
        z_turned = m.sem("z_turned")
        raw_ready = m.sems("raw_ready", 4)
        stats_ready = m.sems("stats_ready", 4)
        stats_seen = m.sem("stats_seen")
        var_ready = m.sems("var_ready", 4)
        std_ready = m.sems("std_ready", 4)
        rstd_ready = m.sems("rstd_ready", 4)
        norm_seen = m.sem("norm_seen")
        normed = m.sems("normed", 4)
        turned = m.sems("turned", 2)
        high_ready = m.sems("high_ready", 3)
        low_ready = m.sems("low_ready", 3)
        appnp_done = m.sem("appnp_done")
        gcn_done = m.sem("gcn_done")
        gcn_ready = m.sem("gcn_ready")
        gcn_turned = m.sem("gcn_turned")
        rows_y_ready = m.sem("rows_y_ready")
        last_done = m.sem("last_done")
        stored = [m.sems(f"stored{n}_", 2) for n in range(5)]
        sp_seen = m.sem("sp_seen")
        block = ctx.enter_context(nc.Block())

        @block.sync
        def _(sp):
            def load(t):
                n = later(t.n, -1)
                if n is not None:
                    n = snap(sp, n)
                    sp.wait_ge(z_ready, n)
                    sp.sem_inc(sp_seen, 1)
                sp.dma_start(y[:, t.par, :, 0:t.cols],
                             g.y_table[bass.ds(t.i * P, P), :].rearrange("p (k c) -> p k c", k=KC)[:, :, 0:t.cols]
                             ).then_inc(y_loaded[t.par], 16)
                if n is not None:
                    sp.wait_ge(raw_ready[0], n)
                    sp.sem_inc(sp_seen, 1)
                sp.dma_start(x[0:t.parts, t.par, 0:t.rows, :], t.nodes(g.x)).then_inc(x_loaded[t.par], 16)

            def store(n, rows, table, ready):
                def one(t):
                    sp.wait_ge(ready, t.n1)
                    sp.sem_inc(sp_seen, 1)
                    sp.dma_start(t.nodes(table), rows[0:t.parts, t.par, 0:t.rows, :]).then_inc(stored[n][t.par], 16)
                return one

            block_loop(sp, g, [(0, load), (1, store(0, rows1, g.x1_table, normed[0])),
                               (1, store(1, rows2, g.x2_table, normed[1])),
                               (2, store(2, rows3, g.x3_table, normed[2])),
                               (3, store(3, rows_y, g.y1_table, rows_y_ready)),
                               (4, store(4, rows4, g.out, normed[3]))])
            for n in range(5):
                for par in range(2):
                    sp.wait_ge(stored[n][par], 16 * ((g.NBLK + 1 - par) // 2))

        @block.tensor
        def _(pe):
            def turn_rows(t, rows, free):
                for k in range(KC):
                    for r in range(t.rows):
                        ins = pe.transpose(turned_ps[:, k, r * t.parts:(r + 1) * t.parts],
                                           rows[0:t.parts, t.par, r, k * P:(k + 1) * P], g.ident[0:t.parts, 0:t.parts])
                return ins

            def turn_features(t, cols):
                for r in range(t.rows):
                    for k in range(KC):
                        ins = pe.transpose(rows_ps[0:t.parts, r, k * P:(k + 1) * P],
                                           cols[:, k, r * t.parts:(r + 1) * t.parts], g.ident[:, :])
                return ins

            def to_rows(t, out, part, weights, bias):
                for r in range(t.rows):
                    span = slice(r * t.parts, (r + 1) * t.parts)
                    for n in range(2):
                        pe.matmul(out[0:t.parts, r, :], g.sel0[:, 0:t.parts], g.bias_rows[:, n, bias, :],
                                  start=n == 0, stop=False, skip_group_check=True)
                    for k in range(KC):
                        ins = mm3(pe, out[0:t.parts, r, :], (high[part][:, k, span], low[part][:, k, span]),
                                  (weights[:, 0, k, :], weights[:, 1, k, :]), False, k == KC - 1)
                return ins

            def stage4(t):
                pe.wait_ge(low_ready[2], t.n1)
                pe.wait_ge(raw_ready[3], t.n)
                to_rows(t, last_ps, 2, g.ws1, 2).then_inc(last_done, 1)

            def stage3(t):
                pe.wait_ge(normed[2], t.n1)
                pe.wait_ge(low_ready[0], t.n1)
                turn_rows(t, rows3, None).then_inc(turned[1], 1)
                pe.wait_ge(low_ready[1], t.n1)
                pe.wait_ge(raw_ready[2], t.n1)
                for n in range(KC):
                    for k in range(KC):
                        ins = mm3(pe, layer_ps[:, n, 0:t.cols],
                                  [g.ws0[:, part, k, n * P:(n + 1) * P] for part in range(2)],
                                  (high[1][:, k, 0:t.cols], low[1][:, k, 0:t.cols]), k == 0, k == KC - 1)
                ins.then_inc(gcn_done, 1)
                pe.wait_ge(gcn_ready, t.n1)
                n = min(t.n + 2, g.NBLK) if isinstance(t.n, int) else t.n + 2
                pe.wait_ge(raw_ready[0], snap(pe, n))
                turn_features(t, gcn).then_inc(gcn_turned, 1)

            def stage2(t):
                pe.wait_ge(normed[1], t.n1)
                pe.wait_ge(low_ready[1], t.n)
                turn_rows(t, rows2, None).then_inc(turned[0], 1)
                pe.wait_ge(low_ready[0], t.n1)
                pe.wait_ge(gcn_ready, t.n)
                layer = layer_ps[:, :, :].rearrange("p a (b n) -> p (a b) n", n=D)
                to_rows(t, layer, 0, g.wl2, 0).then_inc(appnp_done, 1)

            def stage1(t):
                pe.wait_ge(z_ready, t.n1)
                if (n := later(t.n, -1)) is not None:
                    pe.wait_ge(rows_y_ready, snap(pe, n))
                turn_features(t, z).then_inc(z_turned, 1)

            block_loop(pe, g, [(3, stage4), (2, stage3), (1, stage2), (0, stage1)])

        @block.scalar
        def _(act):
            def std(t, n):
                act.wait_ge(var_ready[n], t.n1)
                act.activation(dev[0:t.parts, n, 0, 0:t.rows], mom[0:t.parts, n, 0:t.rows, 1], ACT.Sqrt,
                               bias=g.ln_eps[0:t.parts, :]).then_inc(std_ready[n], 1)

            def stage4(t):
                std(t, 3)

            def stage3(t):
                act.wait_ge(turned[1], t.n1)
                act.wait_ge(gcn_done, t.n)
                act.activation(high[1][:, :, 0:t.cols], turned_ps[:, :, 0:t.cols], ACT.Copy).then_inc(high_ready[1], 1)
                act.wait_ge(gcn_done, t.n1)
                act.wait_ge(low_ready[2], t.n)
                act.wait_ge(gcn_turned, t.n)
                for n in range(KC):
                    ins = act.activation(gcn[:, n, 0:t.cols], layer_ps[:, n, 0:t.cols], ACT.Relu,
                                         bias=g.bs_col[:, 0, n:n + 1])
                ins.then_inc(gcn_ready, 1)
                act.wait_ge(gcn_ready, t.n1)
                act.wait_ge(last_done, t.n)
                act.activation(high[2][:, :, 0:t.cols], gcn[:, :, 0:t.cols], ACT.Copy).then_inc(high_ready[2], 1)
                act.wait_ge(gcn_turned, t.n1)
                act.wait_ge(stored[3][t.par], t.h16)
                act.activation(rows_y[0:t.parts, t.par, 0:t.rows, :], rows_ps[0:t.parts, 0:t.rows, :], ACT.Copy
                               ).then_inc(rows_y_ready, 1)

            def stage2(t):
                act.wait_ge(turned[0], t.n1)
                act.wait_ge(appnp_done, t.n)
                act.activation(high[0][:, :, 0:t.cols], turned_ps[:, :, 0:t.cols], ACT.Relu).then_inc(high_ready[0], 1)
                std(t, 2)

            def stage1(t):
                act.wait_ge(y_loaded[t.par], t.h17)
                act.wait_ge(z_turned, t.n)
                for f in range(KC):
                    ins = act.activation(z[:, f, 0:t.cols], y[:, t.par, f, 0:t.cols], ACT.Identity,
                                         scale=g.bn_scale[:, f:f + 1], bias=g.bn_shift[:, f:f + 1])
                ins.then_inc(z_ready, 1)
                std(t, 0)
                std(t, 1)

            block_loop(act, g, [(3, stage4), (2, stage3), (1, stage2), (0, stage1)])

        @block.vector
        def _(v):
            def norm_stats(t, n, rows):
                v.wait_ge(raw_ready[n] if n != 1 else normed[0], t.n1)
                for r in range(t.rows):
                    ins = v.bn_stats(stats[0:t.parts, n, r, :], rows[0:t.parts, r, :])
                ins.then_inc(stats_ready[n], 1)
                v.wait_ge(stats_ready[n], t.n1)
                v.wait_ge(normed[n], t.n)
                v.sem_inc(stats_seen, 1)
                for r in range(t.rows):
                    ins = v.bn_aggr(mom[0:t.parts, n, r, :], stats[0:t.parts, n, r, :])
                ins.then_inc(var_ready[n], 1)
                v.wait_ge(std_ready[n], t.n1)
                v.reciprocal(dev[0:t.parts, n, 1, 0:t.rows], dev[0:t.parts, n, 0, 0:t.rows]).then_inc(rstd_ready[n], 1)

            def split(t, part, src, ready, relu=False):
                v.wait_ge(ready, t.n1)
                a, b, c = low[part][:, :, 0:t.cols], src[:, :, 0:t.cols], high[part][:, :, 0:t.cols].bitcast(F32)
                if relu:
                    ins = v.scalar_tensor_tensor(out=a, in0=b, scalar=0.0, in1=c, op0=ALU.max, op1=ALU.subtract)
                else:
                    ins = v.tensor_tensor(a, b, c, ALU.subtract)
                ins.then_inc(low_ready[part], 1)

            def stage4(t):
                v.wait_ge(last_done, t.n1)
                v.wait_ge(normed[3], t.n)
                v.scalar_tensor_tensor(out=raw[2][0:t.parts, 0:t.rows, :], in0=last_ps[0:t.parts, 0:t.rows, :],
                                       scalar=0.0, in1=rows3[0:t.parts, t.par, 0:t.rows, :], op0=ALU.max, op1=ALU.add
                                       ).then_inc(raw_ready[3], 1)
                norm_stats(t, 3, raw[2])

            def stage3(t):
                split(t, 1, turned_ps, high_ready[1])
                split(t, 2, gcn, high_ready[2])

            def stage2(t):
                split(t, 0, turned_ps, high_ready[0], relu=True)
                v.wait_ge(appnp_done, t.n1)
                v.wait_ge(normed[2], t.n)
                layer = layer_ps[:, :, :].rearrange("p a (b n) -> p (a b) n", n=D)
                v.tensor_tensor(raw[1][0:t.parts, 0:t.rows, :], layer[0:t.parts, 0:t.rows, :],
                                rows2[0:t.parts, t.par, 0:t.rows, :], ALU.add).then_inc(raw_ready[2], 1)
                norm_stats(t, 2, raw[1])

            def stage1(t):
                v.wait_ge(z_turned, t.n1)
                v.wait_ge(x_loaded[t.par], t.h17)
                v.wait_ge(normed[0], t.n)
                v.tensor_tensor(raw[0][0:t.parts, 0:t.rows, :], rows_ps[0:t.parts, 0:t.rows, :],
                                x[0:t.parts, t.par, 0:t.rows, :], ALU.add).then_inc(raw_ready[0], 1)
                norm_stats(t, 0, raw[0])
                norm_stats(t, 1, rows1[:, t.par])

            block_loop(v, g, [(3, stage4), (2, stage3), (1, stage2), (0, stage1)])

        @block.gpsimd
        def _(pool):
            def norm(t, n, src, out, table, wait=()):
                pool.wait_ge(rstd_ready[n], t.n1)
                pool.wait_ge(stored[table][t.par], t.h16)
                for sem, value in wait:
                    pool.wait_ge(sem, value)
                pool.sem_inc(norm_seen, 1)
                for r in range(t.rows):
                    ins = pool.tensor_scalar(out[0:t.parts, t.par, r, :], src[0:t.parts, r, :],
                                             mom[0:t.parts, n, r, 0:1], dev[0:t.parts, n, 1, r:r + 1],
                                             ALU.subtract, ALU.mult)
                ins.then_inc(normed[n], 1)

            def stage4(t):
                norm(t, 3, raw[2], rows4, 4)

            def stage2(t):
                n = later(t.n, -1)
                norm(t, 2, raw[1], rows3, 2, [(raw_ready[3], snap(pool, n))] if n is not None else [])

            def stage1(t):
                norm(t, 0, raw[0], rows1, 0)
                n = later(t.n, -1)
                norm(t, 1, rows1[:, t.par], rows2, 1, [(raw_ready[2], snap(pool, n))] if n is not None else [])

            block_loop(pool, g, [(3, stage4), (1, stage2), (0, stage1)])




def gnn_program(nc, x, src, dst, ew, eps, W1, b1, W2, b2, gamma, beta, Wgat, a_src, a_dst, WL2, bL2, WL3, bL3,
                resW, resb, out):
    g = Program()
    g.x, g.src, g.dst, g.ew, g.eps, g.W1, g.b1, g.W2, g.b2 = x, src, dst, ew, eps, W1, b1, W2, b2
    g.gamma, g.beta, g.Wgat, g.a_src, g.a_dst, g.WL2, g.bL2 = gamma, beta, Wgat, a_src, a_dst, WL2, bL2
    g.WL3, g.bL3, g.resW, g.resb, g.out = WL3, bL3, resW, resb, out
    N, E = x.shape[0], src.shape[0]
    g.N, g.E = N, E
    g.ES = -(-E // (T4 * P))
    g.ET = ET = T4 * g.ES
    g.EP = EP = ET * P
    g.NB = -(-ET // P)
    full, rest = divmod(N, BLOCK)
    assert rest and full >= 8 and g.ES >= 4 and N < 65535
    g.NBLK = full + 1
    g.tail = tail_shape(rest)
    g.NTP = max(p for p in range(1, P + 1) if N % p == 0)
    g.NTR = N // g.NTP

    def table(name, shape, dt=F32):
        return nc.dram_tensor(name, shape, dt).ap()

    g.agg_table = table("agg_table", [N, D])
    g.y_table = table("y_table", [g.NBLK * P, KC * BLOCK])
    g.x1_table = table("x1_table", [N, D])
    g.x2_table = table("x2_table", [N + 2 * EP, D])
    g.x3_table = table("x3_table", [N + EP, D])
    g.y1_table = table("y1_table", [N + EP, D])
    g.x1_slots = table("x1_slots", [EP, D])
    g.h_slots = table("h_slots", [EP, D])
    g.score_lines = table("line_table", [H, 2, EP])
    g.node_table = table("node_table", [N, 4])
    g.key_rows = table("key_rows", [1, EP], U16)

    with ExitStack() as ctx:
        m = Memory(nc, ctx, "all")
        g.keys = m.sb("keys", [P, EP + 2], U16)
        g.edge_fields = m.sb("edge_fields", [P, ET + T4, NFIELD])
        g.bn_scale = m.sb("bn_scale", [P, KC])
        g.bn_shift = m.sb("bn_shift", [P, KC])
        g.ident = m.sb("ident", [P, P])
        g.sel0 = m.sb("sel0", [P, P], F32R)
        g.ln_eps = m.sb("ln_eps", [P, 1])
        g.eps1 = m.sb("eps1", [P, 1])
        g.b1_col = m.sb("b1_col", [P, 2 * D // P])
        g.b2_col = m.sb("b2_col", [P, KC])
        g.gamma_col = m.sb("gamma_col", [P, KC])
        g.beta_col = m.sb("beta_col", [P, KC])
        g.bs_col = m.sb("bs_col", [P, 2, KC])
        g.bias_rows = m.sb("bias_rows", [P, 2, 3, D], F32R)
        g.wl2, g.wg0, g.wg1, g.wres, g.ws0, g.ws1, g.wgat, g.wat = (
            m.sb(f"w_{name}", [P, 2, KC, D], F32R)
            for name in ("l2", "gcn0", "gcn1", "res", "sum0", "sum1", "gat", "scores"))

        with ExitStack() as first_half:
            m = Memory(nc, first_half, "half1")
            g.deg_in = m.sb("deg_in", [P, ET, 4], F32R)
            g.deg = m.sb("deg", [P, ET, 4])
            g.slot_row = m.sb("slot_row", [P, ET])
            g.slot_info = m.sb("slot_info", [P, ET, 4])
            g.src_info = m.sb("src_info", [P, ET, 4])
            g.bn_stats = m.sb("bn_stats", [P, KC, g.NBLK, 6])
            g.w1 = m.sb("w1", [P, 2, KC, 2 * D], F32R)
            g.w2 = m.sb("w2", [P, 2, 2 * KC, D], F32R)
            setup(nc, g)
            edge_layer(nc, g, "sum0", g.x, SRC, None)
            degrees(nc, g)
            gin_hidden(nc, g)
            norm_and_fields(nc, g)
        dense_layers(nc, g)
        gat_scores(nc, g)
        gat_sum(nc, g)
        x2, h1 = (g.x2_table, N), (g.x2_table, N + EP)
        x3, y1 = (g.x3_table, N), (g.y1_table, N)
        edge_layer(nc, g, "hop1", g.x2_table[0:N + EP, :], ROW, C_APPNP, [x2], 0, D_KEEP, D_HALF, result=h1)
        edge_layer(nc, g, "hop2", g.x2_table, ROW_H, C_APPNP, [h1, x2], 0, D_HALF2, D_HALF, [g.wl2], True, 0,
                   result=x3, norm=True)
        edge_layer(nc, g, "gcn1", g.x3_table, ROW, C_GCN, [x3], 0, DIS2, DIS, [g.wg0, g.wres], False, 1, result=y1)
        edge_layer(nc, g, "gcn2", g.y1_table, ROW, C_GCN, [y1, x3], 0, DIS2, DIS, [g.wg1, g.wres], False, 2,
                   norm=True)


_INS = ["x", "src", "dst", "edge_weight", "L0_gnn_eps", "L0_gnn_W1", "L0_gnn_b1", "L0_gnn_W2", "L0_gnn_b2",
        "L0_gnn_gamma", "L0_gnn_beta", "L1_gnn_W", "L1_gnn_a_src", "L1_gnn_a_dst", "L2_gnn_W", "L2_gnn_b",
        "L3_gnn_W", "L3_gnn_b", "L3_gnn_resW", "L3_gnn_resb"]


def kernel(**inputs):
    import numpy as _np
    import concourse.bacc as _bacc
    from concourse import mybir as _mybir
    from concourse.bass_utils import run_bass_kernel_spmd as _run

    nc = _bacc.Bacc("TRN2", target_bir_lowering=False, num_devices=1)
    arrays, args = {}, []
    for name in _INS:
        a = _np.ascontiguousarray(inputs[name])
        arrays[f"in_{name}_dram"] = a
        args.append(nc.dram_tensor(f"in_{name}_dram", a.shape, _mybir.dt.from_np(a.dtype), kind="ExternalInput").ap())
    out = nc.dram_tensor("out_0_dram", inputs["x"].shape, _mybir.dt.float32, kind="ExternalOutput").ap()
    gnn_program(nc, *args, out)
    r = _run(nc, [arrays], core_ids=[0])
    return r.results[0]["out_0_dram"]
```

```python
from contextlib import ExitStack

import concourse.bass as bass
from concourse import mybir

F32 = mybir.dt.float32
F32R = mybir.dt.float32r
I32 = mybir.dt.int32
U16 = mybir.dt.uint16
ALU = mybir.AluOpType
ACT = mybir.ActivationFunctionType

P = 128
D = 256
KC = D // P
H = 8
DH = D // H
T8 = 8
T4 = 4
MS = 4
R4 = 4
BLOCK = P * R4
LN_EPS = 1e-5
BN_EPS = 1e-5
GAT_EPS = 1e-8
NEG_SLOPE = 0.2
BIG = 1e30
SKIP = float(1 << 23)

(KEY, CARRY, SRC, DSTG, SCAT, ROW, ROW_H, C_APPNP, C_GCN, D_HALF, D_KEEP, D_HALF2, DIS, DIS2, EW, LAST) = range(16)
NFIELD = 16


def snap(eng, v):
    return v if isinstance(v, int) else eng.snap(v)


def tail_shape(rows):
    for r in range(1, R4 + 1):
        if rows % r == 0 and rows // r <= P and (rows // r) % 16 == 0:
            return rows // r, r
    raise ValueError(f"no layout for {rows} rows")


class Memory:

    def __init__(self, nc, ctx, phase):
        self.nc, self.ctx, self.phase, self.used = nc, ctx, phase, []
        ctx.callback(self.end)

    def end(self):
        if self.used:
            self.nc.clear_and_free_semaphores(self.used)
            self.nc.all_engine_barrier()

    def sb(self, name, shape, dt=F32):
        return self.ctx.enter_context(self.nc.sbuf_tensor(f"{self.phase}_{name}", shape, dt))

    def ps(self, name, shape):
        return self.ctx.enter_context(self.nc.psum_tensor(f"{self.phase}_{name}_psum", shape, F32))

    def sem(self, name):
        self.used.append(self.nc.alloc_semaphore(f"{self.phase}_{name}"))
        return self.used[-1]

    def sems(self, name, n):
        return [self.sem(f"{name}{i}") for i in range(n)]


class Program:
    pass


def mm3(pe, out, lhs, rhs, first, last):
    for n, (a, b) in enumerate(((0, 0), (0, 1), (1, 0))):
        m = pe.matmul(out, lhs[a], rhs[b], start=first and n == 0, stop=last and n == 2,
                      skip_group_check=True)
    return m




def setup(nc, g):
    N, E, ET, NB = g.N, g.E, g.ET, g.NB
    with ExitStack() as ctx:
        m = Memory(nc, ctx, "set")
        stage = m.sb("stage", [P, 13, 512])
        arow = m.sb("arow", [P, 2, D])
        prod = m.sb("prod", [P, 2, KC, D])
        brow = m.sb("brow", [P, 3, 2, D])
        bg_col = m.sb("bg_col", [P, 2, KC])
        bres_col = m.sb("bres_col", [P, KC])
        eps_in = m.sb("eps_in", [P, 1])
        raw_i = m.sb("raw_i", [P, 3, NB, P], I32)
        raw_f = m.sb("raw_f", [P, 4, NB, P])
        key16 = m.sb("key16", [P, NB, P], U16)
        rowid = m.sb("rowid", [P, ET], I32)
        pid = m.sb("pid", [P, 1], I32)
        pidf = m.sb("pidf", [P, 1])
        p127 = m.sb("p127", [P, 1])
        ones = m.sb("ones", [P, P])
        colf = m.sb("colf", [P, P])
        zeros = m.sb("zeros", [P, 4096])
        nt = m.sb("nt", [g.NTP, g.NTR, 4])
        ps = m.ps("ps", [P, 8, 512])
        load_w = m.sem("load_w")
        load_e = m.sem("load_e")
        blank = m.sem("blank")
        iotas = m.sem("iotas")
        ident_ready = m.sem("ident_ready")
        key16_ready = m.sem("key16_ready")
        rawf_ready = m.sem("rawf_ready")
        fields_copied = m.sem("fields_copied")
        step = m.sem("step")
        turned = m.sem("turned")
        w_turned = m.sem("w_turned")
        zeroed = m.sem("zeroed")
        init = m.sem("init")
        keys_out = m.sem("keys_out")
        keys_in = m.sem("keys_in")

        def two(n):
            return stage[:, n, :].rearrange("p (k n) -> p k n", n=D)

        st_w1 = stage[:, 0:2, :]
        st_w2 = stage[:, 2:4, :].rearrange("p a (b n) -> p (a b) n", n=D)
        st_gat, st_l2, st_g0, st_g1, st_res, st_s0, st_s1, st_l2t, st_at = (two(n) for n in range(4, 13))

        by_k = "(k p) n -> p k n"
        weights = [(st_w1, g.W1.rearrange(by_k, p=P)), (st_w2, g.W2.rearrange(by_k, p=P)),
                   (st_l2, g.WL2.rearrange(by_k, p=P)), (st_g0, g.WL3[0].rearrange(by_k, p=P)),
                   (st_g1, g.WL3[1].rearrange(by_k, p=P)), (st_res, g.resW.rearrange(by_k, p=P)),
                   (arow[:, 0, :], g.a_src.rearrange("(a h) f -> a (h f)", a=1).broadcast_to([P, D])),
                   (arow[:, 1, :], g.a_dst.rearrange("(a h) f -> a (h f)", a=1).broadcast_to([P, D])),
                   (eps_in[:, :], g.eps.rearrange("(a b) -> a b", a=1).broadcast_to([P, 1]))]
        for k in range(KC):
            weights.append((st_gat[:, k, :].rearrange("p (h f) -> p h f", h=H),
                            g.Wgat[:, k * P:(k + 1) * P, :].rearrange("h p f -> p h f")))
        for out, vec in ((g.b1_col[:, :], g.b1), (g.b2_col[:, :], g.b2), (g.gamma_col[:, :], g.gamma),
                         (g.beta_col[:, :], g.beta), (bg_col[:, 0], g.bL3[0]), (bg_col[:, 1], g.bL3[1]),
                         (bres_col[:, :], g.resb)):
            weights.append((out, vec.rearrange("(c p) -> p c", p=P)))
        rows = [(brow[0:1, 0, 0, :], g.bL2), (brow[0:1, 1, 0, :], g.bL3[0]), (brow[0:1, 2, 0, :], g.bL3[1]),
                (brow[0:1, 1, 1, :], g.resb), (brow[0:1, 2, 1, :], g.resb)]
        weights += [(out, vec.rearrange("(a n) -> a n", a=1)) for out, vec in rows]

        edges = []
        for n, (vec, skip) in enumerate(((g.dst, 0), (g.dst, 1), (g.src, 0), (g.ew, 0))):
            tile = raw_i[:, n] if n < 3 else raw_f[:, 3]
            full, rest = divmod(E - skip, P)
            for q in range(NB):
                n_rows = min(P, full - q * P)
                if n_rows > 0:
                    lo = skip + q * P * P
                    edges.append((tile[0:n_rows, q, :], vec[lo:lo + n_rows * P].rearrange("(t p) -> t p", p=P)))
            if rest:
                lo = skip + full * P
                edges.append((tile[full % P:full % P + 1, full // P, 0:rest],
                              vec[lo:lo + rest].rearrange("(a n) -> a n", a=1)))
        zero_rows = N * D // 4096
        zero_n = -(-zero_rows // P)

        block = ctx.enter_context(nc.Block())

        @block.sync
        def _(sp):
            sp.wait_ge(blank, 2)
            sp.wait_ge(blank, 5)
            for out, src in edges:
                sp.dma_start(out, src).then_inc(load_e, 16)
            sp.wait_ge(blank, 6)
            flat = g.agg_table.rearrange("(a r) d -> a (r d)", r=4096 // D)
            for lo in range(0, zero_rows, P):
                n = min(P, zero_rows - lo)
                sp.dma_start(flat[lo:lo + n, :], zeros[0:n, :]).then_inc(zeroed, 16)
            sp.wait_ge(iotas, 3)
            sp.wait_ge(blank, 8)
            sp.dma_start(g.node_table.rearrange("(p r) c -> p (r c)", p=g.NTP),
                         nt[:, :, :].rearrange("p r c -> p (r c)")).then_inc(init, 16)
            sp.wait_ge(key16_ready, 1)
            for q in range(NB):
                n = min(P, ET - q * P)
                sp.dma_start(g.key_rows[0:1, q * P * P:q * P * P + n * P].rearrange("a (t p) -> (a t) p", p=P),
                             key16[0:n, q, :]).then_inc(keys_out, 16)
            sp.wait_ge(keys_out, 16 * NB)
            sp.wait_ge(blank, 9)
            sp.dma_start(g.keys[:, 1:1 + g.EP], g.key_rows.broadcast_to([P, g.EP])).then_inc(keys_in, 16)
            sp.wait_ge(keys_in, 16)
            sp.wait_ge(init, 16)
            sp.wait_ge(zeroed, 16 * zero_n)

        @block.scalar
        def _(act):
            act.wait_ge(blank, 1)
            for out, src in weights:
                act.dma_start(out, src, allow_slow_non_contiguous=True).then_inc(load_w, 16)

        @block.gpsimd
        def _(pool):
            pool.iota(rowid[:, :], [[2 * P, ET // 2], [1, 2]], base=N, channel_multiplier=2).then_inc(iotas, 1)
            pool.iota(pid[:, :], [[1, 1]], base=0, channel_multiplier=1).then_inc(iotas, 1)
            pool.iota(nt[:, :, 0:1].bitcast(I32).rearrange("p r c -> p (r c)"), [[1, g.NTR]], base=0,
                      channel_multiplier=g.NTR).then_inc(iotas, 1)

        @block.vector
        def _(v):
            linked = 0

            def link(ins):
                nonlocal linked
                ins.then_inc(step, 1)
                linked += 1
                v.wait_ge(step, linked)

            v.memset(brow[:, :, :, :], 0.0).then_inc(blank, 1)
            v.memset(raw_i[:, 0:2], N).then_inc(blank, 1)
            v.memset(raw_i[:, 2], 0).then_inc(blank, 1)
            v.memset(raw_f[:, 3], 0.0).then_inc(blank, 1)
            v.memset(g.ln_eps[:, :], LN_EPS).then_inc(blank, 1)
            v.memset(zeros[:, :], 0.0).then_inc(blank, 1)
            v.memset(nt[:, :, 1:3], 1.0).then_inc(blank, 1)
            v.memset(nt[:, :, 3:4], 0.0).then_inc(blank, 1)
            v.memset(g.keys[:, :], 65535).then_inc(blank, 1)
            v.memset(g.edge_fields[:, :, :], 0.0).then_inc(blank, 1)
            v.memset(stage[:, 12, :], 0.0).then_inc(blank, 1)
            v.wait_ge(iotas, 3)
            v.wait_ge(blank, 11)
            link(v.tensor_copy(pidf[:, :], pid[:, :]))
            link(v.memset(ones[:, :], 1.0))
            link(v.tensor_tensor_scan(colf[:, :], ones[:, :], ones[:, :], -1.0, ALU.mult, ALU.add))
            link(v.tensor_scalar(g.ident[:, :], colf[:, :], pidf[:, 0:1], None, ALU.is_equal))
            link(v.tensor_scalar(g.sel0[:, :], ones[:, :], g.ident[:, 0:1], None, ALU.mult))
            v.tensor_scalar(p127[:, :], pidf[:, :], float(P - 1), None, ALU.is_equal).then_inc(ident_ready, 1)
            v.wait_ge(ident_ready, 1)
            v.wait_ge(load_e, 16 * len(edges))
            v.tensor_copy(key16[:, :, :], raw_i[:, 0]).then_inc(key16_ready, 1)
            v.tensor_copy(raw_f[:, 0:3], raw_i[:, :]).then_inc(rawf_ready, 1)
            fields = g.edge_fields
            n_ps = 0
            for field in (KEY, LAST, SRC, EW):
                for q in range(NB):
                    n = min(P, ET - q * P)
                    v.wait_ge(turned, n_ps + 1)
                    v.tensor_copy(fields[:, q * P:q * P + n, field], ps[:, n_ps % 8, 0:n]).then_inc(fields_copied, 1)
                    n_ps += 1
            v.wait_ge(fields_copied, 4 * NB)

            def f(c):
                return fields[:, 0:ET, c]

            link(v.tensor_tensor(f(LAST), f(LAST), f(KEY), ALU.not_equal))
            link(v.tensor_scalar(f(SCAT), f(LAST), -SKIP, SKIP, ALU.mult, ALU.add))
            link(v.tensor_tensor(f(SCAT), f(SCAT), f(KEY), ALU.add))
            link(v.tensor_scalar(f(DSTG), f(KEY), float(N - 1), None, ALU.min))
            link(v.tensor_scalar(fields[:, 1:ET, CARRY], fields[:, 0:ET - 1, KEY], 1.0, p127[:, 0:1],
                                 ALU.add, ALU.mult))
            link(v.tensor_scalar(f(CARRY), f(CARRY), -1.0, None, ALU.add))
            link(v.tensor_copy(g.deg_in[:, :, 0], f(EW)))
            link(v.tensor_tensor(g.deg_in[:, :, 1], f(EW), g.deg_in[:, :, 0].bitcast(F32), ALU.subtract))
            link(v.tensor_scalar(g.deg_in[:, :, 2], f(EW), 0.0, 1.0, ALU.mult, ALU.add))
            link(v.tensor_scalar(g.deg_in[:, :, 3], f(EW), 0.0, None, ALU.mult))
            link(v.tensor_copy(g.slot_row[:, :], rowid[:, :]))

            v.wait_ge(load_w, 16 * len(weights))
            for s in range(2):
                for k in range(KC):
                    link(v.tensor_tensor(prod[:, s, k, :], st_gat[:, k, :], arow[:, s, :], ALU.mult))
                for k in range(KC):
                    link(v.tensor_reduce(st_at[:, k, s * P:s * P + H],
                                         prod[:, s, k].rearrange("p (h f) -> p h f", h=H),
                                         mybir.AxisListType.X, ALU.add))
            link(v.tensor_tensor(st_s0, st_g0, st_res, ALU.add))
            link(v.tensor_tensor(st_s1, st_g1, st_res, ALU.add))
            for l in range(2):
                link(v.tensor_tensor(g.bs_col[:, l], bg_col[:, l], bres_col[:, :], ALU.add))
            link(v.tensor_tensor(brow[:, :, 0, :], brow[:, :, 0, :], brow[:, :, 1, :], ALU.add))
            link(v.tensor_scalar(g.eps1[:, :], eps_in[:, :], 1.0, None, ALU.add))
            v.wait_ge(w_turned, KC * KC)
            for k in range(KC):
                for n in range(KC):
                    link(v.tensor_copy(st_l2t[:, k, n * P:(n + 1) * P], ps[:, 2 * k + n, 0:P]))
            for w, src in ((g.w1, st_w1), (g.w2, st_w2), (g.wl2, st_l2t), (g.wg0, st_g0), (g.wg1, st_g1),
                           (g.wres, st_res), (g.ws0, st_s0), (g.ws1, st_s1), (g.wgat, st_gat), (g.wat, st_at),
                           (g.bias_rows, brow[:, :, 0, :])):
                link(v.tensor_copy(w[:, 0], src))
                link(v.tensor_tensor(w[:, 1], src, w[:, 0].bitcast(F32), ALU.subtract))

        @block.tensor
        def _(pe):
            pe.wait_ge(ident_ready, 1)
            pe.wait_ge(rawf_ready, 1)
            n_ps = 0
            for n in range(4):
                for q in range(NB):
                    n_rows = min(P, ET - q * P)
                    if n_ps >= 8:
                        pe.wait_ge(fields_copied, n_ps - 7)
                    pe.transpose(ps[:, n_ps % 8, 0:n_rows], raw_f[0:n_rows, n, q, :], g.ident[0:n_rows, 0:n_rows]
                                 ).then_inc(turned, 1)
                    n_ps += 1
            pe.wait_ge(fields_copied, 4 * NB)
            pe.wait_ge(load_w, 16 * len(weights))
            for k in range(KC):
                for n in range(KC):
                    pe.transpose(ps[:, 2 * k + n, 0:P], st_l2[:, n, k * P:(k + 1) * P], g.ident[:, :]
                                 ).then_inc(w_turned, 1)




class Tile:

    def __init__(self, values, k):
        self.values, self.k = values, k
        self.b, self.m = k % T8, k % MS
        self.s, self.s1, self.s2 = (values.s.get(k // T8 + n) for n in range(3))
        self.now = values.now(k // MS + 1)
        self.d16, self.d17 = values.dma(k // T8), values.dma(k // T8 + 1)
        self.duo = self.b // 2

    def back(self, d):
        return Tile(self.values, self.k - d)

    def at(self, step):
        return self.s * (T8 * step) + self.b * step


class Values:

    def __init__(self, eng, q, most, dma):
        self.q, self.loop = q, not isinstance(q, int)
        low = -(-most // T8)
        self.s = {o: snap(eng, q + o) if o else q for o in range(-low, 3)}
        if self.loop:
            self.nows = {o: snap(eng, q * (T8 // MS) + o) for o in range((-most) // MS + 1 - T8 // MS, T8 // MS + 1)}
            self.dmas = {o: snap(eng, (q + o) * 16) for o in range(-low, 2)} if dma else {}

    def now(self, o):
        if self.loop:
            return self.nows.get(o)
        return max(0, self.q * (T8 // MS) + o)

    def dma(self, o):
        if self.loop:
            return self.dmas.get(o)
        return max(0, (self.q + o) * 16)


def tile_loop(eng, steps, stages, dma=True):
    most = max(lag for lag, _ in stages)

    def step(q):
        values = Values(eng, q, most, dma)
        for c in range(T8):
            for lag, work in stages:
                if values.loop or 0 <= q * T8 + c - lag < steps * T8:
                    work(Tile(values, c - lag))

    q0 = 1 + -(-most // T8)
    for q in range(q0):
        step(q)
    with eng.Fori(q0, steps) as q:
        step(q)
    for q in range(steps, steps - 1 + q0):
        step(q)


class EdgeSum:

    def __init__(self, m, g, table, index, coef, width=D):
        self.g, self.table, self.index, self.coef, self.width = g, table, index, coef, width
        self.degrees = index == SRC
        self.rows = m.sb("rows", [P, T8, width])
        self.high = m.sb("high", [P, MS, width], F32R)
        self.low = m.sb("low", [P, MS, width], F32R)
        self.same = m.sb("same", [P, MS, P], F32R)
        self.carry = m.sb("carry", [P, MS, P])
        self.here = m.sb("here", [P, T8, NFIELD])
        self.next_index = m.sb("next_index", [P, T8], I32)
        self.summed = m.sb("summed", [P, T8, width + (4 if self.degrees else 0)])
        self.ps = [m.ps(f"sums{b}", [P, 512]) for b in range(2)]
        self.index_ready = m.sems("index_ready", MS)
        self.index_seen = m.sem("index_seen")
        self.gathered = m.sems("gathered", T8 if table is not None else MS)
        self.here_ready = m.sems("here_ready", MS)
        self.high_ready = m.sems("high_ready", MS)
        self.same_ready = m.sems("same_ready", MS)
        self.low_ready = m.sems("low_ready", MS)
        self.summed_in_psum = m.sems("summed_in_psum", MS)
        self.summed_ready = m.sems("summed_ready", MS)
        self.blank = m.sem("blank")

    def first(self, v):
        v.memset(self.summed[:, :, :], 0.0).then_inc(self.blank, 1)
        for b in range(T8 if self.table is not None else 0):
            v.tensor_copy(self.next_index[:, b:b + 1], self.g.edge_fields[:, b, self.index:self.index + 1]
                          ).then_inc(self.index_ready[b % MS], 1)

    def pool_gather(self, pool, t):
        pool.wait_ge(self.index_ready[t.m], t.now)
        pool.sem_inc(self.index_seen, 1)
        pool.indirect_dma_start(self.rows[:, t.b, 0:D], None, self.table,
                                bass.IndirectOffsetOnAxis(self.next_index[:, t.b:t.b + 1], 0)
                                ).then_inc(self.gathered[t.b], 16)

    def act_high(self, act, t):
        if self.coef is not None:
            act.wait_ge(self.here_ready[t.m], t.now)
        if self.table is not None:
            act.wait_ge(self.gathered[t.b], t.d17)
        else:
            act.wait_ge(self.gathered[t.m], t.now)
        act.wait_ge(self.summed_in_psum[t.m], t.back(MS).now)
        scale = 1.0 if self.coef is None else self.here[:, t.b, self.coef:self.coef + 1]
        act.activation(self.high[:, t.m, :], self.rows[:, t.b, :], ACT.Copy, scale=scale
                       ).then_inc(self.high_ready[t.m], 1)

    def act_evacuate(self, act, t):
        act.wait_ge(self.summed_in_psum[t.m], t.now)
        w = self.summed.shape[2]
        act.activation(self.summed[:, t.b, :], self.ps[t.b % 2][:, 0:w], ACT.Copy
                       ).then_inc(self.summed_ready[t.m], 1)

    def vec_fields(self, v, t):
        g = self.g
        v.wait_ge(self.summed_in_psum[t.m], t.back(MS).now)
        v.tensor_scalar(self.here[:, t.b, :], g.edge_fields[:, bass.ds(t.at(1), 1), :].rearrange("p a c -> p (a c)"),
                        1.0, None, ALU.mult).then_inc(self.here_ready[t.m], 1)
        v.wait_ge(self.here_ready[t.m], t.now)
        keys = g.keys[:, bass.ds(t.at(P) + 1, P)]
        v.tensor_scalar(self.same[:, t.m, :], keys, self.here[:, t.b, KEY:KEY + 1], None, ALU.is_equal)
        v.tensor_scalar(self.carry[:, t.m, :], keys, self.here[:, t.b, CARRY:CARRY + 1], None, ALU.is_equal
                        ).then_inc(self.same_ready[t.m], 1)

    def vec_low(self, v, t):
        g = self.g
        v.wait_ge(self.high_ready[t.m], t.now)
        scale = 1.0 if self.coef is None else self.here[:, t.b, self.coef:self.coef + 1]
        v.scalar_tensor_tensor(out=self.low[:, t.m, :], in0=self.rows[:, t.b, :], scalar=scale,
                               in1=self.high[:, t.m, :].bitcast(F32), op0=ALU.mult, op1=ALU.subtract
                               ).then_inc(self.low_ready[t.m], 1)
        if self.table is not None:
            v.wait_ge(self.low_ready[t.m], t.now)
            v.tensor_scalar(self.next_index[:, t.b:t.b + 1],
                            g.edge_fields[:, bass.ds(t.at(1) + T8, 1), self.index], 1.0, None, ALU.mult
                            ).then_inc(self.index_ready[t.m], 1)

    def pe_sum(self, pe, t):
        g = self.g
        pe.wait_ge(self.same_ready[t.m], t.now)
        pe.wait_ge(self.low_ready[t.m], t.now)
        ps, w = self.ps[t.b % 2], self.width
        last = t.back(2)
        pe.wait_ge(self.summed_ready[last.m], last.now)
        pe.matmul(ps[:, 0:w], self.same[:, t.m, :], self.high[:, t.m, :], start=True, stop=False,
                  skip_group_check=True)
        pe.matmul(ps[:, 0:w], self.same[:, t.m, :], self.low[:, t.m, :], start=False, stop=False,
                  skip_group_check=True)
        if self.degrees:
            pe.matmul(ps[:, w:w + 4], self.same[:, t.m, :],
                      g.deg_in[:, bass.ds(t.at(1), 1), :].rearrange("p a c -> p (a c)"),
                      start=False, stop=False, skip_group_check=True)
            w += 4
        before = t.back(1)
        if isinstance(t.s, int) and t.s == 0 and t.b == 0:
            pe.wait_ge(self.blank, 1)
        else:
            pe.wait_ge(self.summed_ready[before.m], before.now)
        pe.matmul(ps[:, 0:w], self.carry[:, t.m, :], self.summed[:, before.b, :], start=False, stop=True,
                  skip_group_check=True).then_inc(self.summed_in_psum[t.m], 1)


def edge_loop(eng, steps, lead=None, tail1=None):

    def step(s, before, after):
        for b in range(T4):
            if tail1:
                tail1(s, b)
            if lead and after is not None:
                lead(after, s, b)

    if lead:
        for b in range(T4):
            lead(0, None, b)
    step(0, None, 1)
    with eng.Fori(1, steps - 2) as s:
        step(s, snap(eng, s - 1), snap(eng, s + 1))
    step(steps - 2, steps - 3, steps - 1)
    step(steps - 1, steps - 2, None)


def slot_rows(table, base, s, duo, tiles=None):
    tiles = tiles or T4
    return table[bass.ds(s * (tiles * P) + (base + duo * 2 * P), 2 * P), :].rearrange("(p j) f -> p j f", p=P)


def edge_layer(nc, g, phase, table, index, coef, states=(), self_coef=None, sum_coef=None,
               weights=None, relu_first=False, bias=None, result=None, norm=False):
    ES = g.ES
    degrees = index == SRC
    products = weights is not None
    halves = len(states) > 1 and relu_first
    chunks = KC * (len(weights) if products else 0)
    scatter_to = g.agg_table if degrees else (g.out if result is None else None)
    with ExitStack() as ctx:
        m = Memory(nc, ctx, phase)
        e = EdgeSum(m, g, table, index, coef)
        state = [m.sb(f"state{n}", [P, T8, D]) for n in range(len(states))]
        loaded = [m.sems(f"loaded{n}_", T8 // 2) for n in range(len(states))]
        own = m.sb("own", [P, MS, D])
        own_ready = m.sems("own_ready", MS)
        res = m.sb("res", [P, T8, D])
        res_ready = m.sems("res_ready", MS)
        stored = m.sems("stored", T8 // 2)
        scattered = m.sems("scattered", T8)
        scatter_ready = m.sems("scatter_ready", MS)
        scatter_seen = m.sem("scatter_seen")
        next_scatter = m.sb("next_scatter", [P, T8], I32)
        deg_ready = m.sems("deg_ready", MS)
        sp_seen = m.sem("sp_seen")
        half_ready = m.sems("half_ready", MS)
        mixed_ready = m.sems("mixed_ready", MS)
        turned = m.sems("turned", MS)
        turned_high_ready = m.sems("turned_high_ready", MS)
        turned_low_ready = m.sems("turned_low_ready", MS)
        layer_ready = m.sems("layer_ready", MS)
        layer_read = m.sems("layer_read", MS)
        if products:
            mixed = m.sb("mixed", [P, MS, D])
            turned_ps = [m.ps(f"turned{k}", [P, chunks, P]) for k in range(2)]
            turned_high = m.sb("turned_high", [P, 2, chunks, P], F32R)
            turned_low = m.sb("turned_low", [P, 2, chunks, P], F32R)
            layer_ps = [m.ps(f"layer{k}", [P, 512]) for k in range(2)]
        if norm:
            stats = m.sb("stats", [P, MS, 6])
            moments = m.sb("moments", [P, MS, 2])
            dev = m.sb("dev", [P, MS, 2])
            stats_ready = m.sems("stats_ready", MS)
            stats_seen = m.sem("stats_seen")
            var_ready = m.sems("var_ready", MS)
            std_ready = m.sems("std_ready", MS)
            rstd_ready = m.sems("rstd_ready", MS)
        state_read = layer_read if norm else (turned if products else own_ready)
        block = ctx.enter_context(nc.Block())

        @block.sync
        def _(sp):
            def load(t):
                if t.b % 2:
                    return
                for n, (tab, base) in enumerate(states):
                    for last in (t.back(T8), t.back(T8 - 1)):
                        sp.wait_ge(state_read[last.m], last.now)
                    sp.sem_inc(sp_seen, 1)
                    sp.dma_start(state[n][:, t.b:t.b + 2, :], slot_rows(tab, base, t.s, t.duo, T8)
                                 ).then_inc(loaded[n][t.duo], 16)

            def store(t):
                if t.b % 2 == 0:
                    return
                sp.wait_ge(res_ready[t.back(1).m], t.back(1).now)
                sp.wait_ge(res_ready[t.m], t.now)
                sp.sem_inc(sp_seen, 1)
                sp.dma_start(slot_rows(*result, t.s, t.duo, T8), res[:, t.b - 1:t.b + 1, :]).then_inc(stored[t.duo], 16)

            stages = [(0, load)] if states else []
            if result is not None:
                stages.append((T8, store))
            if stages:
                tile_loop(sp, ES, stages, dma=False)
            if result is not None:
                for duo in range(T8 // 2):
                    sp.wait_ge(stored[duo], 16 * ES)

        @block.gpsimd
        def _(pool):
            def scatter(t):
                pool.wait_ge(scatter_ready[t.m], t.now)
                pool.wait_ge(scatter_from_ready[t.m], t.now)
                pool.sem_inc(scatter_seen, 1)
                pool.indirect_dma_start(scatter_to, bass.IndirectOffsetOnAxis(next_scatter[:, t.b:t.b + 1], 0),
                                        scatter_from[:, t.b, 0:D], None, bounds_check=limit, oob_is_err=False
                                        ).then_inc(scattered[t.b], 16)

            scatter_from, scatter_from_ready = (e.summed, e.summed_ready) if degrees else (res, res_ready)
            stages = [(0, lambda t: e.pool_gather(pool, t))]
            if scatter_to is not None:
                limit = pool.alloc_register(f"{phase}_limit")
                pool.reg_mov(limit, g.N - 1)
                stages.append((6 if degrees else 8, scatter))
            tile_loop(pool, ES, stages, dma=False)
            if scatter_to is not None:
                for b in range(T8):
                    pool.wait_ge(scattered[b], 16 * ES)

        @block.scalar
        def _(act):
            def evacuate(t):
                if degrees:
                    act.wait_ge(deg_ready[t.m], t.back(T8).now)
                    act.wait_ge(scattered[t.b], t.d16)
                elif products:
                    act.wait_ge(mixed_ready[t.m], t.back(T8).now)
                else:
                    act.wait_ge(res_ready[t.m], t.back(T8).now)
                e.act_evacuate(act, t)

            def own_row(t):
                act.wait_ge(loaded[0][t.duo], t.d17)
                act.wait_ge(e.here_ready[t.m], t.now)
                act.wait_ge((mixed_ready if products else res_ready)[t.m], t.back(MS).now)
                act.activation(own[:, t.m, :], state[0][:, t.b, :], ACT.Copy,
                               scale=e.here[:, t.b, self_coef:self_coef + 1]).then_inc(own_ready[t.m], 1)

            def high_turned(t):
                act.wait_ge(turned[t.m], t.now)
                act.wait_ge(layer_ready[t.back(2).m], t.back(2).now)
                act.activation(turned_high[:, t.b % 2], turned_ps[t.b % 2][:, :, :],
                               ACT.Relu if relu_first else ACT.Copy).then_inc(turned_high_ready[t.m], 1)

            def root(t):
                act.wait_ge(var_ready[t.m], t.now)
                act.activation(dev[:, t.m, 0:1], moments[:, t.m, 1:2], ACT.Sqrt, bias=g.ln_eps[:, :]
                               ).then_inc(std_ready[t.m], 1)

            def finish(t):
                act.wait_ge(layer_ready[t.m], t.now)
                act.wait_ge(stored[t.duo], t.d16)
                act.activation(res[:, t.b, :], layer_ps[t.b % 2][:, 0:D], ACT.Relu).then_inc(res_ready[t.m], 1)

            stages = [(8, root)] if norm else []
            stages += [(6, high_turned)] if products else []
            stages += [(3, lambda t: e.act_high(act, t))]
            stages += [(4, own_row)] if states else []
            stages += [(7, finish)] if products and not norm else []
            stages += [(4, evacuate)]
            tile_loop(act, ES, stages)

        @block.vector
        def _(v):
            e.first(v)

            def fields(t):
                last = t.back(T8)
                if scatter_to is not None:
                    v.wait_ge(scatter_ready[t.m], last.now)
                if not degrees:
                    v.wait_ge((mixed_ready if products else res_ready)[t.m], last.now)
                e.vec_fields(v, t)

            def scatter_index(t):
                v.wait_ge(scattered[t.b], t.d16)
                v.tensor_copy(next_scatter[:, t.b:t.b + 1], e.here[:, t.b, SCAT:SCAT + 1]
                              ).then_inc(scatter_ready[t.m], 1)

            def keep_degrees(t):
                v.wait_ge(e.summed_ready[t.m], t.now)
                v.tensor_scalar(g.deg[:, bass.ds(t.at(1), 1), :].rearrange("p a c -> p (a c)"),
                                e.summed[:, t.b, D:D + 4], 1.0, None, ALU.mult).then_inc(deg_ready[t.m], 1)

            def half_row(t):
                v.wait_ge(own_ready[t.m], t.now)
                v.wait_ge(loaded[1][t.duo], t.d17)
                v.scalar_tensor_tensor(out=own[:, t.m, :], in0=state[1][:, t.b, :], scalar=0.5,
                                       in1=own[:, t.m, :], op0=ALU.mult, op1=ALU.add).then_inc(half_ready[t.m], 1)

            def mix(t):
                v.wait_ge((half_ready if halves else own_ready)[t.m], t.now)
                v.wait_ge(e.summed_ready[t.m], t.now)
                if products:
                    v.wait_ge(turned[t.m], t.back(MS).now)
                    to, ready = mixed[:, t.m, :], mixed_ready
                else:
                    v.wait_ge(stored[t.duo], t.d16)
                    to, ready = res[:, t.b, :], res_ready
                v.scalar_tensor_tensor(out=to, in0=e.summed[:, t.b, 0:D],
                                       scalar=e.here[:, t.b, sum_coef:sum_coef + 1], in1=own[:, t.m, :],
                                       op0=ALU.mult, op1=ALU.add).then_inc(ready[t.m], 1)

            def low_turned(t):
                v.wait_ge(turned_high_ready[t.m], t.now)
                high = turned_high[:, t.b % 2].bitcast(F32)
                if relu_first:
                    ins = v.scalar_tensor_tensor(out=turned_low[:, t.b % 2], in0=turned_ps[t.b % 2][:, :, :],
                                                 scalar=0.0, in1=high, op0=ALU.max, op1=ALU.subtract)
                else:
                    ins = v.tensor_tensor(turned_low[:, t.b % 2], turned_ps[t.b % 2][:, :, :], high, ALU.subtract)
                ins.then_inc(turned_low_ready[t.m], 1)

            def add_row(t):
                v.wait_ge(layer_ready[t.m], t.now)
                v.wait_ge(loaded[-1][t.duo], t.d17)
                if scatter_to is None:
                    v.wait_ge(stored[t.duo], t.d16)
                else:
                    v.wait_ge(scattered[t.b], t.d16)
                v.scalar_tensor_tensor(out=res[:, t.b, :], in0=layer_ps[t.b % 2][:, 0:D], scalar=0.0,
                                       in1=state[-1][:, t.b, :], op0=ALU.add if relu_first else ALU.max, op1=ALU.add
                                       ).then_inc(layer_read[t.m], 1)
                v.wait_ge(layer_read[t.m], t.now)
                v.wait_ge(rstd_ready[t.m], t.back(MS).now)
                v.bn_stats(stats[:, t.m, :], res[:, t.b, :]).then_inc(stats_ready[t.m], 1)
                v.wait_ge(stats_ready[t.m], t.now)
                v.wait_ge(res_ready[t.m], t.back(MS).now)
                v.sem_inc(stats_seen, 1)
                v.bn_aggr(moments[:, t.m, :], stats[:, t.m, :]).then_inc(var_ready[t.m], 1)

            def finish(t):
                v.wait_ge(std_ready[t.m], t.now)
                v.reciprocal(dev[:, t.m, 1:2], dev[:, t.m, 0:1]).then_inc(rstd_ready[t.m], 1)
                v.wait_ge(rstd_ready[t.m], t.now)
                v.tensor_scalar(res[:, t.b, :], res[:, t.b, :], moments[:, t.m, 0:1], dev[:, t.m, 1:2],
                                ALU.subtract, ALU.mult).then_inc(res_ready[t.m], 1)

            stages = [(8, finish)] if norm else []
            stages += [(5, scatter_index)] if scatter_to is not None else []
            stages += [(5, half_row)] if halves else []
            stages += [(5, keep_degrees if degrees else mix)]
            stages += [(2, fields)]
            stages += [(6, low_turned)] if products else []
            stages += [(3, lambda t: e.vec_low(v, t))]
            stages += [(7, add_row)] if norm else []
            tile_loop(v, ES, stages)

        @block.tensor
        def _(pe):
            def turn(t):
                pe.wait_ge(mixed_ready[t.m], t.now)
                pe.wait_ge(turned_low_ready[t.back(2).m], t.back(2).now)
                rows = [mixed[:, t.m, :]]
                if len(weights) > 1:
                    rows.append(state[0][:, t.b, :])
                    pe.wait_ge(loaded[0][t.duo], t.d17)
                for n, row in enumerate(rows):
                    for k in range(KC):
                        ins = pe.transpose(turned_ps[t.b % 2][:, KC * n + k, :], row[:, k * P:(k + 1) * P],
                                           g.ident[:, :])
                ins.then_inc(turned[t.m], 1)

            def layer(t):
                pe.wait_ge(turned_low_ready[t.m], t.now)
                read = layer_read if norm else res_ready
                pe.wait_ge(read[t.back(2).m], t.back(2).now)
                out = layer_ps[t.b % 2][:, 0:D]
                for n in range(2):
                    pe.matmul(out, g.sel0[:, :], g.bias_rows[:, n, bias, :], start=n == 0, stop=False,
                              skip_group_check=True)
                for c in range(chunks):
                    w = weights[c // KC]
                    ins = mm3(pe, out, (turned_high[:, t.b % 2, c, :], turned_low[:, t.b % 2, c, :]),
                              (w[:, 0, c % KC, :], w[:, 1, c % KC, :]), False, c == chunks - 1)
                ins.then_inc(layer_ready[t.m], 1)

            stages = [(7, layer)] if products else []
            stages += [(4, lambda t: e.pe_sum(pe, t))]
            stages += [(5, turn)] if products else []
            tile_loop(pe, ES, stages)


def gat_scores(nc, g):
    ET = g.ET
    ES = ET // T4
    with ExitStack() as ctx:
        m = Memory(nc, ctx, "score")
        src_rows = m.sb("src_rows", [P, T4, D])
        dst_rows = m.sb("dst_rows", [P, T4, D])
        next_src = m.sb("next_src", [P, T4], I32)
        next_dst = m.sb("next_dst", [P, T4], I32)
        high = m.sb("high", [P, T4, 2 * KC, P], F32R)
        low = m.sb("low", [P, T4, 2 * KC, P], F32R)
        h_rows = m.sb("h_rows", [P, T4, D])
        raw = m.sb("raw", [H, T4, P])
        fence = m.sb("fence", [H, T4, P])
        lines = m.sb("lines", [H, 2, T4, P])
        turned_ps = [m.ps(f"turned{k}", [P, 2 * KC, P]) for k in range(2)]
        h_ps = [m.ps(f"h{k}", [P, 512]) for k in range(2)]
        s_ps = [m.ps(f"s{k}", [P, 512]) for k in range(2)]
        index_ready = m.sems("index_ready", T4)
        index_seen = m.sem("index_seen")
        src_gathered = m.sems("src_gathered", T4)
        dst_gathered = m.sems("dst_gathered", T4)
        x1_stored = m.sems("x1_stored", 2)
        turned = m.sems("turned", T4)
        high_ready = m.sems("high_ready", T4)
        low_ready = m.sems("low_ready", T4)
        h_done = m.sems("h_done", T4)
        s_done = m.sems("s_done", T4)
        h_ready = m.sems("h_ready", T4)
        h_stored = m.sems("h_stored", 2)
        raw_ready = m.sems("raw_ready", T4)
        fence_ready = m.sems("fence_ready", T4)
        fence_cut = m.sems("fence_cut", T4)
        score_ready = m.sems("score_ready", T4)
        line_ready = m.sems("line_ready", T4)
        lines_stored = m.sem("lines_stored")
        first_line = m.sem("first_line")
        sp_seen = m.sem("sp_seen")

        def slot(b):
            return T4 - 1 - b

        def tile(s, b):
            return (ET - 1 - b) - s * T4

        def turn(s, b):
            return slot((b - 2) % T4), (lambda s1: s if b < 2 else s1)

        block = ctx.enter_context(nc.Block())

        @block.sync
        def _(sp):
            def store_x1(s, duo):
                s16 = snap(sp, s * 16 + 16)
                sp.wait_ge(dst_gathered[2 * duo], s16)
                sp.wait_ge(dst_gathered[2 * duo + 1], s16)
                sp.sem_inc(sp_seen, 1)
                sp.dma_start(slot_rows(g.x1_slots, 0, (ES - 1) - s, duo), dst_rows[:, 2 * duo:2 * duo + 2, :]
                             ).then_inc(x1_stored[duo], 16)

            def store_rest(s):
                s1 = snap(sp, s + 1)
                for duo in (1, 0):
                    sp.wait_ge(h_ready[2 * duo], s1)
                    sp.wait_ge(h_ready[2 * duo + 1], s1)
                    sp.sem_inc(sp_seen, 1)
                    sp.dma_start(slot_rows(g.h_slots, 0, (ES - 1) - s, duo), h_rows[:, 2 * duo:2 * duo + 2, :]
                                 ).then_inc(h_stored[duo], 16)
                for b in range(T4):
                    sp.wait_ge(line_ready[b], s1)
                sp.sem_inc(sp_seen, 1)
                sp.dma_start(g.score_lines[:, :, bass.ds((ES - 1) * T4 * P - s * (T4 * P), T4 * P)],
                             lines[:, :, :, :].rearrange("h a t p -> h a (t p)")).then_inc(lines_stored, 16)

            for duo in (1, 0):
                store_x1(0, duo)
            with sp.Fori(0, ES - 1) as s:
                s1 = snap(sp, s + 1)
                for duo in (1, 0):
                    store_x1(s1, duo)
                store_rest(s)
            store_rest(ES - 1)
            for duo in range(2):
                sp.wait_ge(x1_stored[duo], 16 * ES)
                sp.wait_ge(h_stored[duo], 16 * ES)
            sp.wait_ge(lines_stored, 16 * ES)

        @block.gpsimd
        def _(pool):
            def lead(s, before, b):
                c = slot(b)
                pool.wait_ge(index_ready[c], snap(pool, s + 1))
                pool.wait_ge(x1_stored[c // 2], snap(pool, s * 16))
                pool.sem_inc(index_seen, 1)
                pool.indirect_dma_start(src_rows[:, c, :], None, g.x1_table,
                                        bass.IndirectOffsetOnAxis(next_src[:, c:c + 1], 0)
                                        ).then_inc(src_gathered[c], 16)
                pool.indirect_dma_start(dst_rows[:, c, :], None, g.x1_table,
                                        bass.IndirectOffsetOnAxis(next_dst[:, c:c + 1], 0)
                                        ).then_inc(dst_gathered[c], 16)

            edge_loop(pool, ES, lead)

        @block.tensor
        def _(pe):
            def lead(s, before, b):
                c = slot(b)
                s1 = snap(pe, s + 1)
                s16 = snap(pe, s * 16 + 16)
                prev, count = turn(s, b)
                pe.wait_ge(src_gathered[c], s16)
                pe.wait_ge(dst_gathered[c], s16)
                pe.wait_ge(low_ready[prev], count(s1))
                for n, rows in enumerate((src_rows, dst_rows)):
                    for k in range(KC):
                        ins = pe.transpose(turned_ps[b % 2][:, KC * n + k, :], rows[:, c, k * P:(k + 1) * P],
                                           g.ident[:, :])
                ins.then_inc(turned[c], 1)

            def tail1(s, b):
                c = slot(b)
                s1 = snap(pe, s + 1)
                prev, count = turn(s, b)
                pe.wait_ge(low_ready[c], s1)
                pe.wait_ge(h_ready[prev], count(s1))
                pe.wait_ge(raw_ready[prev], count(s1))
                for k in range(KC):
                    ins = mm3(pe, h_ps[b % 2][:, 0:D], (high[:, c, k, :], low[:, c, k, :]),
                              (g.wgat[:, 0, k, :], g.wgat[:, 1, k, :]), k == 0, k == KC - 1)
                ins.then_inc(h_done[c], 1)
                for n in range(2):
                    for k in range(KC):
                        w = [g.wat[:, part, k, n * P:(n + 1) * P] for part in range(2)]
                        ins = mm3(pe, s_ps[b % 2][:, 0:P], w, (high[:, c, KC * n + k, :], low[:, c, KC * n + k, :]),
                                  n == k == 0, n == 1 and k == KC - 1)
                ins.then_inc(s_done[c], 1)

            edge_loop(pe, ES, lead, tail1)

        @block.scalar
        def _(act):
            def lead(s, before, b):
                c = slot(b)
                act.wait_ge(turned[c], snap(act, s + 1))
                act.wait_ge(s_done[c], s)
                act.activation(high[:, c], turned_ps[b % 2][:, :, :], ACT.Copy).then_inc(high_ready[c], 1)

            def tail1(s, b):
                c = slot(b)
                s1 = snap(act, s + 1)
                act.wait_ge(h_done[c], s1)
                act.wait_ge(h_stored[c // 2], snap(act, s * 16))
                act.activation(h_rows[:, c, :], h_ps[b % 2][:, 0:D], ACT.Copy).then_inc(h_ready[c], 1)
                act.wait_ge(s_done[c], s1)
                act.wait_ge(score_ready[c], s)
                act.activation(raw[:, c, :], s_ps[b % 2][0:H, 0:P], ACT.Copy).then_inc(raw_ready[c], 1)

            edge_loop(act, ES, lead, tail1)

        @block.vector
        def _(v):
            v.memset(lines[:, :, :, :], 0.0).then_inc(first_line, 1)
            for b in range(T4):
                for to, field in ((next_src, SRC), (next_dst, DSTG)):
                    ins = v.tensor_copy(to[:, slot(b):slot(b) + 1], g.edge_fields[:, tile(0, b), field:field + 1])
                ins.then_inc(index_ready[slot(b)], 1)
            v.wait_ge(first_line, 1)

            def lead(s, before, b):
                c = slot(b)
                s1 = snap(v, s + 1)
                v.wait_ge(high_ready[c], s1)
                v.tensor_tensor(low[:, c], turned_ps[b % 2][:, :, :], high[:, c].bitcast(F32), ALU.subtract
                                ).then_inc(low_ready[c], 1)
                if isinstance(s, int) and s == ES - 1:
                    return
                for to, field in ((next_src, SRC), (next_dst, DSTG)):
                    at = (ET - T4 - 1 - b) - s * T4
                    ins = v.tensor_scalar(to[:, c:c + 1], g.edge_fields[:, bass.ds(at, 1), field], 1.0, None, ALU.mult)
                ins.then_inc(index_ready[c], 1)

            def tail1(s, b):
                c = slot(b)
                s1 = snap(v, s + 1)
                at = tile(s, b) * P + 1 if isinstance(s, int) else ((ET - 1 - b) * P + 1) - s * (T4 * P)
                v.tensor_tensor(fence[:, c, :], g.keys[0:H, bass.ds(at, P)], g.keys[0:H, bass.ds(at + 1, P)],
                                ALU.is_equal).then_inc(fence_ready[c], 1)
                v.wait_ge(fence_ready[c], s1)
                v.tensor_scalar(fence[:, c, :], fence[:, c, :], 1.0, BIG, ALU.subtract, ALU.mult
                                ).then_inc(fence_cut[c], 1)
                v.wait_ge(raw_ready[c], s1)
                v.wait_ge(lines_stored, snap(v, s * 16))
                v.scalar_tensor_tensor(out=lines[:, 0, c, :], in0=raw[:, c, :], scalar=NEG_SLOPE, in1=raw[:, c, :],
                                       op0=ALU.mult, op1=ALU.max).then_inc(score_ready[c], 1)
                v.wait_ge(fence_cut[c], s1)
                v.wait_ge(score_ready[c], s1)
                prev = slot((b - 1) % T4)
                v.wait_ge(line_ready[prev], s1 if b else s)
                v.tensor_tensor_scan(lines[:, 1, c, ::-1], fence[:, c, ::-1], lines[:, 0, c, ::-1],
                                     lines[:, 1, prev, 0:1], ALU.add, ALU.max).then_inc(line_ready[c], 1)

            edge_loop(v, ES, lead, tail1)


def gat_sum(nc, g):
    ES = g.ES
    W = D + H
    with ExitStack() as ctx:
        m = Memory(nc, ctx, "gat")
        e = EdgeSum(m, g, None, None, None, width=W)
        lines = m.sb("lines", [H, 2, T8 * P])
        fence = m.sb("fence", [H, T8 * P])
        top = m.sb("top", [H, T8 * P])
        diff = m.sb("diff", [H, T8 * P])
        prob = m.sb("prob", [H, T8 * P])
        prob_ps = m.ps("prob", [P, 512])
        probs = m.sb("probs", [P, T8, H])
        h_rows = m.sb("h_rows", [P, T8, D])
        x1 = m.sb("x1", [P, T8, D])
        den = m.sb("den", [P, MS, 2, H])
        mean = m.sb("mean", [P, MS, D])
        res = m.sb("res", [P, T8, D])
        stats = m.sb("stats", [P, MS, 6])
        moments = m.sb("moments", [P, MS, 2])
        dev = m.sb("dev", [P, MS, 2])
        lines_loaded = m.sem("lines_loaded")
        fence_ready = m.sem("fence_ready")
        fence_cut = m.sem("fence_cut")
        top_ready = m.sem("top_ready")
        diff_ready = m.sem("diff_ready")
        exp_ready = m.sem("exp_ready")
        prob_turned = m.sem("prob_turned")
        probs_ready = m.sem("probs_ready")
        h_loaded = m.sems("h_loaded", T8 // 2)
        x1_loaded = m.sems("x1_loaded", T8 // 2)
        den_ready = m.sems("den_ready", MS)
        rden_ready = m.sems("rden_ready", MS)
        mean_ready = m.sems("mean_ready", MS)
        sum_ready = m.sems("sum_ready", MS)
        stats_ready = m.sems("stats_ready", MS)
        stats_seen = m.sem("stats_seen")
        var_ready = m.sems("var_ready", MS)
        std_ready = m.sems("std_ready", MS)
        rstd_ready = m.sems("rstd_ready", MS)
        norm_seen = m.sem("norm_seen")
        res_ready = m.sems("res_ready", MS)
        stored = m.sems("stored", T8 // 2)
        sp_seen = m.sem("sp_seen")
        pe_seen = m.sem("pe_seen")
        block = ctx.enter_context(nc.Block())

        @block.sync
        def _(sp):
            def load_lines(t):
                if t.b != 0:
                    return
                sp.wait_ge(diff_ready, t.s)
                sp.sem_inc(sp_seen, 1)
                sp.dma_start(lines[:, :, :], g.score_lines[:, :, bass.ds(t.at(P), T8 * P)]).then_inc(lines_loaded, 16)

            def load_h(t):
                if t.b % 2:
                    return
                for last in (t.back(T8), t.back(T8 - 1)):
                    sp.wait_ge(e.gathered[last.m], last.now)
                sp.sem_inc(sp_seen, 1)
                sp.dma_start(h_rows[:, t.b:t.b + 2, :], slot_rows(g.h_slots, 0, t.s, t.duo, T8)
                             ).then_inc(h_loaded[t.duo], 16)

            def load_x1(t):
                if t.b % 2:
                    return
                for last in (t.back(T8), t.back(T8 - 1)):
                    sp.wait_ge(sum_ready[last.m], last.now)
                sp.sem_inc(sp_seen, 1)
                sp.dma_start(x1[:, t.b:t.b + 2, :], slot_rows(g.x1_slots, 0, t.s, t.duo, T8)
                             ).then_inc(x1_loaded[t.duo], 16)

            def store(t):
                if t.b % 2 == 0:
                    return
                for done in (t.back(1), t):
                    sp.wait_ge(res_ready[done.m], done.now)
                sp.sem_inc(sp_seen, 1)
                sp.dma_start(slot_rows(g.x2_table, g.N, t.s, t.duo, T8), res[:, t.b - 1:t.b + 1, :]
                             ).then_inc(stored[t.duo], 16)

            tile_loop(sp, ES, [(0, load_lines), (2, load_h), (4, load_x1), (16, store)], dma=False)
            for duo in range(T8 // 2):
                sp.wait_ge(stored[duo], 16 * ES)

        @block.tensor
        def _(pe):
            def turn_probs(t):
                if t.b != T8 - 1:
                    return
                pe.wait_ge(exp_ready, t.s1)
                pe.wait_ge(probs_ready, t.s)
                pe.sem_inc(pe_seen, 1)
                for b in range(T8):
                    ins = pe.transpose(prob_ps[:, b * H:(b + 1) * H], prob[:, b * P:(b + 1) * P], g.ident[0:H, 0:H])
                ins.then_inc(prob_turned, 1)

            tile_loop(pe, ES, [(11, lambda t: e.pe_sum(pe, t)), (0, turn_probs)], dma=False)

        @block.scalar
        def _(act):
            def exps(t):
                if t.b != T8 - 2:
                    return
                act.wait_ge(diff_ready, t.s1)
                act.wait_ge(prob_turned, t.s)
                act.activation(prob[:, :], diff[:, :], ACT.Exp).then_inc(exp_ready, 1)

            def keep_probs(t):
                if t.b != 0:
                    return
                act.wait_ge(prob_turned, t.s1)
                act.wait_ge(e.gathered[t.back(1).m], t.back(1).now)
                act.activation(probs[:, :, :], prob_ps[:, 0:T8 * H].rearrange("p (b h) -> p b h", h=H), ACT.Copy
                               ).then_inc(probs_ready, 1)

            def evacuate(t):
                act.wait_ge(mean_ready[t.m], t.back(T8).now)
                e.act_evacuate(act, t)

            def root(t):
                act.wait_ge(var_ready[t.m], t.now)
                act.activation(dev[:, t.m, 0:1], moments[:, t.m, 1:2], ACT.Sqrt, bias=g.ln_eps[:, :]
                               ).then_inc(std_ready[t.m], 1)

            tile_loop(act, ES, [(13, root), (8, keep_probs), (10, lambda t: e.act_high(act, t)), (11, evacuate),
                                (0, exps)], dma=False)

        @block.vector
        def _(v):
            e.first(v)
            v.memset(top[:, :], 0.0).then_inc(fence_cut, 1)

            def scores(t):
                if t.b == 0:
                    v.wait_ge(top_ready, t.s)
                    v.tensor_tensor(fence[:, :], g.keys[0:H, bass.ds(t.at(P) + 1, T8 * P)],
                                    g.keys[0:H, bass.ds(t.at(P), T8 * P)], ALU.is_equal).then_inc(fence_ready, 1)
                elif t.b == 1:
                    v.wait_ge(fence_ready, t.s1)
                    v.tensor_scalar(fence[:, :], fence[:, :], 1.0, BIG, ALU.subtract, ALU.mult
                                    ).then_inc(fence_cut, 1)
                elif t.b == 3:
                    v.wait_ge(lines_loaded, t.d17)
                    v.wait_ge(fence_cut, t.s2)
                    v.wait_ge(top_ready, t.s)
                    v.tensor_tensor_scan(top[:, :], fence[:, :], lines[:, 1, :], top[:, T8 * P - 1:T8 * P],
                                         ALU.add, ALU.max).then_inc(top_ready, 1)
                elif t.b == 5:
                    v.wait_ge(top_ready, t.s1)
                    v.wait_ge(exp_ready, t.s)
                    v.tensor_tensor(diff[:, :], lines[:, 0, :], top[:, :], ALU.subtract).then_inc(diff_ready, 1)

            def weigh(t):
                if t.b == 0:
                    v.wait_ge(probs_ready, t.s1)
                v.wait_ge(h_loaded[t.duo], t.d17)
                v.wait_ge(e.low_ready[t.m], t.back(T8).now)
                p = probs[:, t.b, :]
                v.tensor_tensor(e.rows[:, t.b, 0:D].rearrange("p (h f) -> p h f", h=H),
                                h_rows[:, t.b, :].rearrange("p (h f) -> p h f", h=H),
                                p.unsqueeze(2).broadcast_to([P, H, DH]), ALU.mult)
                v.tensor_copy(e.rows[:, t.b, D:W], p).then_inc(e.gathered[t.m], 1)

            def divide(t):
                v.wait_ge(e.summed_ready[t.m], t.now)
                v.tensor_scalar(den[:, t.m, 0, :], e.summed[:, t.b, D:W], GAT_EPS, None, ALU.add
                                ).then_inc(den_ready[t.m], 1)
                v.wait_ge(den_ready[t.m], t.now)
                v.reciprocal(den[:, t.m, 1, :], den[:, t.m, 0, :]).then_inc(rden_ready[t.m], 1)
                v.wait_ge(rden_ready[t.m], t.now)
                v.wait_ge(res_ready[t.m], t.back(MS).now)
                v.tensor_tensor(mean[:, t.m, :].rearrange("p (h f) -> p h f", h=H),
                                e.summed[:, t.b, 0:D].rearrange("p (h f) -> p h f", h=H),
                                den[:, t.m, 1, :].unsqueeze(2).broadcast_to([P, H, DH]), ALU.mult
                                ).then_inc(mean_ready[t.m], 1)
                v.wait_ge(mean_ready[t.m], t.now)
                v.wait_ge(x1_loaded[t.duo], t.d17)
                v.tensor_tensor(mean[:, t.m, :], mean[:, t.m, :], x1[:, t.b, :], ALU.add).then_inc(sum_ready[t.m], 1)
                v.wait_ge(sum_ready[t.m], t.now)
                v.bn_stats(stats[:, t.m, :], mean[:, t.m, :]).then_inc(stats_ready[t.m], 1)
                v.wait_ge(stats_ready[t.m], t.now)
                v.sem_inc(stats_seen, 1)
                v.bn_aggr(moments[:, t.m, :], stats[:, t.m, :]).then_inc(var_ready[t.m], 1)

            def invert(t):
                v.wait_ge(std_ready[t.m], t.now)
                v.reciprocal(dev[:, t.m, 1:2], dev[:, t.m, 0:1]).then_inc(rstd_ready[t.m], 1)

            tile_loop(v, ES, [(13, invert), (9, weigh), (12, divide), (9, lambda t: e.vec_fields(v, t)),
                              (10, lambda t: e.vec_low(v, t)), (0, scores)])

        @block.gpsimd
        def _(pool):
            def norm(t):
                pool.wait_ge(rstd_ready[t.m], t.now)
                pool.wait_ge(stored[t.duo], t.d16)
                pool.sem_inc(norm_seen, 1)
                pool.tensor_scalar(res[:, t.b, :], mean[:, t.m, :], moments[:, t.m, 0:1], dev[:, t.m, 1:2],
                                   ALU.subtract, ALU.mult).then_inc(res_ready[t.m], 1)

            tile_loop(pool, ES, [(13, norm)])




class Step:

    def __init__(self, eng, g, i, h, par, loop):
        self.i, self.par = i, par
        last = not loop and i == g.NBLK - 1
        self.parts, self.rows = g.tail if last else (P, R4)
        self.cols = self.parts * self.rows
        self.n, self.n1 = i, snap(eng, i + 1)
        self.h, self.h1 = h, snap(eng, h + 1)
        self.h16, self.h17 = snap(eng, h * 16), snap(eng, h * 16 + 16)

    def nodes(self, table):
        rows = table[bass.ds(self.i * BLOCK, self.cols), :]
        return rows.rearrange("(p r) f -> p r f", p=self.parts)


def block_loop(eng, g, stages):
    lags = [lag for lag, _ in stages]
    most, least = max(lags), min(lags)

    def step(q, c):
        loop = not isinstance(q, int)
        for lag, stage in stages:
            k = c - lag
            i, h = q * 2 + k, q + k // 2
            if loop or 0 <= i < g.NBLK:
                stage(Step(eng, g, i if not loop else eng.snap(i), h if not loop else eng.snap(h), k % 2, loop))

    q0 = (most + 3) // 2
    q1 = (g.NBLK - 2 + least + 1) // 2
    for q in range(q0):
        step(q, 0)
        step(q, 1)
    with eng.Fori(q0, q1) as q:
        step(q, 0)
        step(q, 1)
    q = q1
    while 2 * q <= g.NBLK - 1 + most:
        step(q, 0)
        step(q, 1)
        q += 1


def later(v, k):
    if isinstance(v, int):
        return v + k if v + k > 0 else None
    return v + k


def gin_hidden(nc, g):
    NCH = 2 * D // P
    with ExitStack() as ctx:
        m = Memory(nc, ctx, "gin")
        x = m.sb("x", [P, 2, R4, D])
        agg = m.sb("agg", [P, 2, R4, D])
        xin = m.sb("xin", [P, 2, R4, D])
        x_high = m.sb("x_high", [P, KC, BLOCK], F32R)
        x_low = m.sb("x_low", [P, KC, BLOCK], F32R)
        hid = m.sb("hid", [P, 2, BLOCK])
        hid_high = m.sb("hid_high", [P, NCH, BLOCK], F32R)
        hid_low = m.sb("hid_low", [P, NCH, BLOCK], F32R)
        y = m.sb("y", [P, 2, KC, BLOCK])
        map_index = m.sb("map_index", [P, T4], I32)
        map_rows = m.sb("map_rows", [P, T4, 4])
        x_ps = m.ps("x", [P, KC, BLOCK])
        hid_ps = m.ps("hid", [P, NCH, BLOCK])
        y_ps = m.ps("y", [P, KC, BLOCK])
        x_loaded = m.sems("x_loaded", 2)
        agg_loaded = m.sems("agg_loaded", 2)
        xin_ready = m.sems("xin_ready", 2)
        turned = m.sem("turned")
        x_high_ready = m.sem("x_high_ready")
        x_low_ready = m.sem("x_low_ready")
        hid_done = m.sems("hid_done", NCH)
        hid_ready = m.sems("hid_ready", NCH)
        hid_high_ready = m.sems("hid_high_ready", NCH)
        hid_low_ready = m.sems("hid_low_ready", NCH)
        y_done = m.sem("y_done")
        y_ready = m.sem("y_ready")
        y_stored = m.sems("y_stored", 2)
        stats_seen = m.sem("stats_seen")
        stats_done = m.sem("stats_done")
        map_staged = m.sem("map_staged")
        map_seen = m.sem("map_seen")
        map_written = m.sems("map_written", T4)
        map_read = m.sems("map_read", T4)
        map_kept = m.sem("map_kept")
        sp_seen = m.sem("sp_seen")
        block = ctx.enter_context(nc.Block())

        @block.sync
        def _(sp):
            def load(t):
                sp.wait_ge(xin_ready[t.par], t.h)
                sp.sem_inc(sp_seen, 1)
                sp.dma_start(x[0:t.parts, t.par, 0:t.rows, :], t.nodes(g.x)).then_inc(x_loaded[t.par], 16)
                sp.dma_start(agg[0:t.parts, t.par, 0:t.rows, :], t.nodes(g.agg_table)).then_inc(agg_loaded[t.par], 16)

            def store(t):
                sp.wait_ge(y_ready, t.n1)
                sp.sem_inc(sp_seen, 1)
                sp.dma_start(g.y_table[bass.ds(t.i * P, P), :].rearrange("p (k c) -> p k c", k=KC)[:, :, 0:t.cols],
                             y[:, t.par, :, 0:t.cols]).then_inc(y_stored[t.par], 16)

            block_loop(sp, g, [(0, load), (2, store)])
            for par in range(2):
                sp.wait_ge(y_stored[par], 16 * ((g.NBLK + 1 - par) // 2))

        @block.gpsimd
        def _(pool):
            limit = pool.alloc_register("map_limit")
            pool.reg_mov(limit, g.N - 1)
            with pool.Fori(0, g.ET // T4) as s:
                s1, s17 = pool.snap(s + 1), pool.snap(s * 16 + 16)
                pool.tensor_copy(map_index[:, :], g.edge_fields[:, bass.ds(s * T4, T4), SCAT])
                pool.tensor_copy(map_rows[:, :, :], g.slot_info[:, bass.ds(s * T4, T4), :]).then_inc(map_staged, 1)
                pool.wait_ge(map_staged, s1)
                pool.sem_inc(map_seen, 1)
                for b in range(T4):
                    pool.indirect_dma_start(g.node_table, bass.IndirectOffsetOnAxis(map_index[:, b:b + 1], 0),
                                            map_rows[:, b, :], None, bounds_check=limit, oob_is_err=False
                                            ).then_inc(map_written[b], 16)
                for b in range(T4):
                    pool.wait_ge(map_written[b], s17)
                pool.sem_inc(map_seen, 1)
            with pool.Fori(0, g.ET // T4) as s:
                s17 = pool.snap(s * 16 + 16)
                s1n = pool.snap(s + (g.ET // T4 + 1))
                pool.tensor_copy(map_index[:, :], g.edge_fields[:, bass.ds(s * T4, T4), SRC]).then_inc(map_staged, 1)
                pool.wait_ge(map_staged, s1n)
                pool.sem_inc(map_seen, 1)
                for b in range(T4):
                    pool.indirect_dma_start(map_rows[:, b, :], None, g.node_table,
                                            bass.IndirectOffsetOnAxis(map_index[:, b:b + 1], 0)
                                            ).then_inc(map_read[b], 16)
                for b in range(T4):
                    pool.wait_ge(map_read[b], s17)
                pool.sem_inc(map_seen, 1)
                pool.tensor_copy(g.src_info[:, bass.ds(s * T4, T4), :], map_rows[:, :, :]).then_inc(map_kept, 1)

        @block.vector
        def _(v):
            def prepare(t):
                v.wait_ge(x_loaded[t.par], t.h17)
                v.wait_ge(agg_loaded[t.par], t.h17)
                if (n := later(t.n, -1)) is not None:
                    v.wait_ge(turned, snap(v, n))
                v.scalar_tensor_tensor(out=xin[0:t.parts, t.par, 0:t.rows, :], in0=x[0:t.parts, t.par, 0:t.rows, :],
                                       scalar=g.eps1[0:t.parts, :], in1=agg[0:t.parts, t.par, 0:t.rows, :],
                                       op0=ALU.mult, op1=ALU.add).then_inc(xin_ready[t.par], 1)

            def hidden(t):
                for c in range(NCH):
                    v.wait_ge(hid_done[c], t.n1)
                    v.wait_ge(hid_low_ready[(c - 2) % NCH], t.n if c < 2 else t.n1)
                    v.tensor_scalar(hid[:, c % 2, 0:t.cols], hid_ps[:, c, 0:t.cols], g.b1_col[:, c:c + 1], 0.0,
                                    ALU.add, ALU.max).then_inc(hid_ready[c], 1)
                    v.wait_ge(hid_ready[c], t.n1)
                    v.wait_ge(hid_high_ready[c], t.n1)
                    v.tensor_tensor(hid_low[:, c, 0:t.cols], hid[:, c % 2, 0:t.cols],
                                    hid_high[:, c, 0:t.cols].bitcast(F32), ALU.subtract).then_inc(hid_low_ready[c], 1)

            def turned_low(t):
                v.wait_ge(x_high_ready, t.n1)
                v.tensor_tensor(x_low[:, :, 0:t.cols], x_ps[:, :, 0:t.cols], x_high[:, :, 0:t.cols].bitcast(F32),
                                ALU.subtract).then_inc(x_low_ready, 1)

            def moments(t):
                v.wait_ge(y_ready, t.n1)
                v.sem_inc(stats_seen, 1)
                for f in range(KC):
                    ins = v.bn_stats(g.bn_stats[:, f, bass.ds(t.i, 1), :].rearrange("p a c -> p (a c)"),
                                     y[:, t.par, f, 0:t.cols])
                ins.then_inc(stats_done, 1)

            block_loop(v, g, [(0, prepare), (1, hidden), (0, turned_low), (1, moments)])

        @block.scalar
        def _(act):
            def hidden(t):
                for c in range(NCH):
                    act.wait_ge(hid_ready[c], t.n1)
                    if c == 0:
                        act.wait_ge(y_done, t.n)
                    act.activation(hid_high[:, c, 0:t.cols], hid[:, c % 2, 0:t.cols], ACT.Copy
                                   ).then_inc(hid_high_ready[c], 1)

            def turned_high(t):
                act.wait_ge(turned, t.n1)
                act.wait_ge(hid_done[NCH - 1], t.n)
                act.activation(x_high[:, :, 0:t.cols], x_ps[:, :, 0:t.cols], ACT.Copy).then_inc(x_high_ready, 1)

            def evacuate(t):
                act.wait_ge(y_done, t.n1)
                act.wait_ge(y_stored[t.par], t.h16)
                if (n := later(t.n, -1)) is not None:
                    act.wait_ge(stats_done, snap(act, n))
                for f in range(KC):
                    ins = act.activation(y[:, t.par, f, 0:t.cols], y_ps[:, f, 0:t.cols], ACT.Identity,
                                         bias=g.b2_col[:, f:f + 1])
                ins.then_inc(y_ready, 1)

            block_loop(act, g, [(1, hidden), (0, turned_high), (1, evacuate)])

        @block.tensor
        def _(pe):
            def first(t):
                pe.wait_ge(x_low_ready, t.n1)
                for c in range(NCH):
                    pe.wait_ge(hid_low_ready[c], t.n)
                    for k in range(KC):
                        ins = mm3(pe, hid_ps[:, c, 0:t.cols],
                                  [g.w1[:, part, k, c * P:(c + 1) * P] for part in range(2)],
                                  (x_high[:, k, 0:t.cols], x_low[:, k, 0:t.cols]), k == 0, k == KC - 1)
                    ins.then_inc(hid_done[c], 1)

            def turn(t):
                pe.wait_ge(xin_ready[t.par], t.h1)
                pe.wait_ge(x_low_ready, t.n)
                for k in range(KC):
                    for r in range(t.rows):
                        ins = pe.transpose(x_ps[:, k, r * t.parts:(r + 1) * t.parts],
                                           xin[0:t.parts, t.par, r, k * P:(k + 1) * P], g.ident[0:t.parts, 0:t.parts])
                ins.then_inc(turned, 1)

            def second(t):
                for c in range(NCH):
                    pe.wait_ge(hid_low_ready[c], t.n1)
                    if c == 0:
                        pe.wait_ge(y_ready, t.n)
                    for f in range(KC):
                        ins = mm3(pe, y_ps[:, f, 0:t.cols],
                                  [g.w2[:, part, c, f * P:(f + 1) * P] for part in range(2)],
                                  (hid_high[:, c, 0:t.cols], hid_low[:, c, 0:t.cols]), c == 0, c == NCH - 1)
                ins.then_inc(y_done, 1)

            block_loop(pe, g, [(1, first), (0, turn), (1, second)])


def norm_and_fields(nc, g):
    ET = g.ET
    with ExitStack() as ctx:
        m = Memory(nc, ctx, "fin")
        mom = m.sb("mom", [P, KC, 2])
        tmp = m.sb("tmp", [P, KC, 2])
        bn_eps = m.sb("bn_eps", [P, 1])
        step = m.sem("step")
        var_ready = m.sem("var_ready")
        std_ready = m.sem("std_ready")
        block = ctx.enter_context(nc.Block())

        @block.scalar
        def _(act):
            act.wait_ge(var_ready, 1)
            act.activation(tmp[:, :, 0], mom[:, :, 1], ACT.Sqrt, bias=bn_eps[:, :]).then_inc(std_ready, 1)

        @block.vector
        def _(v):
            linked = 0

            def link(ins):
                nonlocal linked
                ins.then_inc(step, 1)
                linked += 1
                v.wait_ge(step, linked)

            link(v.memset(bn_eps[:, :], BN_EPS))
            for f in range(KC):
                ins = v.bn_aggr(mom[:, f, :], g.bn_stats[:, f, :, :].rearrange("p n c -> p (n c)"))
            ins.then_inc(var_ready, 1)
            fields = g.edge_fields

            def f(c):
                return fields[:, 0:ET, c]

            dinv, dis = g.slot_info[:, :, 1], g.slot_info[:, :, 2]
            link(v.tensor_copy(f(ROW), g.src_info[:, :, 0:1].bitcast(I32).rearrange("p t c -> p (t c)")))
            link(v.tensor_scalar(f(ROW_H), f(ROW), float(g.N), float(g.EP), ALU.is_ge, ALU.mult))
            link(v.tensor_tensor(f(ROW_H), f(ROW_H), f(ROW), ALU.add))
            link(v.tensor_tensor(f(C_APPNP), f(EW), g.src_info[:, :, 1], ALU.mult))
            link(v.tensor_copy(f(C_GCN), g.src_info[:, :, 2]))
            link(v.tensor_scalar(f(D_HALF), dinv, 0.5, None, ALU.mult))
            link(v.tensor_tensor(f(D_HALF2), f(D_HALF), dinv, ALU.mult))
            link(v.tensor_scalar(f(D_KEEP), f(D_HALF2), 0.5, None, ALU.add))
            link(v.tensor_copy(f(DIS), dis))
            link(v.tensor_tensor(f(DIS2), dis, dis, ALU.mult))
            v.wait_ge(std_ready, 1)
            link(v.reciprocal(tmp[:, :, 1], tmp[:, :, 0]))
            link(v.tensor_tensor(g.bn_scale[:, :], g.gamma_col[:, :], tmp[:, :, 1], ALU.mult))
            link(v.tensor_tensor(tmp[:, :, 0], mom[:, :, 0], g.bn_scale[:, :], ALU.mult))
            link(v.tensor_tensor(g.bn_shift[:, :], g.beta_col[:, :], tmp[:, :, 0], ALU.subtract))


def degrees(nc, g):
    ET = g.ET
    with ExitStack() as ctx:
        m = Memory(nc, ctx, "deg")
        deg = m.sb("deg", [P, 2, ET])
        held = m.sb("held", [P, 2, ET])
        pos = m.sb("pos", [P, 2, ET])
        zero = m.sb("zero", [P, 1])
        step = m.sem("step")
        held_ready = m.sem("held_ready")
        root_ready = m.sem("root_ready")
        block = ctx.enter_context(nc.Block())

        @block.scalar
        def _(act):
            act.wait_ge(held_ready, 1)
            act.activation(deg[:, :, :], held[:, :, :], ACT.Sqrt, bias=zero[:, :]).then_inc(root_ready, 1)

        @block.vector
        def _(v):
            linked = 0

            def link(ins):
                nonlocal linked
                ins.then_inc(step, 1)
                linked += 1
                v.wait_ge(step, linked)

            link(v.memset(zero[:, :], 0.0))
            link(v.scalar_tensor_tensor(out=deg[:, 0, :], in0=g.deg[:, :, 0], scalar=1.0, in1=g.deg[:, :, 1],
                                        op0=ALU.add, op1=ALU.add))
            link(v.tensor_scalar(deg[:, 1, :], g.deg[:, :, 2], 1.0, None, ALU.add))
            link(v.tensor_scalar(pos[:, :, :], deg[:, :, :], 0.0, None, ALU.is_gt))
            v.tensor_scalar(held[:, :, :], deg[:, :, :], 1e-12, None, ALU.max).then_inc(held_ready, 1)
            v.wait_ge(root_ready, 1)
            link(v.reciprocal(held[:, :, :], deg[:, :, :]))
            link(v.tensor_tensor(g.slot_info[:, :, 1], held[:, 0, :], pos[:, 0, :], ALU.mult))
            link(v.tensor_tensor(g.slot_info[:, :, 2], held[:, 1, :], pos[:, 1, :], ALU.mult))
            link(v.tensor_copy(g.slot_info[:, :, 0:1].bitcast(I32).rearrange("p t c -> p (t c)"), g.slot_row[:, :]))
            link(v.memset(g.slot_info[:, :, 3:4], 0.0))


def dense_layers(nc, g):
    with ExitStack() as ctx:
        m = Memory(nc, ctx, "dense")
        y = m.sb("y", [P, 2, KC, BLOCK])
        x = m.sb("x", [P, 2, R4, D])
        z = m.sb("z", [P, KC, BLOCK])
        raw = [m.sb(f"raw{n}", [P, R4, D]) for n in range(3)]
        rows1 = m.sb("rows1", [P, 2, R4, D])
        rows2 = m.sb("rows2", [P, 2, R4, D])
        rows3 = m.sb("rows3", [P, 2, R4, D])
        rows_y = m.sb("rows_y", [P, 2, R4, D])
        rows4 = m.sb("rows4", [P, 2, R4, D])
        high = [m.sb(f"high{n}", [P, KC, BLOCK], F32R) for n in range(3)]
        low = [m.sb(f"low{n}", [P, KC, BLOCK], F32R) for n in range(3)]
        gcn = m.sb("gcn", [P, KC, BLOCK])
        stats = m.sb("stats", [P, 4, R4, 6])
        mom = m.sb("mom", [P, 4, R4, 2])
        dev = m.sb("dev", [P, 4, 2, R4])
        turned_ps = m.ps("turned", [P, KC, BLOCK])
        layer_ps = m.ps("layer", [P, 2, 512])
        rows_ps = m.ps("rows", [P, R4, D])
        last_ps = m.ps("last", [P, R4, D])
        y_loaded = m.sems("y_loaded", 2)
        x_loaded = m.sems("x_loaded", 2)
        z_ready = m.sem("z_ready")
        z_turned = m.sem("z_turned")
        raw_ready = m.sems("raw_ready", 4)
        stats_ready = m.sems("stats_ready", 4)
        stats_seen = m.sem("stats_seen")
        var_ready = m.sems("var_ready", 4)
        std_ready = m.sems("std_ready", 4)
        rstd_ready = m.sems("rstd_ready", 4)
        norm_seen = m.sem("norm_seen")
        normed = m.sems("normed", 4)
        turned = m.sems("turned", 2)
        high_ready = m.sems("high_ready", 3)
        low_ready = m.sems("low_ready", 3)
        appnp_done = m.sem("appnp_done")
        gcn_done = m.sem("gcn_done")
        gcn_ready = m.sem("gcn_ready")
        gcn_turned = m.sem("gcn_turned")
        rows_y_ready = m.sem("rows_y_ready")
        last_done = m.sem("last_done")
        stored = [m.sems(f"stored{n}_", 2) for n in range(5)]
        sp_seen = m.sem("sp_seen")
        block = ctx.enter_context(nc.Block())

        @block.sync
        def _(sp):
            def load(t):
                n = later(t.n, -1)
                if n is not None:
                    n = snap(sp, n)
                    sp.wait_ge(z_ready, n)
                    sp.sem_inc(sp_seen, 1)
                sp.dma_start(y[:, t.par, :, 0:t.cols],
                             g.y_table[bass.ds(t.i * P, P), :].rearrange("p (k c) -> p k c", k=KC)[:, :, 0:t.cols]
                             ).then_inc(y_loaded[t.par], 16)
                if n is not None:
                    sp.wait_ge(raw_ready[0], n)
                    sp.sem_inc(sp_seen, 1)
                sp.dma_start(x[0:t.parts, t.par, 0:t.rows, :], t.nodes(g.x)).then_inc(x_loaded[t.par], 16)

            def store(n, rows, table, ready):
                def one(t):
                    sp.wait_ge(ready, t.n1)
                    sp.sem_inc(sp_seen, 1)
                    sp.dma_start(t.nodes(table), rows[0:t.parts, t.par, 0:t.rows, :]).then_inc(stored[n][t.par], 16)
                return one

            block_loop(sp, g, [(0, load), (1, store(0, rows1, g.x1_table, normed[0])),
                               (1, store(1, rows2, g.x2_table, normed[1])),
                               (2, store(2, rows3, g.x3_table, normed[2])),
                               (3, store(3, rows_y, g.y1_table, rows_y_ready)),
                               (4, store(4, rows4, g.out, normed[3]))])
            for n in range(5):
                for par in range(2):
                    sp.wait_ge(stored[n][par], 16 * ((g.NBLK + 1 - par) // 2))

        @block.tensor
        def _(pe):
            def turn_rows(t, rows, free):
                for k in range(KC):
                    for r in range(t.rows):
                        ins = pe.transpose(turned_ps[:, k, r * t.parts:(r + 1) * t.parts],
                                           rows[0:t.parts, t.par, r, k * P:(k + 1) * P], g.ident[0:t.parts, 0:t.parts])
                return ins

            def turn_features(t, cols):
                for r in range(t.rows):
                    for k in range(KC):
                        ins = pe.transpose(rows_ps[0:t.parts, r, k * P:(k + 1) * P],
                                           cols[:, k, r * t.parts:(r + 1) * t.parts], g.ident[:, :])
                return ins

            def to_rows(t, out, part, weights, bias):
                for r in range(t.rows):
                    span = slice(r * t.parts, (r + 1) * t.parts)
                    for n in range(2):
                        pe.matmul(out[0:t.parts, r, :], g.sel0[:, 0:t.parts], g.bias_rows[:, n, bias, :],
                                  start=n == 0, stop=False, skip_group_check=True)
                    for k in range(KC):
                        ins = mm3(pe, out[0:t.parts, r, :], (high[part][:, k, span], low[part][:, k, span]),
                                  (weights[:, 0, k, :], weights[:, 1, k, :]), False, k == KC - 1)
                return ins

            def stage4(t):
                pe.wait_ge(low_ready[2], t.n1)
                pe.wait_ge(raw_ready[3], t.n)
                to_rows(t, last_ps, 2, g.ws1, 2).then_inc(last_done, 1)

            def stage3(t):
                pe.wait_ge(normed[2], t.n1)
                pe.wait_ge(low_ready[0], t.n1)
                turn_rows(t, rows3, None).then_inc(turned[1], 1)
                pe.wait_ge(low_ready[1], t.n1)
                pe.wait_ge(raw_ready[2], t.n1)
                for n in range(KC):
                    for k in range(KC):
                        ins = mm3(pe, layer_ps[:, n, 0:t.cols],
                                  [g.ws0[:, part, k, n * P:(n + 1) * P] for part in range(2)],
                                  (high[1][:, k, 0:t.cols], low[1][:, k, 0:t.cols]), k == 0, k == KC - 1)
                ins.then_inc(gcn_done, 1)
                pe.wait_ge(gcn_ready, t.n1)
                n = min(t.n + 2, g.NBLK) if isinstance(t.n, int) else t.n + 2
                pe.wait_ge(raw_ready[0], snap(pe, n))
                turn_features(t, gcn).then_inc(gcn_turned, 1)

            def stage2(t):
                pe.wait_ge(normed[1], t.n1)
                pe.wait_ge(low_ready[1], t.n)
                turn_rows(t, rows2, None).then_inc(turned[0], 1)
                pe.wait_ge(low_ready[0], t.n1)
                pe.wait_ge(gcn_ready, t.n)
                layer = layer_ps[:, :, :].rearrange("p a (b n) -> p (a b) n", n=D)
                to_rows(t, layer, 0, g.wl2, 0).then_inc(appnp_done, 1)

            def stage1(t):
                pe.wait_ge(z_ready, t.n1)
                if (n := later(t.n, -1)) is not None:
                    pe.wait_ge(rows_y_ready, snap(pe, n))
                turn_features(t, z).then_inc(z_turned, 1)

            block_loop(pe, g, [(3, stage4), (2, stage3), (1, stage2), (0, stage1)])

        @block.scalar
        def _(act):
            def std(t, n):
                act.wait_ge(var_ready[n], t.n1)
                act.activation(dev[0:t.parts, n, 0, 0:t.rows], mom[0:t.parts, n, 0:t.rows, 1], ACT.Sqrt,
                               bias=g.ln_eps[0:t.parts, :]).then_inc(std_ready[n], 1)

            def stage4(t):
                std(t, 3)

            def stage3(t):
                act.wait_ge(turned[1], t.n1)
                act.wait_ge(gcn_done, t.n)
                act.activation(high[1][:, :, 0:t.cols], turned_ps[:, :, 0:t.cols], ACT.Copy).then_inc(high_ready[1], 1)
                act.wait_ge(gcn_done, t.n1)
                act.wait_ge(low_ready[2], t.n)
                act.wait_ge(gcn_turned, t.n)
                for n in range(KC):
                    ins = act.activation(gcn[:, n, 0:t.cols], layer_ps[:, n, 0:t.cols], ACT.Relu,
                                         bias=g.bs_col[:, 0, n:n + 1])
                ins.then_inc(gcn_ready, 1)
                act.wait_ge(gcn_ready, t.n1)
                act.wait_ge(last_done, t.n)
                act.activation(high[2][:, :, 0:t.cols], gcn[:, :, 0:t.cols], ACT.Copy).then_inc(high_ready[2], 1)
                act.wait_ge(gcn_turned, t.n1)
                act.wait_ge(stored[3][t.par], t.h16)
                act.activation(rows_y[0:t.parts, t.par, 0:t.rows, :], rows_ps[0:t.parts, 0:t.rows, :], ACT.Copy
                               ).then_inc(rows_y_ready, 1)

            def stage2(t):
                act.wait_ge(turned[0], t.n1)
                act.wait_ge(appnp_done, t.n)
                act.activation(high[0][:, :, 0:t.cols], turned_ps[:, :, 0:t.cols], ACT.Relu).then_inc(high_ready[0], 1)
                std(t, 2)

            def stage1(t):
                act.wait_ge(y_loaded[t.par], t.h17)
                act.wait_ge(z_turned, t.n)
                for f in range(KC):
                    ins = act.activation(z[:, f, 0:t.cols], y[:, t.par, f, 0:t.cols], ACT.Identity,
                                         scale=g.bn_scale[:, f:f + 1], bias=g.bn_shift[:, f:f + 1])
                ins.then_inc(z_ready, 1)
                std(t, 0)
                std(t, 1)

            block_loop(act, g, [(3, stage4), (2, stage3), (1, stage2), (0, stage1)])

        @block.vector
        def _(v):
            def norm_stats(t, n, rows):
                v.wait_ge(raw_ready[n] if n != 1 else normed[0], t.n1)
                for r in range(t.rows):
                    ins = v.bn_stats(stats[0:t.parts, n, r, :], rows[0:t.parts, r, :])
                ins.then_inc(stats_ready[n], 1)
                v.wait_ge(stats_ready[n], t.n1)
                v.wait_ge(normed[n], t.n)
                v.sem_inc(stats_seen, 1)
                for r in range(t.rows):
                    ins = v.bn_aggr(mom[0:t.parts, n, r, :], stats[0:t.parts, n, r, :])
                ins.then_inc(var_ready[n], 1)
                v.wait_ge(std_ready[n], t.n1)
                v.reciprocal(dev[0:t.parts, n, 1, 0:t.rows], dev[0:t.parts, n, 0, 0:t.rows]).then_inc(rstd_ready[n], 1)

            def split(t, part, src, ready, relu=False):
                v.wait_ge(ready, t.n1)
                a, b, c = low[part][:, :, 0:t.cols], src[:, :, 0:t.cols], high[part][:, :, 0:t.cols].bitcast(F32)
                if relu:
                    ins = v.scalar_tensor_tensor(out=a, in0=b, scalar=0.0, in1=c, op0=ALU.max, op1=ALU.subtract)
                else:
                    ins = v.tensor_tensor(a, b, c, ALU.subtract)
                ins.then_inc(low_ready[part], 1)

            def stage4(t):
                v.wait_ge(last_done, t.n1)
                v.wait_ge(normed[3], t.n)
                v.scalar_tensor_tensor(out=raw[2][0:t.parts, 0:t.rows, :], in0=last_ps[0:t.parts, 0:t.rows, :],
                                       scalar=0.0, in1=rows3[0:t.parts, t.par, 0:t.rows, :], op0=ALU.max, op1=ALU.add
                                       ).then_inc(raw_ready[3], 1)
                norm_stats(t, 3, raw[2])

            def stage3(t):
                split(t, 1, turned_ps, high_ready[1])
                split(t, 2, gcn, high_ready[2])

            def stage2(t):
                split(t, 0, turned_ps, high_ready[0], relu=True)
                v.wait_ge(appnp_done, t.n1)
                v.wait_ge(normed[2], t.n)
                layer = layer_ps[:, :, :].rearrange("p a (b n) -> p (a b) n", n=D)
                v.tensor_tensor(raw[1][0:t.parts, 0:t.rows, :], layer[0:t.parts, 0:t.rows, :],
                                rows2[0:t.parts, t.par, 0:t.rows, :], ALU.add).then_inc(raw_ready[2], 1)
                norm_stats(t, 2, raw[1])

            def stage1(t):
                v.wait_ge(z_turned, t.n1)
                v.wait_ge(x_loaded[t.par], t.h17)
                v.wait_ge(normed[0], t.n)
                v.tensor_tensor(raw[0][0:t.parts, 0:t.rows, :], rows_ps[0:t.parts, 0:t.rows, :],
                                x[0:t.parts, t.par, 0:t.rows, :], ALU.add).then_inc(raw_ready[0], 1)
                norm_stats(t, 0, raw[0])
                norm_stats(t, 1, rows1[:, t.par])

            block_loop(v, g, [(3, stage4), (2, stage3), (1, stage2), (0, stage1)])

        @block.gpsimd
        def _(pool):
            def norm(t, n, src, out, table, wait=()):
                pool.wait_ge(rstd_ready[n], t.n1)
                pool.wait_ge(stored[table][t.par], t.h16)
                for sem, value in wait:
                    pool.wait_ge(sem, value)
                pool.sem_inc(norm_seen, 1)
                for r in range(t.rows):
                    ins = pool.tensor_scalar(out[0:t.parts, t.par, r, :], src[0:t.parts, r, :],
                                             mom[0:t.parts, n, r, 0:1], dev[0:t.parts, n, 1, r:r + 1],
                                             ALU.subtract, ALU.mult)
                ins.then_inc(normed[n], 1)

            def stage4(t):
                norm(t, 3, raw[2], rows4, 4)

            def stage2(t):
                n = later(t.n, -1)
                norm(t, 2, raw[1], rows3, 2, [(raw_ready[3], snap(pool, n))] if n is not None else [])

            def stage1(t):
                norm(t, 0, raw[0], rows1, 0)
                n = later(t.n, -1)
                norm(t, 1, rows1[:, t.par], rows2, 1, [(raw_ready[2], snap(pool, n))] if n is not None else [])

            block_loop(pool, g, [(3, stage4), (1, stage2), (0, stage1)])




def gnn_program(nc, x, src, dst, ew, eps, W1, b1, W2, b2, gamma, beta, Wgat, a_src, a_dst, WL2, bL2, WL3, bL3,
                resW, resb, out):
    g = Program()
    g.x, g.src, g.dst, g.ew, g.eps, g.W1, g.b1, g.W2, g.b2 = x, src, dst, ew, eps, W1, b1, W2, b2
    g.gamma, g.beta, g.Wgat, g.a_src, g.a_dst, g.WL2, g.bL2 = gamma, beta, Wgat, a_src, a_dst, WL2, bL2
    g.WL3, g.bL3, g.resW, g.resb, g.out = WL3, bL3, resW, resb, out
    N, E = x.shape[0], src.shape[0]
    g.N, g.E = N, E
    g.ES = -(-E // (T8 * P))
    g.ET = ET = T8 * g.ES
    g.EP = EP = ET * P
    g.NB = -(-ET // P)
    full, rest = divmod(N, BLOCK)
    assert rest and full >= 8 and g.ES >= 4 and N < 65535
    g.NBLK = full + 1
    g.tail = tail_shape(rest)
    g.NTP = max(p for p in range(1, P + 1) if N % p == 0)
    g.NTR = N // g.NTP

    def table(name, shape, dt=F32):
        return nc.dram_tensor(name, shape, dt).ap()

    g.agg_table = table("agg_table", [N, D])
    g.y_table = table("y_table", [g.NBLK * P, KC * BLOCK])
    g.x1_table = table("x1_table", [N, D])
    g.x2_table = table("x2_table", [N + 2 * EP, D])
    g.x3_table = table("x3_table", [N + EP, D])
    g.y1_table = table("y1_table", [N + EP, D])
    g.x1_slots = table("x1_slots", [EP, D])
    g.h_slots = table("h_slots", [EP, D])
    g.score_lines = table("line_table", [H, 2, EP])
    g.node_table = table("node_table", [N, 4])
    g.key_rows = table("key_rows", [1, EP], U16)

    with ExitStack() as ctx:
        m = Memory(nc, ctx, "all")
        g.keys = m.sb("keys", [P, EP + 2], U16)
        g.edge_fields = m.sb("edge_fields", [P, ET + T8, NFIELD])
        g.bn_scale = m.sb("bn_scale", [P, KC])
        g.bn_shift = m.sb("bn_shift", [P, KC])
        g.ident = m.sb("ident", [P, P])
        g.sel0 = m.sb("sel0", [P, P], F32R)
        g.ln_eps = m.sb("ln_eps", [P, 1])
        g.eps1 = m.sb("eps1", [P, 1])
        g.b1_col = m.sb("b1_col", [P, 2 * D // P])
        g.b2_col = m.sb("b2_col", [P, KC])
        g.gamma_col = m.sb("gamma_col", [P, KC])
        g.beta_col = m.sb("beta_col", [P, KC])
        g.bs_col = m.sb("bs_col", [P, 2, KC])
        g.bias_rows = m.sb("bias_rows", [P, 2, 3, D], F32R)
        g.wl2, g.wg0, g.wg1, g.wres, g.ws0, g.ws1, g.wgat, g.wat = (
            m.sb(f"w_{name}", [P, 2, KC, D], F32R)
            for name in ("l2", "gcn0", "gcn1", "res", "sum0", "sum1", "gat", "scores"))

        with ExitStack() as first_half:
            m = Memory(nc, first_half, "half1")
            g.deg_in = m.sb("deg_in", [P, ET, 4], F32R)
            g.deg = m.sb("deg", [P, ET, 4])
            g.slot_row = m.sb("slot_row", [P, ET])
            g.slot_info = m.sb("slot_info", [P, ET, 4])
            g.src_info = m.sb("src_info", [P, ET, 4])
            g.bn_stats = m.sb("bn_stats", [P, KC, g.NBLK, 6])
            g.w1 = m.sb("w1", [P, 2, KC, 2 * D], F32R)
            g.w2 = m.sb("w2", [P, 2, 2 * KC, D], F32R)
            setup(nc, g)
            edge_layer(nc, g, "sum0", g.x, SRC, None)
            degrees(nc, g)
            gin_hidden(nc, g)
            norm_and_fields(nc, g)
        dense_layers(nc, g)
        gat_scores(nc, g)
        gat_sum(nc, g)
        x2, h1 = (g.x2_table, N), (g.x2_table, N + EP)
        x3, y1 = (g.x3_table, N), (g.y1_table, N)
        edge_layer(nc, g, "hop1", g.x2_table[0:N + EP, :], ROW, C_APPNP, [x2], D_KEEP, D_HALF, result=h1)
        edge_layer(nc, g, "hop2", g.x2_table, ROW_H, C_APPNP, [h1, x2], D_HALF2, D_HALF, [g.wl2], True, 0,
                   result=x3, norm=True)
        edge_layer(nc, g, "gcn1", g.x3_table, ROW, C_GCN, [x3], DIS2, DIS, [g.wg0, g.wres], False, 1, result=y1)
        edge_layer(nc, g, "gcn2", g.y1_table, ROW, C_GCN, [y1, x3], DIS2, DIS, [g.wg1, g.wres], False, 2,
                   norm=True)


_INS = ["x", "src", "dst", "edge_weight", "L0_gnn_eps", "L0_gnn_W1", "L0_gnn_b1", "L0_gnn_W2", "L0_gnn_b2",
        "L0_gnn_gamma", "L0_gnn_beta", "L1_gnn_W", "L1_gnn_a_src", "L1_gnn_a_dst", "L2_gnn_W", "L2_gnn_b",
        "L3_gnn_W", "L3_gnn_b", "L3_gnn_resW", "L3_gnn_resb"]


def kernel(**inputs):
    import numpy as _np
    import concourse.bacc as _bacc
    from concourse import mybir as _mybir
    from concourse.bass_utils import run_bass_kernel_spmd as _run

    nc = _bacc.Bacc("TRN2", target_bir_lowering=False, num_devices=1)
    arrays, args = {}, []
    for name in _INS:
        a = _np.ascontiguousarray(inputs[name])
        arrays[f"in_{name}_dram"] = a
        args.append(nc.dram_tensor(f"in_{name}_dram", a.shape, _mybir.dt.from_np(a.dtype), kind="ExternalInput").ap())
    out = nc.dram_tensor("out_0_dram", inputs["x"].shape, _mybir.dt.float32, kind="ExternalOutput").ap()
    gnn_program(nc, *args, out)
    r = _run(nc, [arrays], core_ids=[0])
    return r.results[0]["out_0_dram"]
```

```python
from contextlib import ExitStack

import concourse.bass as bass
from concourse import mybir

F32 = mybir.dt.float32
F32R = mybir.dt.float32r
I32 = mybir.dt.int32
U16 = mybir.dt.uint16
ALU = mybir.AluOpType
ACT = mybir.ActivationFunctionType

P = 128
D = 256
KC = D // P
H = 8
DH = D // H
T8 = 8
T4 = 4
MS = 4
R4 = 4
BLOCK = P * R4
LN_EPS = 1e-5
BN_EPS = 1e-5
GAT_EPS = 1e-8
NEG_SLOPE = 0.2
BIG = 1e30
ZERO_COLS = 2048
SKIP = float(1 << 23)

(KEY, CARRY, SRC, DSTG, SCAT, ROW, ROW_H, C_APPNP, C_GCN, D_HALF, D_KEEP, D_HALF2, DIS, DIS2, EW, LAST) = range(16)
NFIELD = 16


def snap(eng, v):
    return v if isinstance(v, int) else eng.snap(v)


def tail_shape(rows):
    for r in range(1, R4 + 1):
        if rows % r == 0 and rows // r <= P and (rows // r) % 16 == 0:
            return rows // r, r
    raise ValueError(f"no layout for {rows} rows")


class Memory:

    def __init__(self, nc, ctx, phase):
        self.nc, self.ctx, self.phase, self.used = nc, ctx, phase, []
        ctx.callback(self.end)

    def end(self):
        if self.used:
            self.nc.clear_and_free_semaphores(self.used)
            self.nc.all_engine_barrier()

    def sb(self, name, shape, dt=F32):
        return self.ctx.enter_context(self.nc.sbuf_tensor(f"{self.phase}_{name}", shape, dt))

    def ps(self, name, shape):
        return self.ctx.enter_context(self.nc.psum_tensor(f"{self.phase}_{name}_psum", shape, F32))

    def sem(self, name):
        self.used.append(self.nc.alloc_semaphore(f"{self.phase}_{name}"))
        return self.used[-1]

    def sems(self, name, n):
        return [self.sem(f"{name}{i}") for i in range(n)]


class Program:
    pass


def mm3(pe, out, lhs, rhs, first, last):
    for n, (a, b) in enumerate(((0, 0), (0, 1), (1, 0))):
        m = pe.matmul(out, lhs[a], rhs[b], start=first and n == 0, stop=last and n == 2,
                      skip_group_check=True)
    return m




def setup(nc, g):
    N, E, ET, NB = g.N, g.E, g.ET, g.NB
    with ExitStack() as ctx:
        m = Memory(nc, ctx, "set")
        stage = m.sb("stage", [P, 13, 512])
        arow = m.sb("arow", [P, 2, D])
        prod = m.sb("prod", [P, 2, KC, D])
        brow = m.sb("brow", [P, 3, 2, D])
        bg_col = m.sb("bg_col", [P, 2, KC])
        bres_col = m.sb("bres_col", [P, KC])
        eps_in = m.sb("eps_in", [P, 1])
        raw_i = m.sb("raw_i", [P, 3, NB, P], I32)
        raw_f = m.sb("raw_f", [P, 4, NB, P])
        key16 = m.sb("key16", [P, NB, P], U16)
        rowid = m.sb("rowid", [P, ET], I32)
        pid = m.sb("pid", [P, 1], I32)
        pidf = m.sb("pidf", [P, 1])
        p127 = m.sb("p127", [P, 1])
        p01 = m.sb("p01", [P, 1])
        bias_high = m.sb("bias_high", [P, 3, D], F32R)
        bias_low = m.sb("bias_low", [P, 3, D])
        ones = m.sb("ones", [P, P])
        colf = m.sb("colf", [P, P])
        zeros = m.sb("zeros", [P, ZERO_COLS])
        nt = m.sb("nt", [g.NTP, g.NTR, 4])
        ps = m.ps("ps", [P, 8, 512])
        load_w = m.sem("load_w")
        load_e = m.sem("load_e")
        blank = m.sem("blank")
        iotas = m.sem("iotas")
        ident_ready = m.sem("ident_ready")
        key16_ready = m.sem("key16_ready")
        rawf_ready = m.sem("rawf_ready")
        fields_copied = m.sem("fields_copied")
        step = m.sem("step")
        turned = m.sem("turned")
        w_turned = m.sem("w_turned")
        zeroed = m.sem("zeroed")
        init = m.sem("init")
        keys_out = m.sem("keys_out")
        keys_in = m.sem("keys_in")

        def two(n):
            return stage[:, n, :].rearrange("p (k n) -> p k n", n=D)

        st_w1 = stage[:, 0:2, :]
        st_w2 = stage[:, 2:4, :].rearrange("p a (b n) -> p (a b) n", n=D)
        st_gat, st_l2, st_g0, st_g1, st_res, st_s0, st_s1, st_l2t, st_at = (two(n) for n in range(4, 13))

        by_k = "(k p) n -> p k n"
        weights = [(st_w1, g.W1.rearrange(by_k, p=P)), (st_w2, g.W2.rearrange(by_k, p=P)),
                   (st_l2, g.WL2.rearrange(by_k, p=P)), (st_g0, g.WL3[0].rearrange(by_k, p=P)),
                   (st_g1, g.WL3[1].rearrange(by_k, p=P)), (st_res, g.resW.rearrange(by_k, p=P)),
                   (arow[:, 0, :], g.a_src.rearrange("(a h) f -> a (h f)", a=1).broadcast_to([P, D])),
                   (arow[:, 1, :], g.a_dst.rearrange("(a h) f -> a (h f)", a=1).broadcast_to([P, D])),
                   (eps_in[:, :], g.eps.rearrange("(a b) -> a b", a=1).broadcast_to([P, 1]))]
        for k in range(KC):
            weights.append((st_gat[:, k, :].rearrange("p (h f) -> p h f", h=H),
                            g.Wgat[:, k * P:(k + 1) * P, :].rearrange("h p f -> p h f")))
        for out, vec in ((g.b1_col[:, :], g.b1), (g.b2_col[:, :], g.b2), (g.gamma_col[:, :], g.gamma),
                         (g.beta_col[:, :], g.beta), (bg_col[:, 0], g.bL3[0]), (bg_col[:, 1], g.bL3[1]),
                         (bres_col[:, :], g.resb)):
            weights.append((out, vec.rearrange("(c p) -> p c", p=P)))
        rows = [(brow[0:2, 0, 0, :], g.bL2), (brow[0:2, 1, 0, :], g.bL3[0]), (brow[0:2, 2, 0, :], g.bL3[1]),
                (brow[0:2, 1, 1, :], g.resb), (brow[0:2, 2, 1, :], g.resb)]
        weights += [(out, vec.rearrange("(a n) -> a n", a=1).broadcast_to([2, D])) for out, vec in rows]

        edges = []
        for n, (vec, skip) in enumerate(((g.dst, 0), (g.dst, 1), (g.src, 0), (g.ew, 0))):
            tile = raw_i[:, n] if n < 3 else raw_f[:, 3]
            full, rest = divmod(E - skip, P)
            for q in range(NB):
                n_rows = min(P, full - q * P)
                if n_rows > 0:
                    lo = skip + q * P * P
                    edges.append((tile[0:n_rows, q, :], vec[lo:lo + n_rows * P].rearrange("(t p) -> t p", p=P)))
            if rest:
                lo = skip + full * P
                edges.append((tile[full % P:full % P + 1, full // P, 0:rest],
                              vec[lo:lo + rest].rearrange("(a n) -> a n", a=1)))
        zero_rows = N * D // ZERO_COLS
        zero_n = -(-zero_rows // P)

        block = ctx.enter_context(nc.Block())

        @block.sync
        def _(sp):
            sp.wait_ge(blank, 2)
            sp.wait_ge(blank, 5)
            for out, src in edges:
                sp.dma_start(out, src).then_inc(load_e, 16)
            sp.wait_ge(blank, 6)
            flat = g.agg_table.rearrange("(a r) d -> a (r d)", r=ZERO_COLS // D)
            for lo in range(0, zero_rows, P):
                n = min(P, zero_rows - lo)
                sp.dma_start(flat[lo:lo + n, :], zeros[0:n, :]).then_inc(zeroed, 16)
            sp.wait_ge(iotas, 3)
            sp.wait_ge(blank, 8)
            sp.dma_start(g.node_table.rearrange("(p r) c -> p (r c)", p=g.NTP),
                         nt[:, :, :].rearrange("p r c -> p (r c)")).then_inc(init, 16)
            sp.wait_ge(key16_ready, 1)
            for q in range(NB):
                n = min(P, ET - q * P)
                sp.dma_start(g.key_rows[0:1, q * P * P:q * P * P + n * P].rearrange("a (t p) -> (a t) p", p=P),
                             key16[0:n, q, :]).then_inc(keys_out, 16)
            sp.wait_ge(keys_out, 16 * NB)
            sp.wait_ge(blank, 9)
            sp.dma_start(g.keys[:, 1:1 + g.EP], g.key_rows.broadcast_to([P, g.EP])).then_inc(keys_in, 16)
            sp.wait_ge(keys_in, 16)
            sp.wait_ge(init, 16)
            sp.wait_ge(zeroed, 16 * zero_n)

        @block.scalar
        def _(act):
            act.wait_ge(blank, 1)
            for out, src in weights:
                act.dma_start(out, src, allow_slow_non_contiguous=True).then_inc(load_w, 16)

        @block.gpsimd
        def _(pool):
            pool.iota(rowid[:, :], [[2 * P, ET // 2], [1, 2]], base=N, channel_multiplier=2).then_inc(iotas, 1)
            pool.iota(pid[:, :], [[1, 1]], base=0, channel_multiplier=1).then_inc(iotas, 1)
            pool.iota(nt[:, :, 0:1].bitcast(I32).rearrange("p r c -> p (r c)"), [[1, g.NTR]], base=0,
                      channel_multiplier=g.NTR).then_inc(iotas, 1)

        @block.vector
        def _(v):
            linked = 0

            def link(ins):
                nonlocal linked
                ins.then_inc(step, 1)
                linked += 1
                v.wait_ge(step, linked)

            v.memset(brow[:, :, :, :], 0.0).then_inc(blank, 1)
            v.memset(raw_i[:, 0:2], N).then_inc(blank, 1)
            v.memset(raw_i[:, 2], 0).then_inc(blank, 1)
            v.memset(raw_f[:, 3], 0.0).then_inc(blank, 1)
            v.memset(g.ln_eps[:, :], LN_EPS)
            v.memset(g.ln_eps2[:, :], LN_EPS ** 2).then_inc(blank, 1)
            v.memset(zeros[:, :], 0.0).then_inc(blank, 1)
            v.memset(nt[:, :, 1:3], 1.0).then_inc(blank, 1)
            v.memset(nt[:, :, 3:4], 0.0).then_inc(blank, 1)
            v.memset(g.keys[:, :], 65535).then_inc(blank, 1)
            v.memset(g.edge_fields[:, :, :], 0.0).then_inc(blank, 1)
            v.memset(stage[:, 12, :], 0.0).then_inc(blank, 1)
            v.wait_ge(iotas, 3)
            v.wait_ge(blank, 11)
            link(v.tensor_copy(pidf[:, :], pid[:, :]))
            link(v.memset(ones[:, :], 1.0))
            link(v.tensor_tensor_scan(colf[:, :], ones[:, :], ones[:, :], -1.0, ALU.mult, ALU.add))
            link(v.tensor_scalar(g.ident[:, :], colf[:, :], pidf[:, 0:1], None, ALU.is_equal))
            link(v.tensor_tensor(p01[:, :], g.ident[:, 0:1], g.ident[:, 1:2], ALU.add))
            link(v.tensor_scalar(g.sel01[:, :], ones[:, :], p01[:, 0:1], None, ALU.mult))
            v.tensor_scalar(p127[:, :], pidf[:, :], float(P - 1), None, ALU.is_equal).then_inc(ident_ready, 1)
            v.wait_ge(ident_ready, 1)
            v.wait_ge(load_e, 16 * len(edges))
            v.tensor_copy(key16[:, :, :], raw_i[:, 0]).then_inc(key16_ready, 1)
            v.tensor_copy(raw_f[:, 0:3], raw_i[:, :]).then_inc(rawf_ready, 1)
            fields = g.edge_fields
            n_ps = 0
            for field in (KEY, LAST, SRC, EW):
                for q in range(NB):
                    n = min(P, ET - q * P)
                    v.wait_ge(turned, n_ps + 1)
                    v.tensor_copy(fields[:, q * P:q * P + n, field], ps[:, n_ps % 8, 0:n]).then_inc(fields_copied, 1)
                    n_ps += 1
            v.wait_ge(fields_copied, 4 * NB)

            def f(c):
                return fields[:, 0:ET, c]

            link(v.tensor_tensor(f(LAST), f(LAST), f(KEY), ALU.not_equal))
            link(v.tensor_scalar(f(SCAT), f(LAST), -SKIP, SKIP, ALU.mult, ALU.add))
            link(v.tensor_tensor(f(SCAT), f(SCAT), f(KEY), ALU.add))
            link(v.tensor_scalar(f(DSTG), f(KEY), float(N - 1), None, ALU.min))
            link(v.tensor_scalar(fields[:, 1:ET, CARRY], fields[:, 0:ET - 1, KEY], 1.0, p127[:, 0:1],
                                 ALU.add, ALU.mult))
            link(v.tensor_scalar(f(CARRY), f(CARRY), -1.0, None, ALU.add))
            link(v.tensor_copy(g.deg_in[:, :, 0], f(EW)))
            link(v.tensor_tensor(g.deg_in[:, :, 1], f(EW), g.deg_in[:, :, 0].bitcast(F32), ALU.subtract))
            link(v.tensor_scalar(g.deg_in[:, :, 2], f(EW), 0.0, 1.0, ALU.mult, ALU.add))
            link(v.tensor_scalar(g.deg_in[:, :, 3], f(EW), 0.0, None, ALU.mult))
            link(v.tensor_copy(g.slot_row[:, :], rowid[:, :]))

            v.wait_ge(load_w, 16 * len(weights))
            for s in range(2):
                for k in range(KC):
                    link(v.tensor_tensor(prod[:, s, k, :], st_gat[:, k, :], arow[:, s, :], ALU.mult))
                for k in range(KC):
                    link(v.tensor_reduce(st_at[:, k, s * P:s * P + H],
                                         prod[:, s, k].rearrange("p (h f) -> p h f", h=H),
                                         mybir.AxisListType.X, ALU.add))
            link(v.tensor_tensor(st_s0, st_g0, st_res, ALU.add))
            link(v.tensor_tensor(st_s1, st_g1, st_res, ALU.add))
            for l in range(2):
                link(v.tensor_tensor(g.bs_col[:, l], bg_col[:, l], bres_col[:, :], ALU.add))
            link(v.tensor_tensor(brow[:, :, 0, :], brow[:, :, 0, :], brow[:, :, 1, :], ALU.add))
            link(v.tensor_scalar(g.eps1[:, :], eps_in[:, :], 1.0, None, ALU.add))
            v.wait_ge(w_turned, KC * KC)
            for k in range(KC):
                for n in range(KC):
                    link(v.tensor_copy(st_l2t[:, k, n * P:(n + 1) * P], ps[:, 2 * k + n, 0:P]))
            for w, src in ((g.w1, st_w1), (g.w2, st_w2), (g.wl2, st_l2t), (g.wg0, st_g0), (g.wg1, st_g1),
                           (g.wres, st_res), (g.ws0, st_s0), (g.ws1, st_s1), (g.wgat, st_gat), (g.wat, st_at)):
                link(v.tensor_copy(w[:, 0], src))
                link(v.tensor_tensor(w[:, 1], src, w[:, 0].bitcast(F32), ALU.subtract))
            link(v.tensor_copy(bias_high[:, :, :], brow[:, :, 0, :]))
            link(v.tensor_tensor(bias_low[:, :, :], brow[:, :, 0, :], bias_high[:, :, :].bitcast(F32), ALU.subtract))
            link(v.tensor_scalar(bias_low[:, :, :], bias_low[:, :, :], g.ident[:, 1:2], None, ALU.mult))
            link(v.scalar_tensor_tensor(out=g.bias_rows[:, :, :], in0=bias_high[:, :, :].bitcast(F32),
                                        scalar=g.ident[:, 0:1], in1=bias_low[:, :, :], op0=ALU.mult, op1=ALU.add))

        @block.tensor
        def _(pe):
            pe.wait_ge(ident_ready, 1)
            pe.wait_ge(rawf_ready, 1)
            n_ps = 0
            for n in range(4):
                for q in range(NB):
                    n_rows = min(P, ET - q * P)
                    if n_ps >= 8:
                        pe.wait_ge(fields_copied, n_ps - 7)
                    pe.transpose(ps[:, n_ps % 8, 0:n_rows], raw_f[0:n_rows, n, q, :], g.ident[0:n_rows, 0:n_rows]
                                 ).then_inc(turned, 1)
                    n_ps += 1
            pe.wait_ge(fields_copied, 4 * NB)
            pe.wait_ge(load_w, 16 * len(weights))
            for k in range(KC):
                for n in range(KC):
                    pe.transpose(ps[:, 2 * k + n, 0:P], st_l2[:, n, k * P:(k + 1) * P], g.ident[:, :]
                                 ).then_inc(w_turned, 1)




class Tile:

    def __init__(self, values, k):
        self.values, self.k = values, k
        self.b, self.m = k % T8, k % MS
        self.s, self.s1, self.s2 = (values.s.get(k // T8 + n) for n in range(3))
        self.now = values.now(k // MS + 1)
        self.d16, self.d17 = values.dma(k // T8), values.dma(k // T8 + 1)
        self.duo = self.b // 2

    def back(self, d):
        return Tile(self.values, self.k - d)

    def at(self, step):
        return self.s * (T8 * step) + self.b * step


class Values:

    def __init__(self, eng, q, most, dma):
        self.q, self.loop = q, not isinstance(q, int)
        low = -(-most // T8)
        self.s = {o: snap(eng, q + o) if o else q for o in range(-low, 3)}
        if self.loop:
            self.nows = {o: snap(eng, q * (T8 // MS) + o) for o in range((-most) // MS + 1 - T8 // MS, T8 // MS + 1)}
            self.dmas = {o: snap(eng, (q + o) * 16) for o in range(-low, 2)} if dma else {}

    def now(self, o):
        if self.loop:
            return self.nows.get(o)
        return max(0, self.q * (T8 // MS) + o)

    def dma(self, o):
        if self.loop:
            return self.dmas.get(o)
        return max(0, (self.q + o) * 16)


def tile_loop(eng, steps, stages, dma=True):
    most = max(lag for lag, _ in stages)

    def step(q):
        values = Values(eng, q, most, dma)
        for c in range(T8):
            for lag, work in stages:
                if values.loop or 0 <= q * T8 + c - lag < steps * T8:
                    work(Tile(values, c - lag))

    q0 = 1 + -(-most // T8)
    for q in range(q0):
        step(q)
    with eng.Fori(q0, steps) as q:
        step(q)
    for q in range(steps, steps - 1 + q0):
        step(q)


class EdgeSum:

    def __init__(self, m, g, table, index, coef, width=D):
        self.g, self.table, self.index, self.coef, self.width = g, table, index, coef, width
        self.degrees = index == SRC
        self.rows = m.sb("rows", [P, T8, width])
        self.high = m.sb("high", [P, MS, width], F32R)
        self.low = m.sb("low", [P, MS, width], F32R)
        self.same = m.sb("same", [P, MS, P], F32R)
        self.carry = m.sb("carry", [P, MS, P])
        self.here = m.sb("here", [P, T8, NFIELD])
        self.next_index = m.sb("next_index", [P, T8], I32)
        self.summed = m.sb("summed", [P, T8, width + (4 if self.degrees else 0)])
        self.ps = [m.ps(f"sums{b}", [P, 512]) for b in range(2)]
        self.index_ready = m.sem("index_ready")
        self.index_seen = m.sem("index_seen")
        self.gathered = m.sems("gathered", T8 if table is not None else MS)
        self.here_ready = m.sem("here_ready")
        self.high_ready = m.sems("high_ready", MS)
        self.same_ready = m.sems("same_ready", MS)
        self.low_ready = m.sems("low_ready", MS)
        self.summed_in_psum = m.sems("summed_in_psum", MS)
        self.summed_ready = m.sems("summed_ready", MS)
        self.blank = m.sem("blank")

    def first(self, v):
        v.memset(self.summed[:, :, :], 0.0).then_inc(self.blank, 1)
        if self.table is not None:
            for b in range(0, T8, MS):
                v.tensor_copy(self.next_index[:, b:b + MS], self.g.edge_fields[:, b:b + MS, self.index]
                              ).then_inc(self.index_ready, 1)

    def pool_gather(self, pool, t):
        pool.wait_ge(self.index_ready, t.now)
        pool.sem_inc(self.index_seen, 1)
        pool.indirect_dma_start(self.rows[:, t.b, 0:D], None, self.table,
                                bass.IndirectOffsetOnAxis(self.next_index[:, t.b:t.b + 1], 0)
                                ).then_inc(self.gathered[t.b], 16)

    def act_high(self, act, t):
        if self.coef is not None:
            act.wait_ge(self.here_ready, t.now)
        if self.table is not None:
            act.wait_ge(self.gathered[t.b], t.d17)
        else:
            act.wait_ge(self.gathered[t.m], t.now)
        act.wait_ge(self.summed_in_psum[t.m], t.back(MS).now)
        scale = 1.0 if self.coef is None else self.here[:, t.b, self.coef:self.coef + 1]
        act.activation(self.high[:, t.m, :], self.rows[:, t.b, :], ACT.Copy, scale=scale
                       ).then_inc(self.high_ready[t.m], 1)

    def act_evacuate(self, act, t):
        act.wait_ge(self.summed_in_psum[t.m], t.now)
        w = self.summed.shape[2]
        act.activation(self.summed[:, t.b, :], self.ps[t.b % 2][:, 0:w], ACT.Copy
                       ).then_inc(self.summed_ready[t.m], 1)

    def vec_here(self, v, t):
        last = t.back(T8 - MS + 1)
        v.wait_ge(self.same_ready[last.m], last.now)
        v.tensor_scalar(self.here[:, t.b:t.b + MS, :], self.g.edge_fields[:, bass.ds(t.at(1), MS), :],
                        1.0, None, ALU.mult).then_inc(self.here_ready, 1)

    def vec_matrices(self, v, t):
        g = self.g
        v.wait_ge(self.here_ready, t.now)
        v.wait_ge(self.summed_in_psum[t.m], t.back(MS).now)
        keys = g.keys[:, bass.ds(t.at(P) + 1, P)]
        v.tensor_scalar(self.same[:, t.m, :], keys, self.here[:, t.b, KEY:KEY + 1], None, ALU.is_equal)
        v.tensor_scalar(self.carry[:, t.m, :], keys, self.here[:, t.b, CARRY:CARRY + 1], None, ALU.is_equal
                        ).then_inc(self.same_ready[t.m], 1)

    def vec_low(self, v, t):
        v.wait_ge(self.high_ready[t.m], t.now)
        scale = 1.0 if self.coef is None else self.here[:, t.b, self.coef:self.coef + 1]
        v.scalar_tensor_tensor(out=self.low[:, t.m, :], in0=self.rows[:, t.b, :], scalar=scale,
                               in1=self.high[:, t.m, :].bitcast(F32), op0=ALU.mult, op1=ALU.subtract
                               ).then_inc(self.low_ready[t.m], 1)

    def vec_index(self, v, t):
        if t.m != MS - 1:
            return
        v.wait_ge(self.low_ready[t.m], t.now)
        v.tensor_scalar(self.next_index[:, t.b - t.m:t.b + 1],
                        self.g.edge_fields[:, bass.ds(t.at(1) + (T8 - MS + 1), MS), self.index], 1.0, None, ALU.mult
                        ).then_inc(self.index_ready, 1)

    def pe_sum(self, pe, t):
        g = self.g
        pe.wait_ge(self.same_ready[t.m], t.now)
        pe.wait_ge(self.low_ready[t.m], t.now)
        ps, w = self.ps[t.b % 2], self.width
        last = t.back(2)
        pe.wait_ge(self.summed_ready[last.m], last.now)
        pe.matmul(ps[:, 0:w], self.same[:, t.m, :], self.high[:, t.m, :], start=True, stop=False,
                  skip_group_check=True)
        pe.matmul(ps[:, 0:w], self.same[:, t.m, :], self.low[:, t.m, :], start=False, stop=False,
                  skip_group_check=True)
        if self.degrees:
            pe.matmul(ps[:, w:w + 4], self.same[:, t.m, :],
                      g.deg_in[:, bass.ds(t.at(1), 1), :].rearrange("p a c -> p (a c)"),
                      start=False, stop=False, skip_group_check=True)
            w += 4
        before = t.back(1)
        if isinstance(t.s, int) and t.s == 0 and t.b == 0:
            pe.wait_ge(self.blank, 1)
        else:
            pe.wait_ge(self.summed_ready[before.m], before.now)
        pe.matmul(ps[:, 0:w], self.carry[:, t.m, :], self.summed[:, before.b, :], start=False, stop=True,
                  skip_group_check=True).then_inc(self.summed_in_psum[t.m], 1)


def edge_loop(eng, steps, lead=None, tail1=None):

    def step(s, before, after):
        for b in range(T4):
            if tail1:
                tail1(s, b)
            if lead and after is not None:
                lead(after, s, b)

    if lead:
        for b in range(T4):
            lead(0, None, b)
    step(0, None, 1)
    with eng.Fori(1, steps - 2) as s:
        step(s, snap(eng, s - 1), snap(eng, s + 1))
    step(steps - 2, steps - 3, steps - 1)
    step(steps - 1, steps - 2, None)


def slot_rows(table, base, s, duo, tiles=None):
    tiles = tiles or T4
    return table[bass.ds(s * (tiles * P) + (base + duo * 2 * P), 2 * P), :].rearrange("(p j) f -> p j f", p=P)


def edge_layer(nc, g, phase, table, index, coef, states=(), self_coef=None, sum_coef=None,
               weights=None, relu_first=False, bias=None, result=None, norm=False):
    ES = g.ES
    degrees = index == SRC
    products = weights is not None
    halves = len(states) > 1 and relu_first
    chunks = KC * (len(weights) if products else 0)
    scatter_to = g.agg_table if degrees else (g.out if result is None else None)
    with ExitStack() as ctx:
        m = Memory(nc, ctx, phase)
        e = EdgeSum(m, g, table, index, coef)
        state = [m.sb(f"state{n}", [P, T8, D]) for n in range(len(states))]
        loaded = [m.sems(f"loaded{n}_", T8 // 2) for n in range(len(states))]
        own = m.sb("own", [P, MS, D])
        own_ready = m.sems("own_ready", MS)
        res = m.sb("res", [P, T8, D])
        res_ready = m.sems("res_ready", MS)
        stored = m.sems("stored", T8 // 2)
        scattered = m.sems("scattered", T8)
        scatter_ready = m.sems("scatter_ready", MS)
        scatter_seen = m.sem("scatter_seen")
        next_scatter = m.sb("next_scatter", [P, T8], I32)
        deg_ready = m.sems("deg_ready", MS)
        sp_seen = m.sem("sp_seen")
        half_ready = m.sems("half_ready", MS)
        mixed_ready = m.sems("mixed_ready", MS)
        turned = m.sems("turned", MS)
        turned_high_ready = m.sems("turned_high_ready", MS)
        turned_low_ready = m.sems("turned_low_ready", MS)
        layer_ready = m.sems("layer_ready", MS)
        layer_read = m.sems("layer_read", MS)
        if products:
            mixed = m.sb("mixed", [P, MS, D])
            turned_ps = [m.ps(f"turned{k}", [P, chunks, P]) for k in range(2)]
            turned_high = m.sb("turned_high", [P, 2, chunks, P], F32R)
            turned_low = m.sb("turned_low", [P, 2, chunks, P], F32R)
            layer_ps = [m.ps(f"layer{k}", [P, 512]) for k in range(2)]
        if norm:
            stats = m.sb("stats", [P, MS, 6])
            moments = m.sb("moments", [P, MS, 2])
            dev = m.sb("dev", [P, MS, 3])
            shift_ready = m.sems("shift_ready", MS)
            stats_ready = m.sems("stats_ready", MS)
            stats_seen = m.sem("stats_seen")
            var_ready = m.sems("var_ready", MS)
            std_ready = m.sems("std_ready", MS)
            rstd_ready = m.sems("rstd_ready", MS)
        state_read = layer_read if norm else (turned if products else own_ready)
        block = ctx.enter_context(nc.Block())

        @block.sync
        def _(sp):
            def load(t):
                if t.b % 2:
                    return
                for n, (tab, base) in enumerate(states):
                    for last in (t.back(T8), t.back(T8 - 1)):
                        sp.wait_ge(state_read[last.m], last.now)
                    sp.sem_inc(sp_seen, 1)
                    sp.dma_start(state[n][:, t.b:t.b + 2, :], slot_rows(tab, base, t.s, t.duo, T8)
                                 ).then_inc(loaded[n][t.duo], 16)

            def store(t):
                if t.b % 2 == 0:
                    return
                sp.wait_ge(res_ready[t.back(1).m], t.back(1).now)
                sp.wait_ge(res_ready[t.m], t.now)
                sp.sem_inc(sp_seen, 1)
                sp.dma_start(slot_rows(*result, t.s, t.duo, T8), res[:, t.b - 1:t.b + 1, :]).then_inc(stored[t.duo], 16)

            stages = [(0, load)] if states else []
            if result is not None:
                stages.append((T8, store))
            if stages:
                tile_loop(sp, ES, stages, dma=False)
            if result is not None:
                for duo in range(T8 // 2):
                    sp.wait_ge(stored[duo], 16 * ES)

        @block.gpsimd
        def _(pool):
            def scatter(t):
                pool.wait_ge(scatter_ready[t.m], t.now)
                pool.wait_ge(scatter_from_ready[t.m], t.now)
                pool.sem_inc(scatter_seen, 1)
                pool.indirect_dma_start(scatter_to, bass.IndirectOffsetOnAxis(next_scatter[:, t.b:t.b + 1], 0),
                                        scatter_from[:, t.b, 0:D], None, bounds_check=limit, oob_is_err=False
                                        ).then_inc(scattered[t.b], 16)

            scatter_from, scatter_from_ready = (e.summed, e.summed_ready) if degrees else (res, res_ready)
            stages = [(0, lambda t: e.pool_gather(pool, t))]
            if scatter_to is not None:
                limit = pool.alloc_register(f"{phase}_limit")
                pool.reg_mov(limit, g.N - 1)
                stages.append((6 if degrees else 8, scatter))
            tile_loop(pool, ES, stages, dma=False)
            if scatter_to is not None:
                for b in range(T8):
                    pool.wait_ge(scattered[b], 16 * ES)

        @block.scalar
        def _(act):
            def evacuate(t):
                if degrees:
                    act.wait_ge(deg_ready[t.m], t.back(T8).now)
                    act.wait_ge(scattered[t.b], t.d16)
                elif products:
                    act.wait_ge(mixed_ready[t.m], t.back(T8).now)
                else:
                    act.wait_ge(res_ready[t.m], t.back(T8).now)
                e.act_evacuate(act, t)

            def own_row(t):
                act.wait_ge(loaded[0][t.duo], t.d17)
                act.wait_ge(e.here_ready, t.now)
                act.wait_ge((mixed_ready if products else res_ready)[t.m], t.back(MS).now)
                act.activation(own[:, t.m, :], state[0][:, t.b, :], ACT.Copy,
                               scale=e.here[:, t.b, self_coef:self_coef + 1]).then_inc(own_ready[t.m], 1)

            def high_turned(t):
                act.wait_ge(turned[t.m], t.now)
                act.wait_ge(layer_ready[t.back(2).m], t.back(2).now)
                act.activation(turned_high[:, t.b % 2], turned_ps[t.b % 2][:, :, :],
                               ACT.Relu if relu_first else ACT.Copy).then_inc(turned_high_ready[t.m], 1)

            def root(t):
                act.wait_ge(var_ready[t.m], t.now)
                act.activation(dev[:, t.m, 0:1], moments[:, t.m, 1:2], ACT.Sqrt, bias=g.ln_eps[:, :]
                               ).then_inc(std_ready[t.m], 1)

            def normalize(t):
                act.wait_ge(shift_ready[t.m], t.now)
                act.activation(res[:, t.b, :], res[:, t.b, :], ACT.Identity, scale=dev[:, t.m, 1:2],
                               bias=dev[:, t.m, 2:3]).then_inc(res_ready[t.m], 1)

            def finish(t):
                act.wait_ge(layer_ready[t.m], t.now)
                act.wait_ge(stored[t.duo], t.d16)
                act.activation(res[:, t.b, :], layer_ps[t.b % 2][:, 0:D], ACT.Relu).then_inc(res_ready[t.m], 1)

            stages = [(6, high_turned)] if products else []
            stages += [(8, root)] if norm else []
            stages += [(3, lambda t: e.act_high(act, t))]
            stages += [(4, own_row)] if states else []
            stages += [(7, finish)] if products and not norm else []
            stages += [(8, normalize)] if norm else []
            stages += [(4, evacuate)]
            tile_loop(act, ES, stages)

        @block.vector
        def _(v):
            e.first(v)

            def fields(t):
                if t.m:
                    return
                last = t.back(T8 - MS + 1)
                if scatter_to is not None:
                    v.wait_ge(scatter_ready[last.m], last.now)
                if not degrees:
                    v.wait_ge((mixed_ready if products else res_ready)[last.m], last.now)
                e.vec_here(v, t)

            def scatter_index(t):
                v.wait_ge(scattered[t.b], t.d16)
                v.tensor_copy(next_scatter[:, t.b:t.b + 1], e.here[:, t.b, SCAT:SCAT + 1]
                              ).then_inc(scatter_ready[t.m], 1)

            def keep_degrees(t):
                v.wait_ge(e.summed_ready[t.m], t.now)
                v.tensor_scalar(g.deg[:, bass.ds(t.at(1), 1), :].rearrange("p a c -> p (a c)"),
                                e.summed[:, t.b, D:D + 4], 1.0, None, ALU.mult).then_inc(deg_ready[t.m], 1)

            def half_row(t):
                v.wait_ge(own_ready[t.m], t.now)
                v.wait_ge(loaded[1][t.duo], t.d17)
                v.scalar_tensor_tensor(out=own[:, t.m, :], in0=state[1][:, t.b, :], scalar=0.5,
                                       in1=own[:, t.m, :], op0=ALU.mult, op1=ALU.add).then_inc(half_ready[t.m], 1)

            def mix(t):
                v.wait_ge((half_ready if halves else own_ready)[t.m], t.now)
                v.wait_ge(e.summed_ready[t.m], t.now)
                if products:
                    v.wait_ge(turned[t.m], t.back(MS).now)
                    to, ready = mixed[:, t.m, :], mixed_ready
                else:
                    v.wait_ge(stored[t.duo], t.d16)
                    to, ready = res[:, t.b, :], res_ready
                v.scalar_tensor_tensor(out=to, in0=e.summed[:, t.b, 0:D],
                                       scalar=e.here[:, t.b, sum_coef:sum_coef + 1], in1=own[:, t.m, :],
                                       op0=ALU.mult, op1=ALU.add).then_inc(ready[t.m], 1)

            def low_turned(t):
                v.wait_ge(turned_high_ready[t.m], t.now)
                high = turned_high[:, t.b % 2].bitcast(F32)
                if relu_first:
                    ins = v.scalar_tensor_tensor(out=turned_low[:, t.b % 2], in0=turned_ps[t.b % 2][:, :, :],
                                                 scalar=0.0, in1=high, op0=ALU.max, op1=ALU.subtract)
                else:
                    ins = v.tensor_tensor(turned_low[:, t.b % 2], turned_ps[t.b % 2][:, :, :], high, ALU.subtract)
                ins.then_inc(turned_low_ready[t.m], 1)

            def add_row(t):
                v.wait_ge(layer_ready[t.m], t.now)
                v.wait_ge(loaded[-1][t.duo], t.d17)
                if scatter_to is None:
                    v.wait_ge(stored[t.duo], t.d16)
                else:
                    v.wait_ge(scattered[t.b], t.d16)
                v.scalar_tensor_tensor(out=res[:, t.b, :], in0=layer_ps[t.b % 2][:, 0:D], scalar=0.0,
                                       in1=state[-1][:, t.b, :], op0=ALU.add if relu_first else ALU.max, op1=ALU.add
                                       ).then_inc(layer_read[t.m], 1)

            def row_stats(t):
                v.wait_ge(layer_read[t.m], t.now)
                v.wait_ge(rstd_ready[t.m], t.back(MS).now)
                v.bn_stats(stats[:, t.m, :], res[:, t.b, :]).then_inc(stats_ready[t.m], 1)

            def row_moments(t):
                v.wait_ge(stats_ready[t.m], t.now)
                v.wait_ge(res_ready[t.m], t.back(MS).now)
                v.sem_inc(stats_seen, 1)
                v.bn_aggr(moments[:, t.m, :], stats[:, t.m, :]).then_inc(var_ready[t.m], 1)

            def invert(t):
                v.wait_ge(std_ready[t.m], t.now)
                v.reciprocal(dev[:, t.m, 1:2], dev[:, t.m, 0:1]).then_inc(rstd_ready[t.m], 1)

            def shift_by(t):
                v.wait_ge(rstd_ready[t.m], t.now)
                v.scalar_tensor_tensor(out=dev[:, t.m, 2:3], in0=moments[:, t.m, 0:1], scalar=-1.0,
                                       in1=dev[:, t.m, 1:2], op0=ALU.mult, op1=ALU.mult).then_inc(shift_ready[t.m], 1)

            stages = [(2, fields)]
            stages += [(5, half_row)] if halves else []
            stages += [(5, scatter_index)] if scatter_to is not None else []
            stages += [(2, lambda t: e.vec_matrices(v, t))]
            stages += [(8, invert)] if norm else []
            stages += [(8, shift_by)] if norm else []
            stages += [(6, low_turned)] if products else []
            stages += [(5, keep_degrees if degrees else mix)]
            stages += [(7, add_row)] if norm else []
            stages += [(3, lambda t: e.vec_low(v, t))]
            stages += [(7, row_stats)] if norm else []
            stages += [(3, lambda t: e.vec_index(v, t))]
            stages += [(7, row_moments)] if norm else []
            tile_loop(v, ES, stages)

        @block.tensor
        def _(pe):
            def turn(t):
                pe.wait_ge(mixed_ready[t.m], t.now)
                pe.wait_ge(turned_low_ready[t.back(2).m], t.back(2).now)
                rows = [mixed[:, t.m, :]]
                if len(weights) > 1:
                    rows.append(state[0][:, t.b, :])
                    pe.wait_ge(loaded[0][t.duo], t.d17)
                for n, row in enumerate(rows):
                    for k in range(KC):
                        ins = pe.transpose(turned_ps[t.b % 2][:, KC * n + k, :], row[:, k * P:(k + 1) * P],
                                           g.ident[:, :])
                ins.then_inc(turned[t.m], 1)

            def layer(t):
                pe.wait_ge(turned_low_ready[t.m], t.now)
                read = layer_read if norm else res_ready
                pe.wait_ge(read[t.back(2).m], t.back(2).now)
                out = layer_ps[t.b % 2][:, 0:D]
                pe.matmul(out, g.sel01[:, :], g.bias_rows[:, bias, :], start=True, stop=False,
                          skip_group_check=True)
                for c in range(chunks):
                    w = weights[c // KC]
                    ins = mm3(pe, out, (turned_high[:, t.b % 2, c, :], turned_low[:, t.b % 2, c, :]),
                              (w[:, 0, c % KC, :], w[:, 1, c % KC, :]), False, c == chunks - 1)
                ins.then_inc(layer_ready[t.m], 1)

            stages = [(7, layer)] if products else []
            stages += [(4, lambda t: e.pe_sum(pe, t))]
            stages += [(5, turn)] if products else []
            tile_loop(pe, ES, stages)


def gat_scores(nc, g):
    ET = g.ET
    ES = ET // T4
    with ExitStack() as ctx:
        m = Memory(nc, ctx, "score")
        src_rows = m.sb("src_rows", [P, T4, D])
        dst_rows = m.sb("dst_rows", [P, T4, D])
        next_src = m.sb("next_src", [P, T4], I32)
        next_dst = m.sb("next_dst", [P, T4], I32)
        high = m.sb("high", [P, T4, 2 * KC, P], F32R)
        low = m.sb("low", [P, T4, 2 * KC, P], F32R)
        h_rows = m.sb("h_rows", [P, T4, D])
        raw = m.sb("raw", [H, T4, P])
        fence = m.sb("fence", [H, T4, P])
        lines = m.sb("lines", [H, 2, T4, P])
        turned_ps = [m.ps(f"turned{k}", [P, 2 * KC, P]) for k in range(2)]
        h_ps = [m.ps(f"h{k}", [P, 512]) for k in range(2)]
        s_ps = [m.ps(f"s{k}", [P, 512]) for k in range(2)]
        index_ready = m.sems("index_ready", T4)
        index_seen = m.sem("index_seen")
        src_gathered = m.sems("src_gathered", T4)
        dst_gathered = m.sems("dst_gathered", T4)
        x1_stored = m.sems("x1_stored", 2)
        turned = m.sems("turned", T4)
        high_ready = m.sems("high_ready", T4)
        low_ready = m.sems("low_ready", T4)
        h_done = m.sems("h_done", T4)
        s_done = m.sems("s_done", T4)
        h_ready = m.sems("h_ready", T4)
        h_stored = m.sems("h_stored", 2)
        raw_ready = m.sems("raw_ready", T4)
        fence_ready = m.sems("fence_ready", T4)
        fence_cut = m.sems("fence_cut", T4)
        score_ready = m.sems("score_ready", T4)
        line_ready = m.sems("line_ready", T4)
        lines_stored = m.sem("lines_stored")
        first_line = m.sem("first_line")
        sp_seen = m.sem("sp_seen")

        def slot(b):
            return T4 - 1 - b

        def tile(s, b):
            return (ET - 1 - b) - s * T4

        def turn(s, b):
            return slot((b - 2) % T4), (lambda s1: s if b < 2 else s1)

        block = ctx.enter_context(nc.Block())

        @block.sync
        def _(sp):
            def store_x1(s, duo):
                s16 = snap(sp, s * 16 + 16)
                sp.wait_ge(dst_gathered[2 * duo], s16)
                sp.wait_ge(dst_gathered[2 * duo + 1], s16)
                sp.sem_inc(sp_seen, 1)
                sp.dma_start(slot_rows(g.x1_slots, 0, (ES - 1) - s, duo), dst_rows[:, 2 * duo:2 * duo + 2, :]
                             ).then_inc(x1_stored[duo], 16)

            def store_rest(s):
                s1 = snap(sp, s + 1)
                for duo in (1, 0):
                    sp.wait_ge(h_ready[2 * duo], s1)
                    sp.wait_ge(h_ready[2 * duo + 1], s1)
                    sp.sem_inc(sp_seen, 1)
                    sp.dma_start(slot_rows(g.h_slots, 0, (ES - 1) - s, duo), h_rows[:, 2 * duo:2 * duo + 2, :]
                                 ).then_inc(h_stored[duo], 16)
                for b in range(T4):
                    sp.wait_ge(line_ready[b], s1)
                sp.sem_inc(sp_seen, 1)
                sp.dma_start(g.score_lines[:, :, bass.ds((ES - 1) * T4 * P - s * (T4 * P), T4 * P)],
                             lines[:, :, :, :].rearrange("h a t p -> h a (t p)")).then_inc(lines_stored, 16)

            for duo in (1, 0):
                store_x1(0, duo)
            with sp.Fori(0, ES - 1) as s:
                s1 = snap(sp, s + 1)
                for duo in (1, 0):
                    store_x1(s1, duo)
                store_rest(s)
            store_rest(ES - 1)
            for duo in range(2):
                sp.wait_ge(x1_stored[duo], 16 * ES)
                sp.wait_ge(h_stored[duo], 16 * ES)
            sp.wait_ge(lines_stored, 16 * ES)

        @block.gpsimd
        def _(pool):
            def lead(s, before, b):
                c = slot(b)
                pool.wait_ge(index_ready[c], snap(pool, s + 1))
                pool.wait_ge(x1_stored[c // 2], snap(pool, s * 16))
                pool.sem_inc(index_seen, 1)
                pool.indirect_dma_start(src_rows[:, c, :], None, g.x1_table,
                                        bass.IndirectOffsetOnAxis(next_src[:, c:c + 1], 0)
                                        ).then_inc(src_gathered[c], 16)
                pool.indirect_dma_start(dst_rows[:, c, :], None, g.x1_table,
                                        bass.IndirectOffsetOnAxis(next_dst[:, c:c + 1], 0)
                                        ).then_inc(dst_gathered[c], 16)

            edge_loop(pool, ES, lead)

        @block.tensor
        def _(pe):
            def lead(s, before, b):
                c = slot(b)
                s1 = snap(pe, s + 1)
                s16 = snap(pe, s * 16 + 16)
                prev, count = turn(s, b)
                pe.wait_ge(src_gathered[c], s16)
                pe.wait_ge(dst_gathered[c], s16)
                pe.wait_ge(low_ready[prev], count(s1))
                for n, rows in enumerate((src_rows, dst_rows)):
                    for k in range(KC):
                        ins = pe.transpose(turned_ps[b % 2][:, KC * n + k, :], rows[:, c, k * P:(k + 1) * P],
                                           g.ident[:, :])
                ins.then_inc(turned[c], 1)

            def tail1(s, b):
                c = slot(b)
                s1 = snap(pe, s + 1)
                prev, count = turn(s, b)
                pe.wait_ge(low_ready[c], s1)
                pe.wait_ge(h_ready[prev], count(s1))
                pe.wait_ge(raw_ready[prev], count(s1))
                for k in range(KC):
                    ins = mm3(pe, h_ps[b % 2][:, 0:D], (high[:, c, k, :], low[:, c, k, :]),
                              (g.wgat[:, 0, k, :], g.wgat[:, 1, k, :]), k == 0, k == KC - 1)
                ins.then_inc(h_done[c], 1)
                for n in range(2):
                    for k in range(KC):
                        w = [g.wat[:, part, k, n * P:(n + 1) * P] for part in range(2)]
                        ins = mm3(pe, s_ps[b % 2][:, 0:P], w, (high[:, c, KC * n + k, :], low[:, c, KC * n + k, :]),
                                  n == k == 0, n == 1 and k == KC - 1)
                ins.then_inc(s_done[c], 1)

            edge_loop(pe, ES, lead, tail1)

        @block.scalar
        def _(act):
            def lead(s, before, b):
                c = slot(b)
                act.wait_ge(turned[c], snap(act, s + 1))
                act.wait_ge(s_done[c], s)
                act.activation(high[:, c], turned_ps[b % 2][:, :, :], ACT.Copy).then_inc(high_ready[c], 1)

            def tail1(s, b):
                c = slot(b)
                s1 = snap(act, s + 1)
                act.wait_ge(h_done[c], s1)
                act.wait_ge(h_stored[c // 2], snap(act, s * 16))
                act.activation(h_rows[:, c, :], h_ps[b % 2][:, 0:D], ACT.Copy).then_inc(h_ready[c], 1)
                act.wait_ge(s_done[c], s1)
                act.wait_ge(score_ready[c], s)
                act.activation(raw[:, c, :], s_ps[b % 2][0:H, 0:P], ACT.Copy).then_inc(raw_ready[c], 1)

            edge_loop(act, ES, lead, tail1)

        @block.vector
        def _(v):
            v.memset(lines[:, :, :, :], 0.0).then_inc(first_line, 1)
            for b in range(T4):
                for to, field in ((next_src, SRC), (next_dst, DSTG)):
                    ins = v.tensor_copy(to[:, slot(b):slot(b) + 1], g.edge_fields[:, tile(0, b), field:field + 1])
                ins.then_inc(index_ready[slot(b)], 1)
            v.wait_ge(first_line, 1)

            def lead(s, before, b):
                c = slot(b)
                s1 = snap(v, s + 1)
                v.wait_ge(high_ready[c], s1)
                v.tensor_tensor(low[:, c], turned_ps[b % 2][:, :, :], high[:, c].bitcast(F32), ALU.subtract
                                ).then_inc(low_ready[c], 1)
                if isinstance(s, int) and s == ES - 1:
                    return
                for to, field in ((next_src, SRC), (next_dst, DSTG)):
                    at = (ET - T4 - 1 - b) - s * T4
                    ins = v.tensor_scalar(to[:, c:c + 1], g.edge_fields[:, bass.ds(at, 1), field], 1.0, None, ALU.mult)
                ins.then_inc(index_ready[c], 1)

            def tail1(s, b):
                c = slot(b)
                s1 = snap(v, s + 1)
                at = tile(s, b) * P + 1 if isinstance(s, int) else ((ET - 1 - b) * P + 1) - s * (T4 * P)
                v.tensor_tensor(fence[:, c, :], g.keys[0:H, bass.ds(at, P)], g.keys[0:H, bass.ds(at + 1, P)],
                                ALU.is_equal).then_inc(fence_ready[c], 1)
                v.wait_ge(fence_ready[c], s1)
                v.tensor_scalar(fence[:, c, :], fence[:, c, :], 1.0, BIG, ALU.subtract, ALU.mult
                                ).then_inc(fence_cut[c], 1)
                v.wait_ge(raw_ready[c], s1)
                v.wait_ge(lines_stored, snap(v, s * 16))
                v.scalar_tensor_tensor(out=lines[:, 0, c, :], in0=raw[:, c, :], scalar=NEG_SLOPE, in1=raw[:, c, :],
                                       op0=ALU.mult, op1=ALU.max).then_inc(score_ready[c], 1)
                v.wait_ge(fence_cut[c], s1)
                v.wait_ge(score_ready[c], s1)
                prev = slot((b - 1) % T4)
                v.wait_ge(line_ready[prev], s1 if b else s)
                v.tensor_tensor_scan(lines[:, 1, c, ::-1], fence[:, c, ::-1], lines[:, 0, c, ::-1],
                                     lines[:, 1, prev, 0:1], ALU.add, ALU.max).then_inc(line_ready[c], 1)

            edge_loop(v, ES, lead, tail1)


def gat_sum(nc, g):
    ES = g.ES
    W = D + H
    with ExitStack() as ctx:
        m = Memory(nc, ctx, "gat")
        e = EdgeSum(m, g, None, None, None, width=W)
        lines = m.sb("lines", [H, 2, T8 * P])
        fence = m.sb("fence", [H, T8 * P])
        top = m.sb("top", [H, T8 * P])
        diff = m.sb("diff", [H, T8 * P])
        prob = m.sb("prob", [H, T8 * P])
        prob_ps = m.ps("prob", [P, 512])
        probs = m.sb("probs", [P, T8, H])
        h_rows = m.sb("h_rows", [P, T8, D])
        x1 = m.sb("x1", [P, T8, D])
        den = m.sb("den", [P, MS, 2, H])
        mean = m.sb("mean", [P, MS, D])
        res = m.sb("res", [P, T8, D])
        stats = m.sb("stats", [P, MS, 6])
        moments = m.sb("moments", [P, MS, 2])
        dev = m.sb("dev", [P, MS, 2])
        lines_loaded = m.sem("lines_loaded")
        fence_ready = m.sem("fence_ready")
        fence_cut = m.sem("fence_cut")
        top_ready = m.sem("top_ready")
        diff_ready = m.sem("diff_ready")
        exp_ready = m.sem("exp_ready")
        prob_turned = m.sem("prob_turned")
        probs_ready = m.sem("probs_ready")
        h_loaded = m.sems("h_loaded", T8 // 2)
        x1_loaded = m.sems("x1_loaded", T8 // 2)
        den_ready = m.sems("den_ready", MS)
        rden_ready = m.sems("rden_ready", MS)
        mean_ready = m.sems("mean_ready", MS)
        sum_ready = m.sems("sum_ready", MS)
        stats_ready = m.sems("stats_ready", MS)
        stats_seen = m.sem("stats_seen")
        var_ready = m.sems("var_ready", MS)
        std_ready = m.sems("std_ready", MS)
        rstd_ready = m.sems("rstd_ready", MS)
        norm_seen = m.sem("norm_seen")
        res_ready = m.sems("res_ready", MS)
        stored = m.sems("stored", T8 // 2)
        sp_seen = m.sem("sp_seen")
        pe_seen = m.sem("pe_seen")
        block = ctx.enter_context(nc.Block())

        @block.sync
        def _(sp):
            def load_lines(t):
                if t.b != 0:
                    return
                sp.wait_ge(diff_ready, t.s)
                sp.sem_inc(sp_seen, 1)
                sp.dma_start(lines[:, :, :], g.score_lines[:, :, bass.ds(t.at(P), T8 * P)]).then_inc(lines_loaded, 16)

            def load_h(t):
                if t.b % 2:
                    return
                for last in (t.back(T8), t.back(T8 - 1)):
                    sp.wait_ge(e.gathered[last.m], last.now)
                sp.sem_inc(sp_seen, 1)
                sp.dma_start(h_rows[:, t.b:t.b + 2, :], slot_rows(g.h_slots, 0, t.s, t.duo, T8)
                             ).then_inc(h_loaded[t.duo], 16)

            def load_x1(t):
                if t.b % 2:
                    return
                for last in (t.back(T8), t.back(T8 - 1)):
                    sp.wait_ge(sum_ready[last.m], last.now)
                sp.sem_inc(sp_seen, 1)
                sp.dma_start(x1[:, t.b:t.b + 2, :], slot_rows(g.x1_slots, 0, t.s, t.duo, T8)
                             ).then_inc(x1_loaded[t.duo], 16)

            def store(t):
                if t.b % 2 == 0:
                    return
                for done in (t.back(1), t):
                    sp.wait_ge(res_ready[done.m], done.now)
                sp.sem_inc(sp_seen, 1)
                sp.dma_start(slot_rows(g.x2_table, g.N, t.s, t.duo, T8), res[:, t.b - 1:t.b + 1, :]
                             ).then_inc(stored[t.duo], 16)

            tile_loop(sp, ES, [(0, load_lines), (2, load_h), (4, load_x1), (16, store)], dma=False)
            for duo in range(T8 // 2):
                sp.wait_ge(stored[duo], 16 * ES)

        @block.tensor
        def _(pe):
            def turn_probs(t):
                if t.b != T8 - 1:
                    return
                pe.wait_ge(exp_ready, t.s1)
                pe.wait_ge(probs_ready, t.s)
                pe.sem_inc(pe_seen, 1)
                for b in range(T8):
                    ins = pe.transpose(prob_ps[:, b * H:(b + 1) * H], prob[:, b * P:(b + 1) * P], g.ident[0:H, 0:H])
                ins.then_inc(prob_turned, 1)

            tile_loop(pe, ES, [(11, lambda t: e.pe_sum(pe, t)), (0, turn_probs)], dma=False)

        @block.scalar
        def _(act):
            def exps(t):
                if t.b != T8 - 2:
                    return
                act.wait_ge(diff_ready, t.s1)
                act.wait_ge(prob_turned, t.s)
                act.activation(prob[:, :], diff[:, :], ACT.Exp).then_inc(exp_ready, 1)

            def keep_probs(t):
                if t.b != 0:
                    return
                act.wait_ge(prob_turned, t.s1)
                act.wait_ge(e.gathered[t.back(1).m], t.back(1).now)
                act.activation(probs[:, :, :], prob_ps[:, 0:T8 * H].rearrange("p (b h) -> p b h", h=H), ACT.Copy
                               ).then_inc(probs_ready, 1)

            def evacuate(t):
                act.wait_ge(mean_ready[t.m], t.back(T8).now)
                e.act_evacuate(act, t)

            def root(t):
                act.wait_ge(var_ready[t.m], t.now)
                act.activation(dev[:, t.m, 0:1], moments[:, t.m, 1:2], ACT.Sqrt, bias=g.ln_eps[:, :]
                               ).then_inc(std_ready[t.m], 1)

            tile_loop(act, ES, [(13, root), (8, keep_probs), (10, lambda t: e.act_high(act, t)), (11, evacuate),
                                (0, exps)], dma=False)

        @block.vector
        def _(v):
            e.first(v)
            v.memset(top[:, :], 0.0).then_inc(fence_cut, 1)

            def scores(t):
                if t.b == 0:
                    v.wait_ge(top_ready, t.s)
                    v.tensor_tensor(fence[:, :], g.keys[0:H, bass.ds(t.at(P) + 1, T8 * P)],
                                    g.keys[0:H, bass.ds(t.at(P), T8 * P)], ALU.is_equal).then_inc(fence_ready, 1)
                elif t.b == 1:
                    v.wait_ge(fence_ready, t.s1)
                    v.tensor_scalar(fence[:, :], fence[:, :], 1.0, BIG, ALU.subtract, ALU.mult
                                    ).then_inc(fence_cut, 1)
                elif t.b == 3:
                    v.wait_ge(lines_loaded, t.d17)
                    v.wait_ge(fence_cut, t.s2)
                    v.wait_ge(top_ready, t.s)
                    v.tensor_tensor_scan(top[:, :], fence[:, :], lines[:, 1, :], top[:, T8 * P - 1:T8 * P],
                                         ALU.add, ALU.max).then_inc(top_ready, 1)
                elif t.b == 5:
                    v.wait_ge(top_ready, t.s1)
                    v.wait_ge(exp_ready, t.s)
                    v.tensor_tensor(diff[:, :], lines[:, 0, :], top[:, :], ALU.subtract).then_inc(diff_ready, 1)

            def fields(t):
                if t.m == 0:
                    e.vec_here(v, t)

            def weigh(t):
                if t.b == 0:
                    v.wait_ge(probs_ready, t.s1)
                v.wait_ge(h_loaded[t.duo], t.d17)
                v.wait_ge(e.low_ready[t.m], t.back(T8).now)
                p = probs[:, t.b, :]
                v.tensor_tensor(e.rows[:, t.b, 0:D].rearrange("p (h f) -> p h f", h=H),
                                h_rows[:, t.b, :].rearrange("p (h f) -> p h f", h=H),
                                p.unsqueeze(2).broadcast_to([P, H, DH]), ALU.mult)
                v.tensor_copy(e.rows[:, t.b, D:W], p).then_inc(e.gathered[t.m], 1)

            def divide(t):
                v.wait_ge(e.summed_ready[t.m], t.now)
                v.wait_ge(rden_ready[t.m], t.back(MS).now)
                v.tensor_scalar(den[:, t.m, 0, :], e.summed[:, t.b, D:W], GAT_EPS, None, ALU.add
                                ).then_inc(den_ready[t.m], 1)

            def invert_weights(t):
                v.wait_ge(den_ready[t.m], t.now)
                v.reciprocal(den[:, t.m, 1, :], den[:, t.m, 0, :]).then_inc(rden_ready[t.m], 1)

            def average(t):
                v.wait_ge(rden_ready[t.m], t.now)
                v.wait_ge(res_ready[t.m], t.back(MS).now)
                v.tensor_tensor(mean[:, t.m, :].rearrange("p (h f) -> p h f", h=H),
                                e.summed[:, t.b, 0:D].rearrange("p (h f) -> p h f", h=H),
                                den[:, t.m, 1, :].unsqueeze(2).broadcast_to([P, H, DH]), ALU.mult
                                ).then_inc(mean_ready[t.m], 1)

            def add_x1(t):
                v.wait_ge(mean_ready[t.m], t.now)
                v.wait_ge(x1_loaded[t.duo], t.d17)
                v.tensor_tensor(mean[:, t.m, :], mean[:, t.m, :], x1[:, t.b, :], ALU.add).then_inc(sum_ready[t.m], 1)

            def row_stats(t):
                v.wait_ge(sum_ready[t.m], t.now)
                v.bn_stats(stats[:, t.m, :], mean[:, t.m, :]).then_inc(stats_ready[t.m], 1)

            def row_moments(t):
                v.wait_ge(stats_ready[t.m], t.now)
                v.sem_inc(stats_seen, 1)
                v.bn_aggr(moments[:, t.m, :], stats[:, t.m, :]).then_inc(var_ready[t.m], 1)

            def invert(t):
                v.wait_ge(std_ready[t.m], t.now)
                v.reciprocal(dev[:, t.m, 1:2], dev[:, t.m, 0:1]).then_inc(rstd_ready[t.m], 1)

            tile_loop(v, ES, [(12, divide), (9, weigh), (12, invert_weights), (9, fields), (12, average),
                              (13, invert), (9, lambda t: e.vec_matrices(v, t)), (12, add_x1), (12, row_stats),
                              (10, lambda t: e.vec_low(v, t)), (12, row_moments), (0, scores)])

        @block.gpsimd
        def _(pool):
            def norm(t):
                pool.wait_ge(rstd_ready[t.m], t.now)
                pool.wait_ge(stored[t.duo], t.d16)
                pool.sem_inc(norm_seen, 1)
                pool.tensor_scalar(res[:, t.b, :], mean[:, t.m, :], moments[:, t.m, 0:1], dev[:, t.m, 1:2],
                                   ALU.subtract, ALU.mult).then_inc(res_ready[t.m], 1)

            tile_loop(pool, ES, [(13, norm)])




class Step:

    def __init__(self, eng, g, i, h, par, loop):
        self.i, self.par, self.blocks = i, par, g.NBLK
        last = not loop and i == g.NBLK - 1
        self.parts, self.rows = g.tail if last else (P, R4)
        self.cols = self.parts * self.rows
        self.n, self.n1 = i, snap(eng, i + 1)
        self.h, self.h1 = h, snap(eng, h + 1)
        self.h16, self.h17 = snap(eng, h * 16), snap(eng, h * 16 + 16)

    def nodes(self, table):
        rows = table[bass.ds(self.i * BLOCK, self.cols), :]
        return rows.rearrange("(p r) f -> p r f", p=self.parts)


def block_loop(eng, g, stages):
    lags = [lag for lag, _ in stages]
    most, least = max(lags), min(lags)

    def step(q, c):
        loop = not isinstance(q, int)
        for lag, stage in stages:
            k = c - lag
            i, h = q * 2 + k, q + k // 2
            if loop or 0 <= i < g.NBLK:
                stage(Step(eng, g, i if not loop else eng.snap(i), h if not loop else eng.snap(h), k % 2, loop))

    q0 = (most + 3) // 2
    q1 = (g.NBLK - 2 + least + 1) // 2
    for q in range(q0):
        step(q, 0)
        step(q, 1)
    with eng.Fori(q0, q1) as q:
        step(q, 0)
        step(q, 1)
    q = q1
    while 2 * q <= g.NBLK - 1 + most:
        step(q, 0)
        step(q, 1)
        q += 1


def later(v, k):
    if isinstance(v, int):
        return v + k if v + k > 0 else None
    return v + k


def upto(eng, t, k):
    return min(t.n + k, t.blocks) if isinstance(t.n, int) else snap(eng, t.n + k)


def gin_hidden(nc, g):
    NCH = 2 * D // P
    with ExitStack() as ctx:
        m = Memory(nc, ctx, "gin")
        x = m.sb("x", [P, 2, R4, D])
        agg = m.sb("agg", [P, 2, R4, D])
        xin = m.sb("xin", [P, 2, R4, D])
        x_high = m.sb("x_high", [P, KC, BLOCK], F32R)
        x_low = m.sb("x_low", [P, KC, BLOCK], F32R)
        hid = m.sb("hid", [P, 2, BLOCK])
        hid_high = m.sb("hid_high", [P, NCH, BLOCK], F32R)
        hid_low = m.sb("hid_low", [P, NCH, BLOCK], F32R)
        y = m.sb("y", [P, 2, KC, BLOCK])
        map_index = m.sb("map_index", [P, T4], I32)
        map_rows = m.sb("map_rows", [P, T4, 4])
        x_ps = m.ps("x", [P, KC, BLOCK])
        hid_ps = m.ps("hid", [P, NCH, BLOCK])
        y_ps = m.ps("y", [P, KC, BLOCK])
        x_loaded = m.sems("x_loaded", 2)
        agg_loaded = m.sems("agg_loaded", 2)
        xin_ready = m.sems("xin_ready", 2)
        turned = m.sem("turned")
        x_high_ready = m.sem("x_high_ready")
        x_low_ready = m.sem("x_low_ready")
        hid_done = m.sems("hid_done", NCH)
        hid_ready = m.sems("hid_ready", NCH)
        hid_high_ready = m.sems("hid_high_ready", NCH)
        hid_low_ready = m.sems("hid_low_ready", NCH)
        y_done = m.sem("y_done")
        y_ready = m.sem("y_ready")
        y_stored = m.sems("y_stored", 2)
        stats_seen = m.sem("stats_seen")
        stats_done = m.sem("stats_done")
        map_staged = m.sem("map_staged")
        map_seen = m.sem("map_seen")
        map_written = m.sems("map_written", T4)
        map_read = m.sems("map_read", T4)
        map_kept = m.sem("map_kept")
        sp_seen = m.sem("sp_seen")
        block = ctx.enter_context(nc.Block())

        @block.sync
        def _(sp):
            def load(t):
                sp.wait_ge(xin_ready[t.par], t.h)
                sp.sem_inc(sp_seen, 1)
                sp.dma_start(x[0:t.parts, t.par, 0:t.rows, :], t.nodes(g.x)).then_inc(x_loaded[t.par], 16)
                sp.dma_start(agg[0:t.parts, t.par, 0:t.rows, :], t.nodes(g.agg_table)).then_inc(agg_loaded[t.par], 16)

            def store(t):
                sp.wait_ge(y_ready, t.n1)
                sp.sem_inc(sp_seen, 1)
                sp.dma_start(g.y_table[bass.ds(t.i * P, P), :].rearrange("p (k c) -> p k c", k=KC)[:, :, 0:t.cols],
                             y[:, t.par, :, 0:t.cols]).then_inc(y_stored[t.par], 16)

            block_loop(sp, g, [(0, load), (2, store)])
            for par in range(2):
                sp.wait_ge(y_stored[par], 16 * ((g.NBLK + 1 - par) // 2))

        @block.gpsimd
        def _(pool):
            limit = pool.alloc_register("map_limit")
            pool.reg_mov(limit, g.N - 1)
            with pool.Fori(0, g.ET // T4) as s:
                s1, s17 = pool.snap(s + 1), pool.snap(s * 16 + 16)
                pool.tensor_copy(map_index[:, :], g.edge_fields[:, bass.ds(s * T4, T4), SCAT])
                pool.tensor_copy(map_rows[:, :, :], g.slot_info[:, bass.ds(s * T4, T4), :]).then_inc(map_staged, 1)
                pool.wait_ge(map_staged, s1)
                pool.sem_inc(map_seen, 1)
                for b in range(T4):
                    pool.indirect_dma_start(g.node_table, bass.IndirectOffsetOnAxis(map_index[:, b:b + 1], 0),
                                            map_rows[:, b, :], None, bounds_check=limit, oob_is_err=False
                                            ).then_inc(map_written[b], 16)
                for b in range(T4):
                    pool.wait_ge(map_written[b], s17)
                pool.sem_inc(map_seen, 1)
            with pool.Fori(0, g.ET // T4) as s:
                s17 = pool.snap(s * 16 + 16)
                s1n = pool.snap(s + (g.ET // T4 + 1))
                pool.tensor_copy(map_index[:, :], g.edge_fields[:, bass.ds(s * T4, T4), SRC]).then_inc(map_staged, 1)
                pool.wait_ge(map_staged, s1n)
                pool.sem_inc(map_seen, 1)
                for b in range(T4):
                    pool.indirect_dma_start(map_rows[:, b, :], None, g.node_table,
                                            bass.IndirectOffsetOnAxis(map_index[:, b:b + 1], 0)
                                            ).then_inc(map_read[b], 16)
                for b in range(T4):
                    pool.wait_ge(map_read[b], s17)
                pool.sem_inc(map_seen, 1)
                pool.tensor_copy(g.src_info[:, bass.ds(s * T4, T4), :], map_rows[:, :, :]).then_inc(map_kept, 1)

        @block.vector
        def _(v):
            def prepare(t):
                v.wait_ge(x_loaded[t.par], t.h17)
                v.wait_ge(agg_loaded[t.par], t.h17)
                if (n := later(t.n, -1)) is not None:
                    v.wait_ge(turned, snap(v, n))
                v.scalar_tensor_tensor(out=xin[0:t.parts, t.par, 0:t.rows, :], in0=x[0:t.parts, t.par, 0:t.rows, :],
                                       scalar=g.eps1[0:t.parts, :], in1=agg[0:t.parts, t.par, 0:t.rows, :],
                                       op0=ALU.mult, op1=ALU.add).then_inc(xin_ready[t.par], 1)

            def hidden(t):
                for c in range(NCH):
                    v.wait_ge(hid_high_ready[c], t.n1)
                    v.tensor_tensor(hid_low[:, c, 0:t.cols], hid[:, c % 2, 0:t.cols],
                                    hid_high[:, c, 0:t.cols].bitcast(F32), ALU.subtract).then_inc(hid_low_ready[c], 1)

            def turned_low(t):
                v.wait_ge(x_high_ready, t.n1)
                v.tensor_tensor(x_low[:, :, 0:t.cols], x_ps[:, :, 0:t.cols], x_high[:, :, 0:t.cols].bitcast(F32),
                                ALU.subtract).then_inc(x_low_ready, 1)

            def moments(t):
                v.wait_ge(y_ready, t.n1)
                v.sem_inc(stats_seen, 1)
                for f in range(KC):
                    ins = v.bn_stats(g.bn_stats[:, f, bass.ds(t.i, 1), :].rearrange("p a c -> p (a c)"),
                                     y[:, t.par, f, 0:t.cols])
                ins.then_inc(stats_done, 1)

            block_loop(v, g, [(0, prepare), (1, hidden), (0, turned_low), (1, moments)])

        @block.scalar
        def _(act):
            def hidden(t):
                for c in range(NCH + 1):
                    if c < NCH:
                        act.wait_ge(hid_done[c], t.n1)
                        act.wait_ge(hid_low_ready[(c - 2) % NCH], t.n if c < 2 else t.n1)
                        act.activation(hid[:, c % 2, 0:t.cols], hid_ps[:, c, 0:t.cols], ACT.Relu,
                                       bias=g.b1_col[:, c:c + 1]).then_inc(hid_ready[c], 1)
                    if c > 0:
                        act.wait_ge(hid_ready[c - 1], t.n1)
                        if c == 1:
                            act.wait_ge(y_done, t.n)
                        act.activation(hid_high[:, c - 1, 0:t.cols], hid[:, (c - 1) % 2, 0:t.cols], ACT.Copy
                                       ).then_inc(hid_high_ready[c - 1], 1)

            def turned_high(t):
                act.wait_ge(turned, t.n1)
                act.wait_ge(hid_done[NCH - 1], t.n)
                act.activation(x_high[:, :, 0:t.cols], x_ps[:, :, 0:t.cols], ACT.Copy).then_inc(x_high_ready, 1)

            def evacuate(t):
                act.wait_ge(y_done, t.n1)
                act.wait_ge(y_stored[t.par], t.h16)
                if (n := later(t.n, -1)) is not None:
                    act.wait_ge(stats_done, snap(act, n))
                for f in range(KC):
                    ins = act.activation(y[:, t.par, f, 0:t.cols], y_ps[:, f, 0:t.cols], ACT.Identity,
                                         bias=g.b2_col[:, f:f + 1])
                ins.then_inc(y_ready, 1)

            block_loop(act, g, [(1, hidden), (0, turned_high), (1, evacuate)])

        @block.tensor
        def _(pe):
            def first(t):
                pe.wait_ge(x_low_ready, t.n1)
                for c in range(NCH):
                    pe.wait_ge(hid_ready[c], t.n)
                    for k in range(KC):
                        ins = mm3(pe, hid_ps[:, c, 0:t.cols],
                                  [g.w1[:, part, k, c * P:(c + 1) * P] for part in range(2)],
                                  (x_high[:, k, 0:t.cols], x_low[:, k, 0:t.cols]), k == 0, k == KC - 1)
                    ins.then_inc(hid_done[c], 1)

            def turn(t):
                pe.wait_ge(xin_ready[t.par], t.h1)
                pe.wait_ge(x_low_ready, t.n)
                for k in range(KC):
                    for r in range(t.rows):
                        ins = pe.transpose(x_ps[:, k, r * t.parts:(r + 1) * t.parts],
                                           xin[0:t.parts, t.par, r, k * P:(k + 1) * P], g.ident[0:t.parts, 0:t.parts])
                ins.then_inc(turned, 1)

            def second(t):
                for c in range(NCH):
                    pe.wait_ge(hid_low_ready[c], t.n1)
                    if c == 0:
                        pe.wait_ge(y_ready, t.n)
                    for f in range(KC):
                        ins = mm3(pe, y_ps[:, f, 0:t.cols],
                                  [g.w2[:, part, c, f * P:(f + 1) * P] for part in range(2)],
                                  (hid_high[:, c, 0:t.cols], hid_low[:, c, 0:t.cols]), c == 0, c == NCH - 1)
                ins.then_inc(y_done, 1)

            block_loop(pe, g, [(1, first), (0, turn), (1, second)])


def norm_and_fields(nc, g):
    ET = g.ET
    with ExitStack() as ctx:
        m = Memory(nc, ctx, "fin")
        mom = m.sb("mom", [P, KC, 2])
        tmp = m.sb("tmp", [P, KC, 2])
        bn_eps = m.sb("bn_eps", [P, 1])
        step = m.sem("step")
        var_ready = m.sem("var_ready")
        std_ready = m.sem("std_ready")
        block = ctx.enter_context(nc.Block())

        @block.scalar
        def _(act):
            act.wait_ge(var_ready, 1)
            act.activation(tmp[:, :, 0], mom[:, :, 1], ACT.Sqrt, bias=bn_eps[:, :]).then_inc(std_ready, 1)

        @block.vector
        def _(v):
            linked = 0

            def link(ins):
                nonlocal linked
                ins.then_inc(step, 1)
                linked += 1
                v.wait_ge(step, linked)

            link(v.memset(bn_eps[:, :], BN_EPS))
            for f in range(KC):
                ins = v.bn_aggr(mom[:, f, :], g.bn_stats[:, f, :, :].rearrange("p n c -> p (n c)"))
            ins.then_inc(var_ready, 1)
            fields = g.edge_fields

            def f(c):
                return fields[:, 0:ET, c]

            dinv, dis = g.slot_info[:, :, 1], g.slot_info[:, :, 2]
            link(v.tensor_copy(f(ROW), g.src_info[:, :, 0:1].bitcast(I32).rearrange("p t c -> p (t c)")))
            link(v.tensor_scalar(f(ROW_H), f(ROW), float(g.N), float(g.EP), ALU.is_ge, ALU.mult))
            link(v.tensor_tensor(f(ROW_H), f(ROW_H), f(ROW), ALU.add))
            link(v.tensor_tensor(f(C_APPNP), f(EW), g.src_info[:, :, 1], ALU.mult))
            link(v.tensor_copy(f(C_GCN), g.src_info[:, :, 2]))
            link(v.tensor_scalar(f(D_HALF), dinv, 0.5, None, ALU.mult))
            link(v.tensor_tensor(f(D_HALF2), f(D_HALF), dinv, ALU.mult))
            link(v.tensor_scalar(f(D_KEEP), f(D_HALF2), 0.5, None, ALU.add))
            link(v.tensor_copy(f(DIS), dis))
            link(v.tensor_tensor(f(DIS2), dis, dis, ALU.mult))
            v.wait_ge(std_ready, 1)
            link(v.reciprocal(tmp[:, :, 1], tmp[:, :, 0]))
            link(v.tensor_tensor(g.bn_scale[:, :], g.gamma_col[:, :], tmp[:, :, 1], ALU.mult))
            link(v.tensor_tensor(tmp[:, :, 0], mom[:, :, 0], g.bn_scale[:, :], ALU.mult))
            link(v.tensor_tensor(g.bn_shift[:, :], g.beta_col[:, :], tmp[:, :, 0], ALU.subtract))


def degrees(nc, g):
    ET = g.ET
    with ExitStack() as ctx:
        m = Memory(nc, ctx, "deg")
        deg = m.sb("deg", [P, 2, ET])
        held = m.sb("held", [P, 2, ET])
        pos = m.sb("pos", [P, 2, ET])
        zero = m.sb("zero", [P, 1])
        step = m.sem("step")
        held_ready = m.sem("held_ready")
        root_ready = m.sem("root_ready")
        block = ctx.enter_context(nc.Block())

        @block.scalar
        def _(act):
            act.wait_ge(held_ready, 1)
            act.activation(deg[:, :, :], held[:, :, :], ACT.Sqrt, bias=zero[:, :]).then_inc(root_ready, 1)

        @block.vector
        def _(v):
            linked = 0

            def link(ins):
                nonlocal linked
                ins.then_inc(step, 1)
                linked += 1
                v.wait_ge(step, linked)

            link(v.memset(zero[:, :], 0.0))
            link(v.scalar_tensor_tensor(out=deg[:, 0, :], in0=g.deg[:, :, 0], scalar=1.0, in1=g.deg[:, :, 1],
                                        op0=ALU.add, op1=ALU.add))
            link(v.tensor_scalar(deg[:, 1, :], g.deg[:, :, 2], 1.0, None, ALU.add))
            link(v.tensor_scalar(pos[:, :, :], deg[:, :, :], 0.0, None, ALU.is_gt))
            v.tensor_scalar(held[:, :, :], deg[:, :, :], 1e-12, None, ALU.max).then_inc(held_ready, 1)
            v.wait_ge(root_ready, 1)
            link(v.reciprocal(held[:, :, :], deg[:, :, :]))
            link(v.tensor_tensor(g.slot_info[:, :, 1], held[:, 0, :], pos[:, 0, :], ALU.mult))
            link(v.tensor_tensor(g.slot_info[:, :, 2], held[:, 1, :], pos[:, 1, :], ALU.mult))
            link(v.tensor_copy(g.slot_info[:, :, 0:1].bitcast(I32).rearrange("p t c -> p (t c)"), g.slot_row[:, :]))
            link(v.memset(g.slot_info[:, :, 3:4], 0.0))


def dense_layers(nc, g):
    with ExitStack() as ctx:
        m = Memory(nc, ctx, "dense")
        y = m.sb("y", [P, 2, KC, BLOCK])
        x = m.sb("x", [P, 2, R4, D])
        z = m.sb("z", [P, KC, BLOCK])
        raw = [m.sb(f"raw{n}", [P, R4, D]) for n in range(3)]
        rows1 = m.sb("rows1", [P, 2, R4, D])
        rows2 = m.sb("rows2", [P, 2, R4, D])
        rows3 = m.sb("rows3", [P, 2, R4, D])
        rows_y = m.sb("rows_y", [P, 2, R4, D])
        rows4 = m.sb("rows4", [P, 2, R4, D])
        high = [m.sb(f"high{n}", [P, KC, BLOCK], F32R) for n in range(3)]
        low = [m.sb(f"low{n}", [P, KC, BLOCK], F32R) for n in range(3)]
        gcn = m.sb("gcn", [P, KC, BLOCK])
        stats = m.sb("stats", [P, 4, R4, 6])
        mom = m.sb("mom", [P, 4, R4, 2])
        dev = m.sb("dev", [P, 4, 2, R4])
        shift = m.sb("shift", [P, 4, R4])
        dev12 = m.sb("dev12", [P, 2, 2, R4])
        turned_ps = m.ps("turned", [P, KC, BLOCK])
        layer_ps = m.ps("layer", [P, 2, 512])
        rows_ps = m.ps("rows", [P, R4, D])
        last_ps = m.ps("last", [P, R4, D])
        y_loaded = m.sems("y_loaded", 2)
        x_loaded = m.sems("x_loaded", 2)
        z_ready = m.sem("z_ready")
        z_turned = m.sem("z_turned")
        raw_ready = m.sems("raw_ready", 4)
        inverted = m.sems("inverted", 4)
        stats_ready = m.sems("stats_ready", 4)
        stats_seen = m.sem("stats_seen")
        var_ready = m.sems("var_ready", 4)
        std_ready = m.sems("std_ready", 4)
        rstd_ready = m.sems("rstd_ready", 4)
        norm_seen = m.sem("norm_seen")
        normed = m.sems("normed", 4)
        turned = m.sems("turned", 2)
        high_ready = m.sems("high_ready", 3)
        low_ready = m.sems("low_ready", 3)
        appnp_done = m.sem("appnp_done")
        gcn_done = m.sem("gcn_done")
        gcn_ready = m.sem("gcn_ready")
        gcn_turned = m.sem("gcn_turned")
        rows_y_ready = m.sem("rows_y_ready")
        half_normed = m.sem("half_normed")
        last_done = m.sem("last_done")
        stored = [m.sems(f"stored{n}_", 2) for n in range(5)]
        sp_seen = m.sem("sp_seen")
        block = ctx.enter_context(nc.Block())

        @block.sync
        def _(sp):
            def load(t):
                n = later(t.n, -1)
                if n is not None:
                    n = snap(sp, n)
                    sp.wait_ge(z_ready, n)
                    sp.sem_inc(sp_seen, 1)
                sp.dma_start(y[:, t.par, :, 0:t.cols],
                             g.y_table[bass.ds(t.i * P, P), :].rearrange("p (k c) -> p k c", k=KC)[:, :, 0:t.cols]
                             ).then_inc(y_loaded[t.par], 16)
                if n is not None:
                    sp.wait_ge(raw_ready[0], n)
                    sp.sem_inc(sp_seen, 1)
                sp.dma_start(x[0:t.parts, t.par, 0:t.rows, :], t.nodes(g.x)).then_inc(x_loaded[t.par], 16)

            def store(n, rows, table, ready, also=None):
                def one(t):
                    sp.wait_ge(ready, t.n1)
                    if also is not None:
                        sp.wait_ge(also, t.n1)
                    sp.sem_inc(sp_seen, 1)
                    sp.dma_start(t.nodes(table), rows[0:t.parts, t.par, 0:t.rows, :]).then_inc(stored[n][t.par], 16)
                return one

            block_loop(sp, g, [(0, load), (2, store(0, rows1, g.x1_table, normed[0])),
                               (2, store(1, rows2, g.x2_table, normed[1])),
                               (4, store(2, rows3, g.x3_table, normed[2])),
                               (5, store(3, rows_y, g.y1_table, rows_y_ready)),
                               (6, store(4, rows4, g.out, normed[3], half_normed))])
            for n in range(5):
                for par in range(2):
                    sp.wait_ge(stored[n][par], 16 * ((g.NBLK + 1 - par) // 2))

        @block.tensor
        def _(pe):
            def turn_rows(t, rows):
                for k in range(KC):
                    for r in range(t.rows):
                        ins = pe.transpose(turned_ps[:, k, r * t.parts:(r + 1) * t.parts],
                                           rows[0:t.parts, t.par, r, k * P:(k + 1) * P], g.ident[0:t.parts, 0:t.parts])
                return ins

            def turn_features(t, cols):
                for r in range(t.rows):
                    for k in range(KC):
                        ins = pe.transpose(rows_ps[0:t.parts, r, k * P:(k + 1) * P],
                                           cols[:, k, r * t.parts:(r + 1) * t.parts], g.ident[:, :])
                return ins

            def to_rows(t, out, part, weights, bias):
                for r in range(t.rows):
                    span = slice(r * t.parts, (r + 1) * t.parts)
                    pe.matmul(out[0:t.parts, r, :], g.sel01[:, 0:t.parts], g.bias_rows[:, bias, :],
                              start=True, stop=False, skip_group_check=True)
                    for k in range(KC):
                        ins = mm3(pe, out[0:t.parts, r, :], (high[part][:, k, span], low[part][:, k, span]),
                                  (weights[:, 0, k, :], weights[:, 1, k, :]), False, k == KC - 1)
                return ins

            def last_product(t):
                pe.wait_ge(low_ready[2], t.n1)
                pe.wait_ge(raw_ready[3], t.n)
                to_rows(t, last_ps, 2, g.ws1, 2).then_inc(last_done, 1)

            def turn_rows3(t):
                pe.wait_ge(normed[2], t.n1)
                pe.wait_ge(low_ready[0], upto(pe, t, 2))
                turn_rows(t, rows3).then_inc(turned[1], 1)

            def turn_rows2(t):
                pe.wait_ge(normed[1], t.n1)
                if (n := later(t.n, -1)) is not None:
                    pe.wait_ge(low_ready[1], snap(pe, n))
                turn_rows(t, rows2).then_inc(turned[0], 1)

            def gcn_product(t):
                pe.wait_ge(low_ready[1], t.n1)
                pe.wait_ge(raw_ready[2], upto(pe, t, 2))
                for n in range(KC):
                    for k in range(KC):
                        ins = mm3(pe, layer_ps[:, n, 0:t.cols],
                                  [g.ws0[:, part, k, n * P:(n + 1) * P] for part in range(2)],
                                  (high[1][:, k, 0:t.cols], low[1][:, k, 0:t.cols]), k == 0, k == KC - 1)
                ins.then_inc(gcn_done, 1)

            def turn_z(t):
                pe.wait_ge(z_ready, t.n1)
                if (n := later(t.n, -4)) is not None:
                    pe.wait_ge(rows_y_ready, snap(pe, n))
                turn_features(t, z).then_inc(z_turned, 1)

            def appnp_product(t):
                pe.wait_ge(low_ready[0], t.n1)
                if (n := later(t.n, -1)) is not None:
                    pe.wait_ge(gcn_ready, snap(pe, n))
                layer = layer_ps[:, :, :].rearrange("p a (b n) -> p (a b) n", n=D)
                to_rows(t, layer, 0, g.wl2, 0).then_inc(appnp_done, 1)

            def turn_gcn(t):
                pe.wait_ge(gcn_ready, t.n1)
                pe.wait_ge(raw_ready[0], upto(pe, t, 5))
                turn_features(t, gcn).then_inc(gcn_turned, 1)

            block_loop(pe, g, [(4, turn_rows3), (5, last_product), (2, turn_rows2), (4, gcn_product), (0, turn_z),
                               (2, appnp_product), (4, turn_gcn)])

        @block.scalar
        def _(act):
            def root(t, n, out, scale=1.0, bias=g.ln_eps):
                return act.activation(out, mom[0:t.parts, n, 0:t.rows, 1], ACT.Sqrt, bias=bias[0:t.parts, :],
                                      scale=scale)

            def roots12(t):
                act.wait_ge(var_ready[0], t.n1)
                root(t, 0, dev12[0:t.parts, 0, 0, 0:t.rows])
                root(t, 0, dev12[0:t.parts, 0, 1, 0:t.rows], 1.0 + LN_EPS, g.ln_eps2).then_inc(std_ready[0], 1)

            def root_of(n):
                def one(t):
                    act.wait_ge(var_ready[n], t.n1)
                    root(t, n, dev[0:t.parts, n, 0, 0:t.rows]).then_inc(std_ready[n], 1)
                return one

            def norm1(t):
                act.wait_ge(rstd_ready[0], t.n1)
                act.wait_ge(stored[0][t.par], t.h16)
                for r in range(t.rows):
                    ins = act.activation(rows1[0:t.parts, t.par, r, :], raw[0][0:t.parts, r, :], ACT.Identity,
                                         scale=dev12[0:t.parts, 1, 0, r:r + 1], bias=shift[0:t.parts, 0, r:r + 1])
                ins.then_inc(normed[0], 1)

            def norm3(t):
                act.wait_ge(rstd_ready[2], t.n1)
                act.wait_ge(stored[2][t.par], t.h16)
                if (n := later(t.n, -1)) is not None:
                    act.wait_ge(raw_ready[3], snap(act, n))
                for r in range(t.rows):
                    ins = act.activation(rows3[0:t.parts, t.par, r, :], raw[1][0:t.parts, r, :], ACT.Identity,
                                         scale=dev[0:t.parts, 2, 1, r:r + 1], bias=shift[0:t.parts, 2, r:r + 1])
                ins.then_inc(normed[2], 1)

            def high_rows3(t):
                act.wait_ge(turned[1], t.n1)
                act.wait_ge(gcn_done, t.n)
                act.activation(high[1][:, :, 0:t.cols], turned_ps[:, :, 0:t.cols], ACT.Copy).then_inc(high_ready[1], 1)

            def high_rows2(t):
                act.wait_ge(turned[0], t.n1)
                act.wait_ge(appnp_done, t.n)
                act.activation(high[0][:, :, 0:t.cols], turned_ps[:, :, 0:t.cols], ACT.Relu).then_inc(high_ready[0], 1)

            def batch_norm(t):
                act.wait_ge(y_loaded[t.par], t.h17)
                act.wait_ge(z_turned, t.n)
                for f in range(KC):
                    ins = act.activation(z[:, f, 0:t.cols], y[:, t.par, f, 0:t.cols], ACT.Identity,
                                         scale=g.bn_scale[:, f:f + 1], bias=g.bn_shift[:, f:f + 1])
                ins.then_inc(z_ready, 1)

            def gcn_rows(t):
                act.wait_ge(gcn_done, t.n1)
                act.wait_ge(low_ready[2], t.n)
                act.wait_ge(gcn_turned, t.n)
                for n in range(KC):
                    ins = act.activation(gcn[:, n, 0:t.cols], layer_ps[:, n, 0:t.cols], ACT.Relu,
                                         bias=g.bs_col[:, 0, n:n + 1])
                ins.then_inc(gcn_ready, 1)
                act.wait_ge(gcn_ready, t.n1)
                act.wait_ge(last_done, t.n)
                act.activation(high[2][:, :, 0:t.cols], gcn[:, :, 0:t.cols], ACT.Copy).then_inc(high_ready[2], 1)

            def keep_gcn(t):
                act.wait_ge(gcn_turned, t.n1)
                act.wait_ge(stored[3][t.par], t.h16)
                act.activation(rows_y[0:t.parts, t.par, 0:t.rows, :], rows_ps[0:t.parts, 0:t.rows, :], ACT.Copy
                               ).then_inc(rows_y_ready, 1)

            block_loop(act, g, [(4, high_rows3), (1, roots12), (3, root_of(2)), (1, norm1), (2, high_rows2),
                                (0, batch_norm), (5, root_of(3)), (4, gcn_rows), (3, norm3), (4, keep_gcn)])

        @block.vector
        def _(v):
            def moments_of(t, n, rows):
                v.wait_ge(raw_ready[n], t.n1)
                for r in range(t.rows):
                    ins = v.bn_stats(stats[0:t.parts, n, r, :], rows[0:t.parts, r, :])
                ins.then_inc(stats_ready[n], 1)
                v.wait_ge(stats_ready[n], t.n1)
                v.sem_inc(stats_seen, 1)
                for r in range(t.rows):
                    ins = v.bn_aggr(mom[0:t.parts, n, r, :], stats[0:t.parts, n, r, :])
                ins.then_inc(var_ready[n], 1)

            def split(part, src, ready, relu=False):
                def one(t):
                    v.wait_ge(ready, t.n1)
                    a, b, c = low[part][:, :, 0:t.cols], src[:, :, 0:t.cols], high[part][:, :, 0:t.cols].bitcast(F32)
                    if relu:
                        ins = v.scalar_tensor_tensor(out=a, in0=b, scalar=0.0, in1=c, op0=ALU.max, op1=ALU.subtract)
                    else:
                        ins = v.tensor_tensor(a, b, c, ALU.subtract)
                    ins.then_inc(low_ready[part], 1)
                return one

            def shift_by(t, n, rstd):
                v.wait_ge(inverted[n], t.n1)
                v.scalar_tensor_tensor(out=shift[0:t.parts, n, 0:t.rows], in0=mom[0:t.parts, n, 0:t.rows, 0],
                                       scalar=-1.0, in1=rstd, op0=ALU.mult, op1=ALU.mult).then_inc(rstd_ready[n], 1)

            def invert12(t):
                v.wait_ge(std_ready[0], t.n1)
                v.reciprocal(dev12[0:t.parts, 1, :, 0:t.rows], dev12[0:t.parts, 0, :, 0:t.rows]
                             ).then_inc(inverted[0], 1)
                shift_by(t, 0, dev12[0:t.parts, 1, 0, 0:t.rows])

            def invert3(t):
                v.wait_ge(std_ready[2], t.n1)
                v.reciprocal(dev[0:t.parts, 2, 1, 0:t.rows], dev[0:t.parts, 2, 0, 0:t.rows]).then_inc(inverted[2], 1)
                shift_by(t, 2, dev[0:t.parts, 2, 1, 0:t.rows])

            def invert4(t):
                v.wait_ge(std_ready[3], t.n1)
                v.reciprocal(dev[0:t.parts, 3, 1, 0:t.rows], dev[0:t.parts, 3, 0, 0:t.rows]).then_inc(rstd_ready[3], 1)

            def norm4(t):
                v.wait_ge(rstd_ready[3], t.n1)
                v.wait_ge(stored[4][t.par], t.h16)
                for r in range(t.rows // 2):
                    ins = v.tensor_scalar(rows4[0:t.parts, t.par, r, :], raw[2][0:t.parts, r, :],
                                          mom[0:t.parts, 3, r, 0:1], dev[0:t.parts, 3, 1, r:r + 1],
                                          ALU.subtract, ALU.mult)
                ins.then_inc(half_normed, 1)

            def sum4(t):
                v.wait_ge(last_done, t.n1)
                v.wait_ge(half_normed, t.n)
                v.wait_ge(normed[3], t.n)
                v.scalar_tensor_tensor(out=raw[2][0:t.parts, 0:t.rows, :], in0=last_ps[0:t.parts, 0:t.rows, :],
                                       scalar=0.0, in1=rows3[0:t.parts, t.par, 0:t.rows, :], op0=ALU.max, op1=ALU.add
                                       ).then_inc(raw_ready[3], 1)
                moments_of(t, 3, raw[2])

            def sum3(t):
                v.wait_ge(appnp_done, t.n1)
                v.wait_ge(normed[2], t.n)
                layer = layer_ps[:, :, :].rearrange("p a (b n) -> p (a b) n", n=D)
                v.tensor_tensor(raw[1][0:t.parts, 0:t.rows, :], layer[0:t.parts, 0:t.rows, :],
                                rows2[0:t.parts, t.par, 0:t.rows, :], ALU.add).then_inc(raw_ready[2], 1)
                moments_of(t, 2, raw[1])

            def sum1(t):
                v.wait_ge(z_turned, t.n1)
                v.wait_ge(x_loaded[t.par], t.h17)
                v.wait_ge(normed[0], t.n)
                v.wait_ge(normed[1], t.n)
                v.tensor_tensor(raw[0][0:t.parts, 0:t.rows, :], rows_ps[0:t.parts, 0:t.rows, :],
                                x[0:t.parts, t.par, 0:t.rows, :], ALU.add).then_inc(raw_ready[0], 1)
                moments_of(t, 0, raw[0])

            block_loop(v, g, [(3, sum3), (1, invert12), (4, split(1, turned_ps, high_ready[1])), (3, invert3),
                              (5, sum4), (2, split(0, turned_ps, high_ready[0], relu=True)), (5, invert4), (0, sum1),
                              (5, norm4), (4, split(2, gcn, high_ready[2]))])

        @block.gpsimd
        def _(pool):
            def norm2(t):
                pool.wait_ge(rstd_ready[0], t.n1)
                pool.wait_ge(stored[1][t.par], t.h16)
                if (n := later(t.n, -1)) is not None:
                    pool.wait_ge(raw_ready[2], snap(pool, n))
                pool.sem_inc(norm_seen, 1)
                for r in range(t.rows):
                    ins = pool.tensor_scalar(rows2[0:t.parts, t.par, r, :], raw[0][0:t.parts, r, :],
                                             mom[0:t.parts, 0, r, 0:1], dev12[0:t.parts, 1, 1, r:r + 1],
                                             ALU.subtract, ALU.mult)
                ins.then_inc(normed[1], 1)

            def norm4(t):
                pool.wait_ge(rstd_ready[3], t.n1)
                pool.wait_ge(stored[4][t.par], t.h16)
                pool.sem_inc(norm_seen, 1)
                for r in range(t.rows // 2, t.rows):
                    ins = pool.tensor_scalar(rows4[0:t.parts, t.par, r, :], raw[2][0:t.parts, r, :],
                                             mom[0:t.parts, 3, r, 0:1], dev[0:t.parts, 3, 1, r:r + 1],
                                             ALU.subtract, ALU.mult)
                ins.then_inc(normed[3], 1)

            block_loop(pool, g, [(1, norm2), (5, norm4)])




def gnn_program(nc, x, src, dst, ew, eps, W1, b1, W2, b2, gamma, beta, Wgat, a_src, a_dst, WL2, bL2, WL3, bL3,
                resW, resb, out):
    g = Program()
    g.x, g.src, g.dst, g.ew, g.eps, g.W1, g.b1, g.W2, g.b2 = x, src, dst, ew, eps, W1, b1, W2, b2
    g.gamma, g.beta, g.Wgat, g.a_src, g.a_dst, g.WL2, g.bL2 = gamma, beta, Wgat, a_src, a_dst, WL2, bL2
    g.WL3, g.bL3, g.resW, g.resb, g.out = WL3, bL3, resW, resb, out
    N, E = x.shape[0], src.shape[0]
    g.N, g.E = N, E
    g.ES = -(-E // (T8 * P))
    g.ET = ET = T8 * g.ES
    g.EP = EP = ET * P
    g.NB = -(-ET // P)
    full, rest = divmod(N, BLOCK)
    assert rest and tail_shape(rest)[1] > 1 and full >= 8 and g.ES >= 4 and N < 65535
    g.NBLK = full + 1
    g.tail = tail_shape(rest)
    g.NTP = max(p for p in range(1, P + 1) if N % p == 0)
    g.NTR = N // g.NTP

    def table(name, shape, dt=F32):
        return nc.dram_tensor(name, shape, dt).ap()

    g.agg_table = table("agg_table", [N, D])
    g.y_table = table("y_table", [g.NBLK * P, KC * BLOCK])
    g.x1_table = table("x1_table", [N, D])
    g.x2_table = table("x2_table", [N + 2 * EP, D])
    g.x3_table = table("x3_table", [N + EP, D])
    g.y1_table = table("y1_table", [N + EP, D])
    g.x1_slots = table("x1_slots", [EP, D])
    g.h_slots = table("h_slots", [EP, D])
    g.score_lines = table("line_table", [H, 2, EP])
    g.node_table = table("node_table", [N, 4])
    g.key_rows = table("key_rows", [1, EP], U16)

    with ExitStack() as ctx:
        m = Memory(nc, ctx, "all")
        g.keys = m.sb("keys", [P, EP + 2], U16)
        g.edge_fields = m.sb("edge_fields", [P, ET + T8, NFIELD])
        g.bn_scale = m.sb("bn_scale", [P, KC])
        g.bn_shift = m.sb("bn_shift", [P, KC])
        g.ident = m.sb("ident", [P, P])
        g.sel01 = m.sb("sel01", [P, P], F32R)
        g.ln_eps = m.sb("ln_eps", [P, 1])
        g.ln_eps2 = m.sb("ln_eps2", [P, 1])
        g.eps1 = m.sb("eps1", [P, 1])
        g.b1_col = m.sb("b1_col", [P, 2 * D // P])
        g.b2_col = m.sb("b2_col", [P, KC])
        g.gamma_col = m.sb("gamma_col", [P, KC])
        g.beta_col = m.sb("beta_col", [P, KC])
        g.bs_col = m.sb("bs_col", [P, 2, KC])
        g.bias_rows = m.sb("bias_rows", [P, 3, D], F32R)
        g.wl2, g.wg0, g.wg1, g.wres, g.ws0, g.ws1, g.wgat, g.wat = (
            m.sb(f"w_{name}", [P, 2, KC, D], F32R)
            for name in ("l2", "gcn0", "gcn1", "res", "sum0", "sum1", "gat", "scores"))

        with ExitStack() as first_half:
            m = Memory(nc, first_half, "half1")
            g.deg_in = m.sb("deg_in", [P, ET, 4], F32R)
            g.deg = m.sb("deg", [P, ET, 4])
            g.slot_row = m.sb("slot_row", [P, ET])
            g.slot_info = m.sb("slot_info", [P, ET, 4])
            g.src_info = m.sb("src_info", [P, ET, 4])
            g.bn_stats = m.sb("bn_stats", [P, KC, g.NBLK, 6])
            g.w1 = m.sb("w1", [P, 2, KC, 2 * D], F32R)
            g.w2 = m.sb("w2", [P, 2, 2 * KC, D], F32R)
            setup(nc, g)
            edge_layer(nc, g, "sum0", g.x, SRC, None)
            degrees(nc, g)
            gin_hidden(nc, g)
            norm_and_fields(nc, g)
        dense_layers(nc, g)
        gat_scores(nc, g)
        gat_sum(nc, g)
        x2, h1 = (g.x2_table, N), (g.x2_table, N + EP)
        x3, y1 = (g.x3_table, N), (g.y1_table, N)
        edge_layer(nc, g, "hop1", g.x2_table[0:N + EP, :], ROW, C_APPNP, [x2], D_KEEP, D_HALF, result=h1)
        edge_layer(nc, g, "hop2", g.x2_table, ROW_H, C_APPNP, [h1, x2], D_HALF2, D_HALF, [g.wl2], True, 0,
                   result=x3, norm=True)
        edge_layer(nc, g, "gcn1", g.x3_table, ROW, C_GCN, [x3], DIS2, DIS, [g.wg0, g.wres], False, 1, result=y1)
        edge_layer(nc, g, "gcn2", g.y1_table, ROW, C_GCN, [y1, x3], DIS2, DIS, [g.wg1, g.wres], False, 2,
                   norm=True)


_INS = ["x", "src", "dst", "edge_weight", "L0_gnn_eps", "L0_gnn_W1", "L0_gnn_b1", "L0_gnn_W2", "L0_gnn_b2",
        "L0_gnn_gamma", "L0_gnn_beta", "L1_gnn_W", "L1_gnn_a_src", "L1_gnn_a_dst", "L2_gnn_W", "L2_gnn_b",
        "L3_gnn_W", "L3_gnn_b", "L3_gnn_resW", "L3_gnn_resb"]


def kernel(**inputs):
    import numpy as _np
    import concourse.bacc as _bacc
    from concourse import mybir as _mybir
    from concourse.bass_utils import run_bass_kernel_spmd as _run

    nc = _bacc.Bacc("TRN2", target_bir_lowering=False, num_devices=1)
    arrays, args = {}, []
    for name in _INS:
        a = _np.ascontiguousarray(inputs[name])
        arrays[f"in_{name}_dram"] = a
        args.append(nc.dram_tensor(f"in_{name}_dram", a.shape, _mybir.dt.from_np(a.dtype), kind="ExternalInput").ap())
    out = nc.dram_tensor("out_0_dram", inputs["x"].shape, _mybir.dt.float32, kind="ExternalOutput").ap()
    gnn_program(nc, *args, out)
    r = _run(nc, [arrays], core_ids=[0])
    return r.results[0]["out_0_dram"]
```
